# Optimizing a Trainium2 kernel written in Bass

```python
import numpy as np
import jax
import jax.numpy as jnp

def _softmax(x, axis=-1):
    return jax.nn.softmax(x, axis=axis)

def _gelu(x):
    return jax.nn.gelu(x, approximate=True)

def _silu(x):
    return jax.nn.silu(x)

def _sigmoid(x):
    return jax.nn.sigmoid(x)

def _layernorm(x, axis=-1, eps=1e-05):
    m = jnp.mean(x, axis=axis, keepdims=True)
    v = jnp.var(x, axis=axis, keepdims=True)
    return (x - m) / jnp.sqrt(v + eps)

def _scatter_add(tgt, idx, src, axis=0):
    return tgt.at[idx].add(src)

def _segment_sum(src, seg, n):
    return jax.ops.segment_sum(src, seg, n)
kernel_name = 'mk_gnn_preln_d4_gnn_r64_074131'

def setup_inputs(seed: int=0):
    np.random.seed(seed)
    _w = jnp.asarray

    def _rec_inputs():
        import jax
        import jax.numpy as jnp
        _gk = jax.random.key(seed)
        x = -0.0005121 + 1.001 * jax.random.normal(jax.random.fold_in(_gk, 1), (100000, 32), jnp.float32)
        src = jax.random.randint(jax.random.fold_in(_gk, 2), (50000,), 0, 100000, jnp.int32)
        dst = jax.random.randint(jax.random.fold_in(_gk, 3), (50000,), 0, 100000, jnp.int32)
        _o = jnp.argsort(dst, stable=True)
        src = src[_o]
        dst = dst[_o]
        edge_type_86 = jax.random.randint(jax.random.fold_in(_gk, 13), (50000,), 0, 86, jnp.int32)
        return (x, src, dst, edge_type_86)
    x, src, dst, edge_type_86 = _rec_inputs()

    def _L0_gnn_setup():
        import jax, jax.numpy as jnp
        import numpy as np
        N = 100000
        F = 32
        E = 25000
        NEG_SLOPE = 0.2
        key = jax.random.key(seed)
        ks = jax.random.split(key, 6)
        x = jax.random.normal(ks[0], (N, F), dtype=jnp.float32)
        edge_index = jax.random.randint(ks[1], (2, E), 0, N, dtype=jnp.int32)
        scale = 1.0 / np.sqrt(F)
        W = jax.random.normal(ks[2], (F, F), dtype=jnp.float32) * scale
        att_src = jax.random.normal(ks[3], (F,), dtype=jnp.float32) * scale
        att_dst = jax.random.normal(ks[4], (F,), dtype=jnp.float32) * scale
        bias = jax.random.normal(ks[5], (F,), dtype=jnp.float32) * 0.01
        return {'x': x, 'edge_index': edge_index, 'W': W, 'att_src': att_src, 'att_dst': att_dst, 'bias': bias}
    _L0_gnn_all = _L0_gnn_setup()
    _L0_gnn_in = {k: v for k, v in _L0_gnn_all.items() if k in ('W', 'att_src', 'att_dst', 'bias')}
    del _L0_gnn_all

    def _L1_gnn_setup():
        import jax, jax.numpy as jnp
        import numpy as np
        N_NODES = 100000
        N_EDGES = 25000
        IN_C, HID_C, OUT_C = (32, 64, 32)

        def _sage_conv(x, src, dst, W_l, W_r, b, num_nodes):
            msg = x[src]
            agg = jax.ops.segment_sum(msg, dst, num_segments=num_nodes)
            deg = jax.ops.segment_sum(jnp.ones((src.shape[0],), dtype=x.dtype), dst, num_segments=num_nodes)
            mean = agg / jnp.maximum(deg, 1.0)[:, None]
            return mean @ W_l.T + x @ W_r.T + b
        key = jax.random.key(seed)
        ks = jax.random.split(key, 9)
        x = jax.random.normal(ks[0], (N_NODES, IN_C), dtype=jnp.float32)
        edge_index = jax.random.randint(ks[1], (2, N_EDGES), 0, N_NODES, dtype=jnp.int64)
        s1 = 1.0 / np.sqrt(IN_C)
        s2 = 1.0 / np.sqrt(HID_C)
        W1_l = jax.random.uniform(ks[2], (HID_C, IN_C), minval=-s1, maxval=s1, dtype=jnp.float32)
        W1_r = jax.random.uniform(ks[3], (HID_C, IN_C), minval=-s1, maxval=s1, dtype=jnp.float32)
        b1 = jax.random.uniform(ks[4], (HID_C,), minval=-s1, maxval=s1, dtype=jnp.float32)
        W2_l = jax.random.uniform(ks[5], (OUT_C, HID_C), minval=-s2, maxval=s2, dtype=jnp.float32)
        W2_r = jax.random.uniform(ks[6], (OUT_C, HID_C), minval=-s2, maxval=s2, dtype=jnp.float32)
        b2 = jax.random.uniform(ks[7], (OUT_C,), minval=-s2, maxval=s2, dtype=jnp.float32)
        return {'x': x, 'W1_l': W1_l, 'W1_r': W1_r, 'b1': b1, 'W2_l': W2_l, 'W2_r': W2_r, 'b2': b2, 'edge_index': edge_index}
    _L1_gnn_all = _L1_gnn_setup()
    _L1_gnn_in = {k: v for k, v in _L1_gnn_all.items() if k in ('W1_l', 'W1_r', 'b1', 'W2_l', 'W2_r', 'b2')}
    del _L1_gnn_all

    def _L2_gnn_setup():
        import jax, jax.numpy as jnp
        import numpy as np
        N_NODES = 100000
        N_RADIAL = 16
        N_CONICAL = 16
        key = jax.random.key(seed)
        k1, k2, k3, k4 = jax.random.split(key, 4)
        x = jax.random.normal(k1, (N_NODES, 32), dtype=jnp.float32)
        edge_index = jax.random.randint(k2, (2, 25000), 0, N_NODES, dtype=jnp.int32)
        W1 = jax.random.normal(k3, (32, 128), dtype=jnp.float32) * 0.1
        b1 = jnp.zeros((128,), dtype=jnp.float32)
        W2 = jax.random.normal(k4, (128, 32), dtype=jnp.float32) * 0.1
        b2 = jnp.zeros((32,), dtype=jnp.float32)
        return {'x': x, 'edge_index': edge_index, 'W1': W1, 'b1': b1, 'W2': W2, 'b2': b2}
    _L2_gnn_all = _L2_gnn_setup()
    _L2_gnn_in = {k: v for k, v in _L2_gnn_all.items() if k in ('W1', 'b1', 'W2', 'b2')}
    del _L2_gnn_all

    def _L3_gnn_setup():
        import jax, jax.numpy as jnp
        import numpy as np
        N_NODES = 50000
        N_EDGES = 12500
        INP_DIM = 32
        OUT_DIM = 32
        ATTN_DIM = 32
        NUM_RELS = 86
        NUM_BASES = 16
        GAMMA = 0.0
        key = jax.random.key(seed)
        ks = jax.random.split(key, 12)
        return {'h': jax.random.normal(ks[0], (N_NODES, INP_DIM), jnp.float32), 'weight': jax.random.normal(ks[1], (NUM_BASES, INP_DIM, OUT_DIM), jnp.float32), 'w_comp': jax.random.normal(ks[2], (NUM_RELS, NUM_BASES), jnp.float32), 'self_loop_weight': jax.random.normal(ks[3], (INP_DIM, OUT_DIM), jnp.float32), 'A1_w': jax.random.normal(ks[4], (ATTN_DIM, INP_DIM), jnp.float32), 'A1_b': jax.random.normal(ks[5], (ATTN_DIM,), jnp.float32), 'A2_w': jax.random.normal(ks[6], (ATTN_DIM, INP_DIM), jnp.float32), 'A2_b': jax.random.normal(ks[7], (ATTN_DIM,), jnp.float32), 'rel_emb': jax.random.normal(ks[8], (NUM_RELS, ATTN_DIM), jnp.float32), 'src': jax.random.randint(ks[9], (N_EDGES,), 0, N_NODES, jnp.int32), 'dst': jax.random.randint(ks[10], (N_EDGES,), 0, N_NODES, jnp.int32), 'etype': jax.random.randint(ks[11], (N_EDGES,), 0, NUM_RELS, jnp.int32)}
    _L3_gnn_all = _L3_gnn_setup()
    _L3_gnn_in = {k: v for k, v in _L3_gnn_all.items() if k in ('weight', 'w_comp', 'self_loop_weight', 'A1_w', 'A1_b', 'A2_w', 'A2_b', 'rel_emb')}
    del _L3_gnn_all
    return {'x': x, 'src': src, 'dst': dst, 'edge_type_86': edge_type_86, 'L0_gnn_W': _L0_gnn_in['W'], 'L0_gnn_att_src': _L0_gnn_in['att_src'], 'L0_gnn_att_dst': _L0_gnn_in['att_dst'], 'L0_gnn_bias': _L0_gnn_in['bias'], 'L1_gnn_W1_l': _L1_gnn_in['W1_l'], 'L1_gnn_W1_r': _L1_gnn_in['W1_r'], 'L1_gnn_b1': _L1_gnn_in['b1'], 'L1_gnn_W2_l': _L1_gnn_in['W2_l'], 'L1_gnn_W2_r': _L1_gnn_in['W2_r'], 'L1_gnn_b2': _L1_gnn_in['b2'], 'L2_gnn_W1': _L2_gnn_in['W1'], 'L2_gnn_b1': _L2_gnn_in['b1'], 'L2_gnn_W2': _L2_gnn_in['W2'], 'L2_gnn_b2': _L2_gnn_in['b2'], 'L3_gnn_weight': _L3_gnn_in['weight'], 'L3_gnn_w_comp': _L3_gnn_in['w_comp'], 'L3_gnn_self_loop_weight': _L3_gnn_in['self_loop_weight'], 'L3_gnn_A1_w': _L3_gnn_in['A1_w'], 'L3_gnn_A1_b': _L3_gnn_in['A1_b'], 'L3_gnn_A2_w': _L3_gnn_in['A2_w'], 'L3_gnn_A2_b': _L3_gnn_in['A2_b'], 'L3_gnn_rel_emb': _L3_gnn_in['rel_emb']}

def reference(x, src, dst, edge_type_86, L0_gnn_W, L0_gnn_att_src, L0_gnn_att_dst, L0_gnn_bias, L1_gnn_W1_l, L1_gnn_W1_r, L1_gnn_b1, L1_gnn_W2_l, L1_gnn_W2_r, L1_gnn_b2, L2_gnn_W1, L2_gnn_b1, L2_gnn_W2, L2_gnn_b2, L3_gnn_weight, L3_gnn_w_comp, L3_gnn_self_loop_weight, L3_gnn_A1_w, L3_gnn_A1_b, L3_gnn_A2_w, L3_gnn_A2_b, L3_gnn_rel_emb):
    import jax
    import jax.numpy as jnp

    def _L0_gnn_ref(x, edge_index, W, att_src, att_dst, bias):
        import jax, jax.numpy as jnp
        import numpy as np
        N = 100000
        F = 32
        E = 25000
        NEG_SLOPE = 0.2
        h = x @ W
        loops = jnp.arange(N, dtype=edge_index.dtype)
        src = jnp.concatenate([edge_index[0], loops])
        dst = jnp.concatenate([edge_index[1], loops])
        a_src = h @ att_src
        a_dst = h @ att_dst
        e = jax.nn.leaky_relu(a_src[src] + a_dst[dst], NEG_SLOPE)
        m = jax.ops.segment_max(e, dst, num_segments=N)
        ex = jnp.exp(e - m[dst])
        denom = jax.ops.segment_sum(ex, dst, num_segments=N)
        alpha = ex / denom[dst]
        out = jax.ops.segment_sum(alpha[:, None] * h[src], dst, num_segments=N)
        return out + bias

    def _L1_gnn_ref(x, W1_l, W1_r, b1, W2_l, W2_r, b2, edge_index):
        import jax, jax.numpy as jnp
        import numpy as np
        N_NODES = 100000
        N_EDGES = 25000
        IN_C, HID_C, OUT_C = (32, 64, 32)

        def _sage_conv(x, src, dst, W_l, W_r, b, num_nodes):
            msg = x[src]
            agg = jax.ops.segment_sum(msg, dst, num_segments=num_nodes)
            deg = jax.ops.segment_sum(jnp.ones((src.shape[0],), dtype=x.dtype), dst, num_segments=num_nodes)
            mean = agg / jnp.maximum(deg, 1.0)[:, None]
            return mean @ W_l.T + x @ W_r.T + b
        src, dst = (edge_index[0], edge_index[1])
        h = _sage_conv(x, src, dst, W1_l, W1_r, b1, N_NODES)
        h = jax.nn.relu(h)
        out = _sage_conv(h, src, dst, W2_l, W2_r, b2, N_NODES)
        return out

    def _L2_gnn_ref(x, edge_index, W1, b1, W2, b2):
        import jax, jax.numpy as jnp
        import numpy as np
        N_NODES = 100000
        N_RADIAL = 16
        N_CONICAL = 16
        radial = x[:, :N_RADIAL]
        conical = x[:, N_RADIAL:N_RADIAL + N_CONICAL]
        i, j = (edge_index[0], edge_index[1])
        rows = jnp.concatenate([i, j])
        cols = jnp.concatenate([j, i])
        neighbor_sum = jax.ops.segment_sum(conical[cols], rows, num_segments=N_NODES)
        deg = jax.ops.segment_sum(jnp.ones_like(rows, dtype=x.dtype), rows, num_segments=N_NODES)
        deg = jnp.clip(deg, 1.0)[:, None]
        agg = neighbor_sum / deg
        combined = jnp.concatenate([radial, agg], axis=1)
        h = jax.nn.relu(combined @ W1 + b1)
        out = h @ W2 + b2
        return out

    def _L3_gnn_ref(h, weight, w_comp, self_loop_weight, A1_w, A1_b, A2_w, A2_b, rel_emb, src, dst, etype):
        import jax, jax.numpy as jnp
        import numpy as np
        N_NODES = 50000
        N_EDGES = 12500
        INP_DIM = 32
        OUT_DIM = 32
        ATTN_DIM = 32
        NUM_RELS = 86
        NUM_BASES = 16
        GAMMA = 0.0
        E = src.shape[0]
        N = h.shape[0]
        x = h[src]
        y = h[dst]
        c = w_comp[etype]
        xb = jnp.einsum('ei,bio->ebo', x, weight)
        msg = jnp.einsum('eb,ebo->eo', c, xb)
        x_hat = x @ A1_w.T + A1_b
        y_hat = y @ A2_w.T + A2_b + rel_emb[etype]
        scale = jnp.sqrt(jnp.asarray(INP_DIM, h.dtype))
        a = jnp.tanh(jax.nn.relu(jnp.sum(x_hat * y_hat, axis=-1) / scale))
        a = jnp.where(a > GAMMA, a, jnp.zeros_like(a))
        nei = jax.ops.segment_sum(a[:, None] * msg, dst, num_segments=N)
        last_e = jax.ops.segment_max(jnp.arange(E, dtype=jnp.int32), dst, num_segments=N)
        last_e = jnp.clip(last_e, 0, E - 1)
        curr = h[src[last_e]] @ self_loop_weight
        in_deg = jax.ops.segment_sum(jnp.ones((E,), h.dtype), dst, num_segments=N)
        h_new = jnp.where((in_deg > 0)[:, None], nei + curr, jnp.zeros_like(nei))
        return jax.nn.relu(h_new)
    edge_index = jnp.stack([src, dst])
    h = jnp.maximum(_layernorm(x, axis=-1), 0.0)
    x = x + _L0_gnn_ref(h, edge_index, L0_gnn_W, L0_gnn_att_src, L0_gnn_att_dst, L0_gnn_bias)
    h = jnp.maximum(_layernorm(x, axis=-1), 0.0)
    x = x + _L1_gnn_ref(h, L1_gnn_W1_l, L1_gnn_W1_r, L1_gnn_b1, L1_gnn_W2_l, L1_gnn_W2_r, L1_gnn_b2, edge_index)
    h = jnp.maximum(_layernorm(x, axis=-1), 0.0)
    x = x + _L2_gnn_ref(h, edge_index, L2_gnn_W1, L2_gnn_b1, L2_gnn_W2, L2_gnn_b2)
    h = jnp.maximum(_layernorm(x, axis=-1), 0.0)
    x = x + _L3_gnn_ref(h, L3_gnn_weight, L3_gnn_w_comp, L3_gnn_self_loop_weight, L3_gnn_A1_w, L3_gnn_A1_b, L3_gnn_A2_w, L3_gnn_A2_b, L3_gnn_rel_emb, src, dst, edge_type_86)
    return x

_drawn_inputs = setup_inputs


def setup_inputs(seed=0):
    import zlib

    import numpy as np

    out = dict(_drawn_inputs(seed))
    spreads = {'L2_gnn_b1': (0.0, 0.1), 'L2_gnn_b2': (0.0, 0.1)}
    factors = {}
    for name, (base, spread) in spreads.items():
        noise = np.random.default_rng([zlib.crc32(name.encode()), seed]).standard_normal(out[name].shape)
        drawn = base * np.exp(spread * noise) if base else spread * noise
        out[name] = jnp.asarray(drawn.astype(out[name].dtype))
    for name, factor in factors.items():
        out[name] = (out[name] * factor).astype(out[name].dtype)
    return out
```

```python
import concourse.bass as bass
from concourse import mybir
from contextlib import ExitStack

f32 = mybir.dt.float32
i32 = mybir.dt.int32
ALU = mybir.AluOpType
ACT = mybir.ActivationFunctionType
AX = mybir.AxisListType

P = 128
F = 32
N, E = 100000, 50000
C = 28
Q = C // 4
EC = 14
ET = EC * C
EPAD = P * ET
NC = 28
NT = NC * C
NPAD = P * NT
NTRASH = NPAD + P
PAIRS = EC // 2
CARRY = F + 1
OUTSIDE = 1 << 20
HID1, HID2 = 64, 128
CON = 16
CW = CON + 1
NREL, NB = 86, 16
RT = NB + 3 * F
EPS = 1e-5
NEG = -1.0e38


def bc_feat(ap, n=F):
    return ap.unsqueeze(2).to_broadcast([ap.shape[0], ap.shape[1], n])


def bc_tile(ap, n):
    return ap.unsqueeze(1).to_broadcast([ap.shape[0], n, ap.shape[1]])


def dve_norm(nc, dve, w, x, out, T, n, done=None, lo=0, hi=F):
    nc.vector.tensor_reduce(w.stat[:, 0, 0:T], x, AX.X, ALU.add)
    dve.drain()
    nc.vector.scalar_tensor_tensor(out=w.xc[:, 0:T, :], in0=bc_feat(w.stat[:, 0, 0:T]), scalar=-1.0 / F,
                                   in1=x, op0=ALU.mult, op1=ALU.add).then_inc(w.centered, 1)
    dve.wait_ge(w.squared, n + (w.base + 1))
    nc.vector.tensor_reduce(w.stat[:, 1, 0:T], w.sq[:, 0:T, :], AX.X, ALU.add).then_inc(w.summed, 1)
    dve.wait_ge(w.rooted, n + (w.base + 1))
    nc.vector.reciprocal(w.stat[:, 3, 0:T], w.stat[:, 2, 0:T])
    dve.drain()
    last = nc.vector.scalar_tensor_tensor(out=out, in0=w.xc[:, 0:T, lo:hi], scalar=0.0,
                                          in1=bc_feat(w.stat[:, 3, 0:T], hi - lo), op0=ALU.max, op1=ALU.mult)
    if done is not None:
        last.then_inc(done, 1)
    else:
        dve.drain()


def act_norm(nc, act, w, T, n):
    act.wait_ge(w.centered, n + (w.base + 1))
    nc.scalar.activation(w.sq[:, 0:T, :], w.xc[:, 0:T, :], ACT.Square).then_inc(w.squared, 1)
    act.wait_ge(w.summed, n + (w.base + 1))
    nc.scalar.activation(w.stat[:, 2, 0:T], w.stat[:, 1, 0:T], ACT.Sqrt, bias=w.eps[:, 0:1],
                         scale=1.0 / F).then_inc(w.rooted, 1)


def pool_wait(g, pool, *waits):
    for sem, value in waits:
        pool.wait_ge(sem, value)
    pool.sem_inc(g.pool_steps, 1)


class Norm:

    def __init__(self, nc, ctx, g, stage, T, norms):
        self.xc = ctx.enter_context(nc.sbuf_tensor(f"{stage}_xc", [P, T, F], f32))
        self.sq = ctx.enter_context(nc.sbuf_tensor(f"{stage}_sq", [P, T, F], f32))
        self.stat = ctx.enter_context(nc.sbuf_tensor(f"{stage}_stat", [P, 4, T], f32))
        self.eps = g.eps
        self.centered, self.squared, self.summed, self.rooted = g.norm_sems
        self.base = g.norms
        g.norms += norms


class Globals:
    pass


def pe_quads(nc, pt, src, ident, nquads, done):
    for q in range(nquads):
        last = nc.tensor.transpose(pt[:, q * P:(q + 1) * P], src[:, 4 * q:4 * q + 4, :].rearrange("p t f -> p (t f)"),
                                   ident)
    last.then_inc(done, 1)


def stage_setup(nc, g):
    with ExitStack() as ctx:
        sb = lambda name, shape, dt=f32: ctx.enter_context(nc.sbuf_tensor(name, shape, dt))
        dwin = sb("dst_windows", [P, 3, ET], i32)
        dwf = sb("dst_windows_f", [P, 3, ET])
        endf = sb("end_index_f", [P, ET])
        endi = sb("end_index", [P, ET], i32)
        zero = sb("zero", [P, 1024])
        att4 = sb("att_cols", [F, 3])
        wT = sb("W_T", [F, F])
        a2b = sb("A2_b_rows", [NREL, F])
        pw = ctx.enter_context(nc.psum_tensor("p_watt", [P, 512], f32))
        pa = ctx.enter_context(nc.psum_tensor("p_all", [P, 512], f32))
        loaded, cleared, flags, end_stored = (g.sem(n) for n in ("su_loaded", "su_cleared", "su_flags", "su_end_stored"))
        zero_set, padded, ident_set, watt_done = (g.sem(n) for n in ("su_zero_set", "su_padded", "su_ident", "su_watt"))
        att_loaded, att_sum, all_done, dst_loaded = (g.sem(n) for n in ("su_att", "su_att_sum", "su_all", "su_dst"))
        rt_loaded = g.sem("su_rt")
        block = ctx.enter_context(nc.Block())
        NLOAD = 4 + 8 + 8 + 4 + 3 + 4 + 3 + 1 + 4 + 8 + 1
        ROW = NTRASH * CW // P
        assert ROW * P == NTRASH * CW

        @block.sync
        def _(sp):
            for k in range(3):
                sp.dma_start(dwin[:, k, :], g.dst_flat[k:k + EPAD].rearrange("(p t) -> p t", t=ET)).then_inc(dst_loaded, 16)
            sp.dma_start(att4[:, 0:1], g.att_src.unsqueeze(1)).then_inc(att_loaded, 16)
            sp.dma_start(att4[:, 1:2], g.att_dst.unsqueeze(1)).then_inc(att_loaded, 16)
            sp.dma_start(wT[:], g.WT).then_inc(att_loaded, 16)
            sp.dma_start(g.relrow[:, 0:NB], g.w_comp).then_inc(rt_loaded, 16)
            sp.dma_start(g.relrow[:, NB:NB + F], g.rel_emb).then_inc(rt_loaded, 16)
            sp.dma_start(g.relrow[:, NB + F:NB + 2 * F], g.A1_b.partition_broadcast(NREL)).then_inc(rt_loaded, 16)
            sp.dma_start(a2b[:], g.A2_b.partition_broadcast(NREL)).then_inc(rt_loaded, 16)
            sp.wait_ge(padded, 1)
            n = 0

            def load(dst, src):
                nonlocal n
                n += 1
                sp.dma_start(dst, src).then_inc(loaded, 16)

            for j in range(4):
                load(g.w0[F * j:F * (j + 1), F * j:F * (j + 1)], g.W)
                r, jj = j // 2, j % 2
                load(g.w1l[F * j:F * (j + 1), r, HID1 * jj:HID1 * (jj + 1)], g.W1_lT)
                load(g.w1r[F * j:F * (j + 1), r, HID1 * jj:HID1 * (jj + 1)], g.W1_rT)
                load(g.bias0[0:1, F * j:F * (j + 1)], g.bias.unsqueeze(0))
                load(g.w2in[F * j:F * (j + 1), j, :], g.L2_W1)
                load(g.w3y[F * j:F * (j + 1), j, :], g.A2_wT)
                load(g.w3x[F * j:F * (j + 1), j, 0:F], g.A1_wT)
                load(g.w3x[F * j:F * (j + 1), j, F:2 * F], g.slw)
            for jj in range(2):
                k = HID1 * jj
                load(g.w1gr[k:k + HID1, k:k + F], g.W2_lT)
                load(g.w1gr[k:k + HID1, k + F:k + 2 * F], g.W2_rT)
                load(g.b1col[k:k + HID1, 0:1], g.L1_b1.unsqueeze(1))
                load(g.b1gr[0:1, k + F:k + 2 * F], g.L1_b2.unsqueeze(0))
            load(g.w2out[:], g.L2_W2)
            load(g.b2out[:], g.L2_b2.partition_broadcast(P))
            load(g.b2col[:], g.L2_b1.unsqueeze(1))
            load(g.w3[:], g.weight.rearrange("(c b) i o -> (b i) c o", b=4))
            sp.wait_ge(zero_set, 1)
            for table in (g.sum_dst, g.sum_a, g.sum_b):
                flat = table.rearrange("n w -> (n w)").rearrange("(p k) -> p k", k=ROW)
                for k in range(0, ROW, 1024):
                    m = min(1024, ROW - k)
                    sp.dma_start(flat[:, k:k + m], zero[:, 0:m]).then_inc(cleared, 16)
            sp.wait_ge(flags, 1)
            sp.dma_start(g.end_index, endi[:]).then_inc(end_stored, 16)
            sp.wait_ge(end_stored, 16)
            sp.wait_ge(loaded, 16 * n)
            sp.wait_ge(cleared, 16 * 3 * (-(-ROW // 1024)))

        @block.gpsimd
        def _(pool):
            nc.gpsimd.memset(g.ident[:], 0.0)
            nc.gpsimd.memset(g.before[:], 1.0)
            pool.drain()
            nc.gpsimd.affine_select(out=g.ident[:], in_=g.ident[:], compare_op=ALU.not_equal, fill=1.0, base=0,
                                    pattern=[[-1, P]], channel_multiplier=1)
            nc.gpsimd.affine_select(out=g.before[:], in_=g.before[:], compare_op=ALU.is_gt, fill=0.0, base=0,
                                    pattern=[[-1, P]], channel_multiplier=1)
            nc.gpsimd.iota(g.relid_i[:], pattern=[[0, 1]], base=0, channel_multiplier=1)
            pool.drain()
            nc.gpsimd.tensor_copy(g.relid[:], g.relid_i[:])
            pool.drain().then_inc(ident_set, 1)

        @block.vector
        def _(dve):
            dve.sem_inc(g.scatter_sems[3], 2)
            nc.vector.memset(zero[:], 0.0).then_inc(zero_set, 1)
            for t in (g.w0, g.w1l, g.w1r, g.w1gr, g.b1gr, g.w2in, g.w3x, g.w3y):
                nc.vector.memset(t[:], 0.0)
            nc.vector.memset(g.eps[:], EPS)
            nc.vector.memset(g.ones[:], 1.0)
            dve.drain().then_inc(padded, 1)
            nc.vector.memset(g.relrow[:, NB + 2 * F:RT], 0.0)
            dve.wait_ge(rt_loaded, 64)
            nc.vector.tensor_tensor(g.relrow[:, NB:NB + F], g.relrow[:, NB:NB + F], a2b[:], ALU.add)
            dve.wait_ge(att_loaded, 48)
            nc.vector.tensor_tensor(att4[:, 2:3], att4[:, 0:1], att4[:, 1:2], ALU.add).then_inc(att_sum, 1)
            dve.wait_ge(dst_loaded, 48)
            nc.vector.tensor_copy(dwf[:], dwin[:])
            dve.drain()
            nc.vector.tensor_tensor(g.same[:], dwf[:, 1, :], dwf[:, 0, :], ALU.is_equal)
            nc.vector.tensor_tensor(g.more[:], dwf[:, 1, :], dwf[:, 2, :], ALU.is_equal)
            dve.drain()
            nc.vector.tensor_scalar(g.end[:], g.more[:], -1.0, 1.0, ALU.mult, ALU.add)
            nc.vector.tensor_tensor_scan(g.pre[:], g.same[:], g.same[:], 1.0, ALU.mult, ALU.mult)
            nc.vector.tensor_tensor_scan(g.suf[:, ::-1], g.more[:, ::-1], g.more[:, ::-1], 1.0, ALU.mult, ALU.mult)
            nc.vector.tensor_scalar(endf[:], g.more[:], float(OUTSIDE), None, ALU.mult)
            dve.drain()
            nc.vector.tensor_tensor(endf[:], endf[:], dwf[:, 1, :], ALU.add)
            nc.vector.memset(g.deg[:], 1.0)
            dve.drain()
            nc.vector.tensor_copy(endi[:], endf[:]).then_inc(flags, 1)
            nc.vector.tensor_tensor_scan(g.deg[:], g.same[:], g.deg[:], 0.0, ALU.mult, ALU.add)
            dve.drain().then_inc(flags, 1)
            dve.wait_ge(watt_done, 1)
            nc.vector.tensor_copy(g.watt[:], pw[:, 0:3 * F].rearrange("p (k f) -> p k f", f=F))
            dve.wait_ge(all_done, 1)
            nc.vector.tensor_copy(g.preall[:], pa[0:CARRY, 0:P])
            nc.vector.tensor_copy(g.sufall[:], pa[0:CARRY, P:2 * P])
            dve.drain().then_inc(flags, 1)

        @block.tensor
        def _(pe):
            pe.wait_ge(att_sum, 1)
            for k in range(3):
                last = nc.tensor.matmul(pw[:, k * F:(k + 1) * F], att4[:, k:k + 1].to_broadcast([F, P]), wT[:], start=True, stop=True)
            last.then_inc(watt_done, 1)
            pe.wait_ge(flags, 2)
            pe.wait_ge(ident_set, 1)
            nc.tensor.matmul(pa[0:CARRY, 0:P], g.pre[:, ET - 1:ET].to_broadcast([P, CARRY]), g.ident[:], start=True, stop=True)
            nc.tensor.matmul(pa[0:CARRY, P:2 * P], g.suf[:, 0:1].to_broadcast([P, CARRY]), g.ident[:], start=True,
                             stop=True).then_inc(all_done, 1)

    stage_carry(nc, g, "deg", [g.deg[:, ET - 1:ET]])
    with ExitStack() as ctx:
        block = ctx.enter_context(nc.Block())

        @block.vector
        def _(dve):
            nc.vector.scalar_tensor_tensor(out=g.deg[:], in0=g.pre[:], scalar=g.carry[:, 0:1], in1=g.deg[:],
                                           op0=ALU.mult, op1=ALU.add)
            dve.drain()
            nc.vector.reciprocal(g.rdeg[:], g.deg[:])


def stage_carry(nc, g, stage, parts, reverse=False, greatest=False):
    n = sum(p.shape[1] for p in parts)
    with ExitStack() as ctx:
        own = ctx.enter_context(nc.sbuf_tensor(f"{stage}_own", [P, n], f32))
        row = ctx.enter_context(nc.sbuf_tensor(f"{stage}_row", [n, P + 1], f32))
        cut = ctx.enter_context(nc.sbuf_tensor(f"{stage}_cut", [n, P], f32))
        pr = ctx.enter_context(nc.psum_tensor(f"{stage}_prow", [n, P], f32))
        pc = ctx.enter_context(nc.psum_tensor(f"{stage}_pcol", [P, n], f32))
        copied, turned, scanned, back = g.carry_sems
        g.carries += 1
        now = g.carries
        block = ctx.enter_context(nc.Block())

        @block.vector
        def _(dve):
            k = 0
            for part in parts:
                nc.vector.tensor_copy(own[:, k:k + part.shape[1]], part)
                k += part.shape[1]
            nc.vector.memset(row[:, P:P + 1] if reverse else row[:, 0:1], NEG if greatest else 0.0)
            if greatest:
                nc.vector.tensor_scalar(cut[:], g.preall[0:n, :], -NEG, NEG, ALU.mult, ALU.add)
            dve.drain().then_inc(copied, 1)
            dve.wait_ge(turned, now)
            if reverse:
                nc.vector.tensor_tensor_scan(row[:, 0:P][:, ::-1], g.sufall[0:n, ::-1], pr[:, ::-1], 0.0, ALU.mult, ALU.add)
            elif greatest:
                nc.vector.tensor_tensor_scan(row[:, 1:P + 1], cut[:], pr[:], NEG, ALU.add, ALU.max)
            else:
                nc.vector.tensor_tensor_scan(row[:, 1:P + 1], g.preall[0:n, :], pr[:], 0.0, ALU.mult, ALU.add)
            dve.drain().then_inc(scanned, 1)
            dve.wait_ge(back, now)
            nc.vector.tensor_copy((g.carry_back if reverse else g.carry)[:, 0:n], pc[:])

        @block.tensor
        def _(pe):
            pe.wait_ge(copied, now)
            nc.tensor.transpose(pr[:], own[:], g.ident[:]).then_inc(turned, 1)
            pe.wait_ge(scanned, now)
            nc.tensor.transpose(pc[:], row[:, 1:P + 1] if reverse else row[:, 0:P], g.ident[0:n, 0:n]).then_inc(back, 1)


def stage_first_gather(nc, g):
    st = "s1"
    with ExitStack() as ctx:
        sb = lambda name, shape, dt=f32: ctx.enter_context(nc.sbuf_tensor(f"{st}_{name}", shape, dt))
        pb = lambda name: ctx.enter_context(nc.psum_tensor(f"{st}_{name}", [P, 1024], f32))
        S = lambda name: g.sem(f"{st}_{name}")
        w = Norm(nc, ctx, g, st, 2 * C, 10 * PAIRS)
        ring = sb("ring", [P, 2, 2, C, F])
        idx = sb("idx", [P, 2, 2, C], i32)
        hedge = sb("h_edge", [P, 2 * C, F])
        dots = sb("dots", [P, 5, C])
        x0 = sb("x0", [P, 2, C, F])
        x1 = sb("x1", [P, 2, C, F])
        x2 = sb("x2", [P, 2, C, F])
        gt = sb("g", [P, 2, C, F])
        hd = sb("h_node", [P, 2, C, F])
        tsb = sb("h_T", [P, Q * P])
        hid = sb("hid_T", [P, 2, Q * P])
        pT, pW, pH, pG = pb("pT"), pb("pW"), pb("pH"), pb("pG")
        idx_here = [S("idx_here0"), S("idx_here1")]
        rows = [S("rows0"), S("rows1")]
        x0_here = [S("x0_here0"), S("x0_here1")]
        ring_free, h_edge_ready = S("ring_free"), S("h_edge_ready")
        h0_ready, h1_ready, turned, turned_sb = S("h0_ready"), S("h1_ready"), S("turned"), S("turned_sb")
        w_done, hid_done, hid_sb, gr_done, gr_used = S("w_done"), S("hid_done"), S("hid_sb"), S("gr_done"), S("gr_used")
        x1_ready, x2_ready, stored, dense_free = S("x1_ready"), S("x2_ready"), S("stored"), S("dense_free")
        block = ctx.enter_context(nc.Block())
        GAT = 16 * 2 * C

        def cols(t, k, n=C * F):
            return t.rearrange("(p t) f -> p (t f)", p=P)[:, bass.ds(k * (C * F), n)]

        @block.sync
        def _(sp):
            def load_idx(c, a):
                sp.dma_start(idx[:, a, 0, :], g.src[:, bass.ds(c * C, C)]).then_inc(idx_here[a], 16)
                sp.dma_start(idx[:, a, 1, :], g.dst[:, bass.ds(c * C, C)]).then_inc(idx_here[a], 16)

            def load_x(k, b):
                sp.dma_start(x0[:, b].rearrange("p t f -> p (t f)"), cols(g.x, k)).then_inc(x0_here[b], 16)

            sp.sem_inc(dense_free, 2)
            for a in range(2):
                load_idx(a, a)
                load_x(a, a)

            def turn(i, more):
                for a in range(2):
                    for m in range(2):
                        k, b = i * 4 + (2 * a + m), m
                        sp.wait_ge(x1_ready, k + 1)
                        sp.dma_start(cols(g.X1, k), x1[:, b].rearrange("p t f -> p (t f)")).then_inc(stored, 16)
                        if more or a == 0:
                            load_x(k + 2, b)
                        sp.wait_ge(x2_ready, k + 1)
                        sp.dma_start(cols(g.X2, k), x2[:, b].rearrange("p t f -> p (t f)")).then_inc(stored, 16)
                        sp.dma_start(cols(g.G, k), gt[:, b].rearrange("p t f -> p (t f)")).then_inc(stored, 16)
                        sp.wait_ge(stored, (k + 1) * 48)
                        sp.sem_inc(dense_free, 1)
                    if more:
                        sp.wait_ge(rows[a], i * GAT + GAT)
                        load_idx(i * 2 + (a + 2), a)

            with sp.Fori(0, PAIRS - 1) as i:
                turn(i, True)
            turn(PAIRS - 1, False)

        @block.gpsimd
        def _(pool):
            with pool.Fori(0, PAIRS) as i:
                for a in range(2):
                    pool_wait(g, pool, (idx_here[a], i * 32 + 32), (ring_free, i * 2 + (a + 1)))
                    for t in range(C):
                        for k in range(2):
                            pool.indirect_dma_start(
                                out=ring[:, a, k, t, :], out_offset=None, in_=g.x,
                                in_offset=bass.IndirectOffsetOnAxis(ap=idx[:, a, k, t:t + 1], axis=0),
                            ).then_inc(rows[a], 16)

        @block.vector
        def _(dve):
            with dve.Fori(0, PAIRS) as i:
                for a in range(2):
                    def node_a(m):
                        b = m
                        dve.wait_ge(x0_here[b], i * 32 + 16 * (a + 1))
                        dve_norm(nc, dve, w, x0[:, b], hd[:, 0], C, i * 10 + (5 * a + (0, 3)[m]), h0_ready)

                    def node_b(m):
                        b, k = m, i * 4 + (2 * a + m)
                        dve.wait_ge(dense_free, k + 1)
                        dve.wait_ge(w_done, k + 1)
                        nc.vector.tensor_tensor(x1[:, b], x0[:, b], pW[:, 0:C * F].rearrange("p (t f) -> p t f", f=F), ALU.add)
                        dve.drain().then_inc(x1_ready, 1)
                        dve_norm(nc, dve, w, x1[:, b], hd[:, 1], C, i * 10 + (5 * a + (2, 4)[m]), h1_ready)

                    def node_c(m):
                        b, k = m, i * 4 + (2 * a + m)
                        for half in range(2):
                            dve.wait_ge(gr_done, k * 2 + (half + 1))
                            pv = pG[:, 0:C // 2 * 2 * F].rearrange("p (t c) -> p t c", c=2 * F)
                            ts = slice(half * (C // 2), (half + 1) * (C // 2))
                            nc.vector.tensor_tensor(x2[:, b, ts, :], x1[:, b, ts, :], pv[:, :, F:2 * F], ALU.add)
                            nc.vector.tensor_copy(gt[:, b, ts, :], pv[:, :, 0:F])
                            dve.drain().then_inc(gr_used, 1)
                        nc.vector.tensor_copy(w.stat[:, 3, 0:1], w.stat[:, 3, 0:1]).then_inc(x2_ready, 1)

                    def edges():
                        c = i * 2 + a
                        dve.wait_ge(rows[a], i * GAT + GAT)
                        dve.wait_ge(ring_free, c + 2)
                        dve_norm(nc, dve, w, ring[:, a].rearrange("p k t f -> p (k t) f"), hedge[:], 2 * C,
                                 i * 10 + (5 * a + 1))
                        for k, (half, v) in enumerate(((0, 0), (1, 1), (1, 2))):
                            nc.vector.tensor_tensor(w.xc[:, 0:C, :], hedge[:, half * C:(half + 1) * C, :],
                                                    bc_tile(g.watt[:, v, :], C), ALU.mult)
                            dve.drain()
                            nc.vector.tensor_reduce(dots[:, k, :], w.xc[:, 0:C, :], AX.X, ALU.add)
                            dve.drain()
                        nc.vector.tensor_tensor(dots[:, 3, :], dots[:, 0, :], dots[:, 1, :], ALU.add)
                        dve.drain()
                        nc.vector.scalar_tensor_tensor(out=g.e_edge[:, bass.ds(c * C, C)], in0=dots[:, 3, :], scalar=0.2,
                                                       in1=dots[:, 3, :], op0=ALU.mult, op1=ALU.max)
                        nc.vector.scalar_tensor_tensor(out=g.e_self[:, bass.ds(c * C, C)], in0=dots[:, 2, :], scalar=0.2,
                                                       in1=dots[:, 2, :], op0=ALU.mult, op1=ALU.max)
                        dve.drain().then_inc(h_edge_ready, 1)

                    node_a(0)
                    edges()
                    node_b(0)
                    node_a(1)
                    node_c(0)
                    node_b(1)
                    node_c(1)

        @block.scalar
        def _(act):
            act.sem_inc(ring_free, 2)
            with act.Fori(0, PAIRS) as i:
                for a in range(2):
                    def turn(n):
                        act.wait_ge(turned, n + 1)
                        nc.scalar.copy(tsb[:], pT[:, 0:Q * P]).then_inc(turned_sb, 1)

                    def hidden(m):
                        k = i * 4 + (2 * a + m)
                        for half in range(2):
                            act.wait_ge(hid_done, k * 2 + (half + 1))
                            nc.scalar.activation(hid[:, half, :], pH[:, 0:Q * P], ACT.Relu,
                                                 bias=g.b1col[:, 0:1]).then_inc(hid_sb, 1)

                    act_norm(nc, act, w, C, i * 10 + 5 * a)
                    turn(i * 8 + 4 * a)
                    act_norm(nc, act, w, 2 * C, i * 10 + (5 * a + 1))
                    act_norm(nc, act, w, C, i * 10 + (5 * a + 2))
                    turn(i * 8 + (4 * a + 1))
                    hidden(0)
                    act_norm(nc, act, w, C, i * 10 + (5 * a + 3))
                    turn(i * 8 + (4 * a + 2))
                    act.wait_ge(h_edge_ready, i * 2 + (a + 1))
                    nc.scalar.copy(g.agg[:, bass.ds(i * (2 * C) + a * C, C), :], hedge[:, 0:C, :])
                    nc.scalar.copy(g.xd[:, bass.ds(i * (2 * C) + a * C, C), :], ring[:, a, 1])
                    act.drain().then_inc(ring_free, 1)
                    act_norm(nc, act, w, C, i * 10 + (5 * a + 4))
                    turn(i * 8 + (4 * a + 3))
                    hidden(1)

        @block.tensor
        def _(pe):
            with pe.Fori(0, PAIRS) as i:
                for a in range(2):
                    for m in range(2):
                        k = i * 4 + (2 * a + m)
                        pe.wait_ge(h0_ready, k + 1)
                        pe_quads(nc, pT, hd[:, 0], g.ident[:], Q, turned)
                        pe.wait_ge(turned_sb, k * 2 + 1)
                        for q in range(Q):
                            o = pW[:, q * P:(q + 1) * P]
                            nc.tensor.matmul(o, tsb[:, q * P:(q + 1) * P], g.w0[:], start=True, stop=False)
                            last = nc.tensor.matmul(o, g.ones[0:1, :], g.bias0[:], start=False, stop=True)
                        last.then_inc(w_done, 1)
                        pe.wait_ge(h1_ready, k + 1)
                        pe_quads(nc, pT, hd[:, 1], g.ident[:], Q, turned)
                        pe.wait_ge(turned_sb, k * 2 + 2)
                        for half in range(2):
                            if half:
                                pe.wait_ge(hid_sb, k * 2 + 1)
                            for s in range(Q):
                                r = half * Q + s
                                last = nc.tensor.matmul(pH[:, s * P:(s + 1) * P], g.w1r[:, r % 2, :],
                                                        tsb[:, (r // 2) * P:(r // 2 + 1) * P], start=True, stop=True)
                            last.then_inc(hid_done, 1)
                        for half in range(2):
                            pe.wait_ge(hid_sb, k * 2 + (half + 1))
                            if half:
                                pe.wait_ge(gr_used, k * 2 + 1)
                            for s in range(Q):
                                o = pG[:, s * P:(s + 1) * P]
                                nc.tensor.matmul(o, hid[:, half, s * P:(s + 1) * P], g.w1gr[:], start=True, stop=False)
                                last = nc.tensor.matmul(o, g.ones[0:1, :], g.b1gr[:], start=False, stop=True)
                            last.then_inc(gr_done, 1)


def stage_softmax(nc, g):
    with ExitStack() as ctx:
        sb = lambda name: ctx.enter_context(nc.sbuf_tensor(f"sm_{name}", [P, ET], f32))
        top, most, negcut, precut = sb("top"), sb("most"), sb("negcut"), sb("precut")
        with ExitStack() as inner:
            block = inner.enter_context(nc.Block())

            @block.vector
            def _(dve):
                nc.vector.tensor_scalar(negcut[:], g.same[:], -NEG, NEG, ALU.mult, ALU.add)
                nc.vector.tensor_scalar(precut[:], g.pre[:], -NEG, NEG, ALU.mult, ALU.add)
                nc.vector.tensor_tensor(top[:], g.e_edge[:], g.e_self[:], ALU.max)
                dve.drain()
                nc.vector.tensor_tensor_scan(most[:], negcut[:], top[:], NEG, ALU.add, ALU.max)

        stage_carry(nc, g, "sm_max", [most[:, ET - 1:ET]], greatest=True)
        with ExitStack() as inner:
            block = inner.enter_context(nc.Block())

            @block.vector
            def _(dve):
                nc.vector.scalar_tensor_tensor(out=most[:], in0=precut[:], scalar=g.carry[:, 0:1], in1=most[:],
                                               op0=ALU.add, op1=ALU.max)
                dve.drain()
                nc.vector.tensor_tensor(most[:], most[:], g.end[:], ALU.mult)
                dve.drain()
                nc.vector.tensor_tensor_scan(top[:, ::-1], g.more[:, ::-1], most[:, ::-1], 0.0, ALU.mult, ALU.add)

        stage_carry(nc, g, "sm_back", [top[:, 0:1]], reverse=True)
        less, raised = g.sem("sm_less"), g.sem("sm_raised")
        with ExitStack() as inner:
            block = inner.enter_context(nc.Block())

            @block.vector
            def _(dve):
                nc.vector.scalar_tensor_tensor(out=top[:], in0=g.suf[:], scalar=g.carry_back[:, 0:1], in1=top[:],
                                               op0=ALU.mult, op1=ALU.add)
                dve.drain()
                nc.vector.tensor_tensor(g.e_edge[:], g.e_edge[:], top[:], ALU.subtract)
                nc.vector.tensor_tensor(g.e_self[:], g.e_self[:], top[:], ALU.subtract).then_inc(less, 1)
                dve.wait_ge(raised, 2)
                nc.vector.tensor_tensor_scan(g.rden[:], g.same[:], g.e_edge[:], 0.0, ALU.mult, ALU.add)
                nc.vector.tensor_tensor(g.agg[:], g.agg[:], bc_feat(g.e_edge[:]), ALU.mult)
                dve.drain()
                for f in range(F):
                    nc.vector.tensor_tensor_scan(g.agg[:, :, f], g.same[:], g.agg[:, :, f], 0.0, ALU.mult, ALU.add)

            @block.scalar
            def _(act):
                act.wait_ge(less, 1)
                nc.scalar.activation(g.e_edge[:], g.e_edge[:], ACT.Exp).then_inc(raised, 1)
                nc.scalar.activation(g.e_self[:], g.e_self[:], ACT.Exp).then_inc(raised, 1)

        stage_carry(nc, g, "sm_sum", [g.agg[:, ET - 1, :], g.rden[:, ET - 1:ET]])
        with ExitStack() as inner:
            block = inner.enter_context(nc.Block())

            @block.vector
            def _(dve):
                nc.vector.scalar_tensor_tensor(out=g.rden[:], in0=g.pre[:], scalar=g.carry[:, F:F + 1], in1=g.rden[:],
                                               op0=ALU.mult, op1=ALU.add)
                dve.drain()
                nc.vector.tensor_tensor(g.rden[:], g.rden[:], g.e_self[:], ALU.add)
                dve.drain()
                nc.vector.reciprocal(g.rden[:], g.rden[:])
                dve.drain()
                nc.vector.tensor_tensor(g.e_self[:], g.e_self[:], g.rden[:], ALU.mult)


class Scatter:

    def __init__(self, nc, ctx, g, stage, width=F):
        self.rows = ctx.enter_context(nc.sbuf_tensor(f"{stage}_out_rows", [P, 2, C, width], f32))
        self.idx = ctx.enter_context(nc.sbuf_tensor(f"{stage}_out_idx", [P, 2, C], i32))
        self.idx_here, self.done, self.ready, self.free = g.scatter_sems
        self.n = g.scatters
        g.scatters += 1

    def wait_idx(self, eng, i, a):
        eng.wait_ge(self.idx_here[a], i * 16 + 16 * (PAIRS * self.n + 1))

    def wait_done(self, eng, i, a):
        eng.wait_ge(self.done[a], i * ONCE + ONCE * (PAIRS * self.n + 1))

    def wait_ready(self, eng, c):
        eng.wait_ge(self.ready, c + (EC * self.n + 1))

    def wait_free(self, eng, c):
        eng.wait_ge(self.free, c + (EC * self.n + 1))


ONCE = 16 * C


def sp_scatter(g, sp, s):

    def load(c, a):
        sp.dma_start(s.idx[:, a, :], g.end_index[:, bass.ds(c * C, C)]).then_inc(s.idx_here[a], 16)

    load(0, 0)
    load(1, 1)
    with sp.Fori(0, PAIRS - 1) as i:
        for a in range(2):
            s.wait_done(sp, i, a)
            sp.sem_inc(s.free, 1)
            load(i * 2 + (a + 2), a)
    for a in range(2):
        s.wait_done(sp, PAIRS - 1, a)
        sp.sem_inc(s.free, 1)


def pool_scatter(nc, g, pool, s, table):
    with pool.Fori(0, PAIRS) as i:
        for a in range(2):
            s.wait_idx(pool, i, a)
            s.wait_ready(pool, i * 2 + a)
            pool_wait(g, pool)
            for t in range(C):
                pool.indirect_dma_start(
                    out=table, out_offset=bass.IndirectOffsetOnAxis(ap=s.idx[:, a, t:t + 1], axis=0),
                    in_=s.rows[:, a, t, :], in_offset=None, bounds_check=NPAD - 1, oob_is_err=False,
                ).then_inc(s.done[a], 16)


def dve_true_sum(nc, dve, g, tmp, c, lo=0, hi=F):
    part = bass.ds(c * C, C)
    nc.vector.tensor_tensor(tmp, bc_tile(g.carry[:, lo:hi], C), bc_feat(g.pre[:, part], hi - lo), ALU.mult)
    dve.drain()
    nc.vector.tensor_tensor(tmp, tmp, g.agg[:, part, lo:hi], ALU.add)
    dve.drain()


def stage_scatter_x1(nc, g):
    st = "s2"
    with ExitStack() as ctx:
        w = Norm(nc, ctx, g, st, C, EC)
        s = Scatter(nc, ctx, g, st)
        z = ctx.enter_context(nc.sbuf_tensor("s2_z", [P, C, F], f32))
        hd = ctx.enter_context(nc.sbuf_tensor("s2_h_dst", [P, C, F], f32))
        tsb = ctx.enter_context(nc.sbuf_tensor("s2_z_T", [P, Q * P], f32))
        pT = ctx.enter_context(nc.psum_tensor("s2_pT", [P, 1024], f32))
        pW = ctx.enter_context(nc.psum_tensor("s2_pW", [P, 1024], f32))
        z_ready, turned, turned_sb, w_done = (g.sem(f"{st}_{x}") for x in ("z_ready", "turned", "turned_sb", "w_done"))
        block = ctx.enter_context(nc.Block())

        @block.sync
        def _(sp):
            sp_scatter(g, sp, s)

        @block.gpsimd
        def _(pool):
            pool_scatter(nc, g, pool, s, g.X1)

        @block.vector
        def _(dve):
            with dve.Fori(0, PAIRS) as i:
                for a in range(2):
                    c = i * 2 + a
                    part = bass.ds(c * C, C)
                    dve_norm(nc, dve, w, g.xd[:, part, :], hd[:], C, c)
                    nc.vector.tensor_tensor(hd[:], hd[:], bc_feat(g.e_self[:, part]), ALU.mult)
                    dve_true_sum(nc, dve, g, z[:], c)
                    nc.vector.tensor_tensor(z[:], z[:], bc_feat(g.rden[:, part]), ALU.mult)
                    dve.drain()
                    nc.vector.tensor_tensor(z[:], z[:], hd[:], ALU.add).then_inc(z_ready, 1)
                    dve.wait_ge(w_done, c + 1)
                    s.wait_free(dve, c)
                    nc.vector.tensor_tensor(s.rows[:, a], g.xd[:, part, :],
                                            pW[:, 0:C * F].rearrange("p (t f) -> p t f", f=F), ALU.add).then_inc(s.ready, 1)

        @block.scalar
        def _(act):
            with act.Fori(0, PAIRS) as i:
                for a in range(2):
                    c = i * 2 + a
                    act_norm(nc, act, w, C, c)
                    act.wait_ge(turned, c + 1)
                    nc.scalar.copy(tsb[:], pT[:, 0:Q * P]).then_inc(turned_sb, 1)
                    s.wait_ready(act, c)
                    nc.scalar.copy(g.xd[:, bass.ds(c * C, C), :], s.rows[:, a])

        @block.tensor
        def _(pe):
            with pe.Fori(0, PAIRS) as i:
                for a in range(2):
                    c = i * 2 + a
                    pe.wait_ge(z_ready, c + 1)
                    pe_quads(nc, pT, z, g.ident[:], Q, turned)
                    pe.wait_ge(turned_sb, c + 1)
                    for q in range(Q):
                        o = pW[:, q * P:(q + 1) * P]
                        nc.tensor.matmul(o, tsb[:, q * P:(q + 1) * P], g.w0[:], start=True, stop=False)
                        last = nc.tensor.matmul(o, g.ones[0:1, :], g.bias0[:], start=False, stop=True)
                    last.then_inc(w_done, 1)


def stage_gather(nc, g, st, table, norm, lo=0, hi=F, first=None):
    K = hi - lo
    with ExitStack() as ctx:
        w = Norm(nc, ctx, g, st, C, EC) if norm else None
        sb = lambda name, shape, dt=f32: ctx.enter_context(nc.sbuf_tensor(f"{st}_{name}", shape, dt))
        ring = sb("ring", [P, 2, C, F])
        idx = sb("idx", [P, 2, C], i32)
        h = sb("h_src", [P, C, K]) if norm else None
        run = sb("running", [P, 2, C, K])
        idx_here = [g.sem(f"{st}_idx_here{a}") for a in range(2)]
        rows = [g.sem(f"{st}_rows{a}") for a in range(2)]
        ring_free, run_ready, run_free = (g.sem(f"{st}_{x}") for x in ("ring_free", "run_ready", "run_free"))
        block = ctx.enter_context(nc.Block())

        @block.sync
        def _(sp):
            def load(c, a):
                sp.dma_start(idx[:, a, :], g.src[:, bass.ds(c * C, C)]).then_inc(idx_here[a], 16)

            load(0, 0)
            load(1, 1)
            with sp.Fori(0, PAIRS - 1) as i:
                for a in range(2):
                    sp.wait_ge(rows[a], i * ONCE + ONCE)
                    load(i * 2 + (a + 2), a)

        @block.gpsimd
        def _(pool):
            with pool.Fori(0, PAIRS) as i:
                for a in range(2):
                    pool_wait(g, pool, (idx_here[a], i * 16 + 16), (ring_free, i * 2 + (a + 1)))
                    for t in range(C):
                        pool.indirect_dma_start(
                            out=ring[:, a, t, :], out_offset=None, in_=table,
                            in_offset=bass.IndirectOffsetOnAxis(ap=idx[:, a, t:t + 1], axis=0),
                        ).then_inc(rows[a], 16)

        @block.vector
        def _(dve):
            dve.sem_inc(ring_free, 2)
            nc.vector.memset(run[:, 1, C - 1, :], 0.0)
            dve.drain()
            if first is not None:
                first(dve)
            with dve.Fori(0, PAIRS) as i:
                for a in range(2):
                    c = i * 2 + a
                    part = bass.ds(c * C, C)
                    dve.wait_ge(rows[a], i * ONCE + ONCE)
                    if norm:
                        dve_norm(nc, dve, w, ring[:, a], h[:], C, c, lo=lo, hi=hi)
                        dve.drain().then_inc(ring_free, 1)
                    dve.wait_ge(run_free, c + 1)
                    for f in range(K):
                        v = h[:, :, f] if norm else ring[:, a, :, lo + f]
                        nc.vector.tensor_tensor_scan(run[:, a, :, f], g.same[:, part], v, run[:, 1 - a, C - 1, f:f + 1],
                                                     ALU.mult, ALU.add)
                    dve.drain().then_inc(run_ready, 1)
                    if not norm:
                        dve.drain().then_inc(ring_free, 1)

        @block.scalar
        def _(act):
            act.sem_inc(run_free, 2)
            with act.Fori(0, PAIRS) as i:
                for a in range(2):
                    c = i * 2 + a
                    if norm:
                        act_norm(nc, act, w, C, c)
                    act.wait_ge(run_ready, c + 1)
                    nc.scalar.copy(g.agg[:, bass.ds(c * C, C), 0:K], run[:, a]).then_inc(run_free, 1)


def stage_scatter_g(nc, g):
    st = "s4"
    with ExitStack() as ctx:
        sb = lambda name, shape: ctx.enter_context(nc.sbuf_tensor(f"{st}_{name}", shape, f32))
        pb = lambda name: ctx.enter_context(nc.psum_tensor(f"{st}_{name}", [P, 1024], f32))
        S = lambda name: g.sem(f"{st}_{name}")
        w = Norm(nc, ctx, g, st, C, EC)
        s = Scatter(nc, ctx, g, st)
        mean, hd = sb("mean", [P, C, F]), sb("h_dst", [P, C, F])
        tsb, hid = sb("T", [P, 2, Q * P]), sb("hid_T", [P, 2, Q * P])
        pT, pU, pH, pG = pb("pT"), pb("pU"), pb("pH"), pb("pG")
        ready, turned, turned_sb, hid_done, hid_sb, gr_done, gr_used = (
            S(x) for x in ("ready", "turned", "turned_sb", "hid_done", "hid_sb", "gr_done", "gr_used"))
        block = ctx.enter_context(nc.Block())

        @block.sync
        def _(sp):
            sp_scatter(g, sp, s)

        @block.gpsimd
        def _(pool):
            pool_scatter(nc, g, pool, s, g.G)

        @block.vector
        def _(dve):
            with dve.Fori(0, PAIRS) as i:
                for a in range(2):
                    c = i * 2 + a
                    dve_true_sum(nc, dve, g, mean[:], c)
                    nc.vector.tensor_tensor(mean[:], mean[:], bc_feat(g.rdeg[:, bass.ds(c * C, C)]), ALU.mult).then_inc(ready, 1)
                    dve_norm(nc, dve, w, g.xd[:, bass.ds(c * C, C), :], hd[:], C, c, ready)
                    s.wait_free(dve, c)
                    for half in range(2):
                        H = C // 2
                        part = bass.ds(c * C + half * H, H)
                        dve.wait_ge(gr_done, c * 2 + (half + 1))
                        pv = pG[:, 0:H * 2 * F].rearrange("p (t c) -> p t c", c=2 * F)
                        nc.vector.tensor_copy(s.rows[:, a, half * H:(half + 1) * H, :], pv[:, :, 0:F])
                        nc.vector.tensor_tensor(g.xd[:, part, :], g.xd[:, part, :], pv[:, :, F:2 * F], ALU.add)
                        dve.drain().then_inc(gr_used, 1)
                    dve.drain().then_inc(s.ready, 1)

        @block.scalar
        def _(act):
            with act.Fori(0, PAIRS) as i:
                for a in range(2):
                    c = i * 2 + a
                    act_norm(nc, act, w, C, c)
                    for k, p in enumerate((pT, pU)):
                        act.wait_ge(turned, c * 2 + (k + 1))
                        nc.scalar.copy(tsb[:, k, :], p[:, 0:Q * P]).then_inc(turned_sb, 1)
                    for half in range(2):
                        act.wait_ge(hid_done, c * 2 + (half + 1))
                        nc.scalar.activation(hid[:, half, :], pH[:, 0:Q * P], ACT.Relu, bias=g.b1col[:, 0:1]).then_inc(hid_sb, 1)

        @block.tensor
        def _(pe):
            with pe.Fori(0, PAIRS) as i:
                for a in range(2):
                    c = i * 2 + a
                    pe.wait_ge(ready, c * 2 + 1)
                    pe_quads(nc, pT, mean, g.ident[:], Q, turned)
                    pe.wait_ge(ready, c * 2 + 2)
                    pe_quads(nc, pU, hd, g.ident[:], Q, turned)
                    pe.wait_ge(turned_sb, c * 2 + 2)
                    for half in range(2):
                        if half:
                            pe.wait_ge(hid_sb, c * 2 + 1)
                        for k in range(Q):
                            r = half * Q + k
                            q = slice((r // 2) * P, (r // 2 + 1) * P)
                            o = pH[:, k * P:(k + 1) * P]
                            nc.tensor.matmul(o, g.w1l[:, r % 2, :], tsb[:, 0, q], start=True, stop=False)
                            last = nc.tensor.matmul(o, g.w1r[:, r % 2, :], tsb[:, 1, q], start=False, stop=True)
                        last.then_inc(hid_done, 1)
                    for half in range(2):
                        pe.wait_ge(hid_sb, c * 2 + (half + 1))
                        if half:
                            pe.wait_ge(gr_used, c * 2 + 1)
                        for k in range(Q):
                            o = pG[:, k * P:(k + 1) * P]
                            nc.tensor.matmul(o, hid[:, half, k * P:(k + 1) * P], g.w1gr[:], start=True, stop=False)
                            last = nc.tensor.matmul(o, g.ones[0:1, :], g.b1gr[:], start=False, stop=True)
                        last.then_inc(gr_done, 1)


def stage_scatter_x2(nc, g):
    st = "s6"
    with ExitStack() as ctx:
        w = Norm(nc, ctx, g, st, C, EC)
        s = Scatter(nc, ctx, g, st)
        tmp = ctx.enter_context(nc.sbuf_tensor("s6_mean", [P, C, F], f32))
        block = ctx.enter_context(nc.Block())

        @block.sync
        def _(sp):
            sp_scatter(g, sp, s)

        @block.gpsimd
        def _(pool):
            pool_scatter(nc, g, pool, s, g.X2)

        @block.vector
        def _(dve):
            with dve.Fori(0, PAIRS) as i:
                for a in range(2):
                    c = i * 2 + a
                    part = bass.ds(c * C, C)
                    dve_true_sum(nc, dve, g, tmp[:], c)
                    nc.vector.tensor_tensor(tmp[:], tmp[:], bc_feat(g.rdeg[:, part]), ALU.mult)
                    dve.drain()
                    s.wait_free(dve, c)
                    nc.vector.tensor_tensor(s.rows[:, a], g.xd[:, part, :], tmp[:], ALU.add)
                    dve.drain().then_inc(s.ready, 1)
                    dve_norm(nc, dve, w, s.rows[:, a], tmp[:, :, CON:F], C, c, lo=CON, hi=F)
                    nc.vector.tensor_tensor(g.con[:, part, :], tmp[:, :, CON:F], bc_feat(g.end[:, part], CON), ALU.mult)
                    dve.drain()

        @block.scalar
        def _(act):
            with act.Fori(0, PAIRS) as i:
                for a in range(2):
                    act_norm(nc, act, w, C, i * 2 + a)


def stage_symmetric(nc, g):
    st = "s8"
    with ExitStack() as ctx:
        sb = lambda name, shape, dt=f32: ctx.enter_context(nc.sbuf_tensor(f"{st}_{name}", shape, dt))
        S = lambda name: g.sem(f"{st}_{name}")
        s = Scatter(nc, ctx, g, st, CW)
        srcb = sb("src_rows", [P, C, P], i32)
        srcc = sb("src_cols", [P, 2, C], i32)
        eq = sb("equal", [P, C, P])
        eqb = sb("equal_before", [P, C, P])
        val = sb("values", [P, C, CW])
        add = sb("add_rows", [P, 2, C, CW])
        aidx = sb("add_idx", [P, 2, C], i32)
        rank, srcf = sb("rank", [P, C]), sb("src_f", [P, C])
        trash, trash_i = sb("trash", [P, 1]), sb("trash_i", [P, 1], i32)
        pS = ctx.enter_context(nc.psum_tensor("s8_pS", [P, 512], f32))
        here, used, eq_ready, summed, add_ready, trash_set = (
            S(x) for x in ("src_here", "src_used", "eq_ready", "summed", "add_ready", "trash_set"))
        idx_ready, add_free = S("add_idx_ready"), S("add_free")
        added = [S("added_a"), S("added_b")]
        block = ctx.enter_context(nc.Block())
        tables = (g.sum_a, g.sum_b)
        PER = 16 * C

        @block.sync
        def _(sp):
            def load(c, a):
                sp.dma_start(s.idx[:, a, :], g.end_index[:, bass.ds(c * C, C)]).then_inc(s.idx_here[a], 16)

            def load_src(c, a):
                sp.wait_ge(used, c + 1)
                sp.dma_start(srcb[:].rearrange("p t k -> p (t k)"),
                             g.src_rows[bass.ds(c * (C * P), C * P)].partition_broadcast(P)).then_inc(here, 16)
                sp.dma_start(srcc[:, a, :], g.src[:, bass.ds(c * C, C)]).then_inc(here, 16)

            sp.sem_inc(add_free, 2)
            load(0, 0)
            load(1, 1)
            with sp.Fori(0, PAIRS - 1) as i:
                load_src(i * 2, 0)
                load_src(i * 2 + 1, 1)
                for a in range(2):
                    s.wait_done(sp, i, a)
                    sp.sem_inc(s.free, 1)
                    load(i * 2 + (a + 2), a)
                for b in range(2):
                    sp.wait_ge(added[b], i * PER + PER)
                sp.sem_inc(add_free, 2)
            load_src(EC - 2, 0)
            load_src(EC - 1, 1)
            for a in range(2):
                s.wait_done(sp, PAIRS - 1, a)
                sp.sem_inc(s.free, 1)
                sp.wait_ge(added[a], PAIRS * PER)

        @block.gpsimd
        def _(pool):
            nc.gpsimd.iota(trash_i[:], pattern=[[0, 1]], base=NPAD, channel_multiplier=1)
            pool.drain()
            nc.gpsimd.tensor_copy(trash[:], trash_i[:])
            pool.drain().then_inc(trash_set, 1)
            with pool.Fori(0, PAIRS) as i:
                for a in range(2):
                    c = i * 2 + a
                    s.wait_idx(pool, i, a)
                    s.wait_ready(pool, c)
                    pool_wait(g, pool)
                    for t in range(C):
                        pool.indirect_dma_start(
                            out=g.sum_dst, out_offset=bass.IndirectOffsetOnAxis(ap=s.idx[:, a, t:t + 1], axis=0),
                            in_=s.rows[:, a, t, :], in_offset=None, bounds_check=NPAD - 1, oob_is_err=False,
                        ).then_inc(s.done[a], 16)
                        if t == 0:
                            pool_wait(g, pool, (idx_ready, c + 1), (add_ready, c + 1))
                        b, turn = t % 2, (a * C + t) // 2
                        if turn:
                            pool_wait(g, pool, (added[b], i * PER + 16 * turn))
                        pool.indirect_dma_start(
                            out=tables[b], out_offset=bass.IndirectOffsetOnAxis(ap=aidx[:, a, t:t + 1], axis=0),
                            in_=add[:, a, t, :], in_offset=None, bounds_check=NTRASH - 1, oob_is_err=True,
                            compute_op=ALU.add,
                        ).then_inc(added[b], 16)
                for b in range(2):
                    pool.wait_ge(added[b], i * PER + PER)

        @block.vector
        def _(dve):
            dve.sem_inc(used, 1)
            nc.vector.memset(val[:], 1.0)
            dve.drain()
            dve.wait_ge(trash_set, 1)
            with dve.Fori(0, PAIRS) as i:
                for a in range(2):
                    c = i * 2 + a
                    part = bass.ds(c * C, C)
                    s.wait_free(dve, c)
                    dve_true_sum(nc, dve, g, s.rows[:, a, :, 0:CON], c, 0, CON)
                    nc.vector.tensor_copy(s.rows[:, a, :, CON:CW], g.deg[:, part].unsqueeze(2))
                    dve.drain().then_inc(s.ready, 1)
                    nc.vector.tensor_tensor(val[:, :, 0:CON], bc_tile(g.carry_back[:, 0:CON], C),
                                            bc_feat(g.suf[:, part], CON), ALU.mult)
                    dve.drain()
                    nc.vector.tensor_tensor(val[:, :, 0:CON], val[:, :, 0:CON], g.con[:, part, :], ALU.add)
                    dve.wait_ge(here, c * 32 + 32)
                    nc.vector.tensor_copy(srcf[:], srcc[:, a, :])
                    dve.drain()
                    nc.vector.tensor_tensor(eq[:], srcb[:], bc_feat(srcf[:], P), ALU.is_equal)
                    dve.drain().then_inc(eq_ready, 1)
                    dve.drain().then_inc(used, 1)
                    nc.vector.tensor_tensor(eqb[:], eq[:], bc_tile(g.before[:], C), ALU.mult)
                    dve.drain()
                    nc.vector.tensor_reduce(rank[:], eqb[:], AX.X, ALU.add)
                    dve.drain()
                    nc.vector.tensor_scalar(srcf[:], srcf[:], trash[:, 0:1], None, ALU.subtract)
                    dve.drain()
                    nc.vector.scalar_tensor_tensor(out=srcf[:], in0=rank[:], scalar=0.0, in1=srcf[:], op0=ALU.is_equal,
                                                   op1=ALU.mult)
                    dve.drain()
                    dve.wait_ge(add_free, c + 1)
                    nc.vector.tensor_scalar(aidx[:, a, :], srcf[:], trash[:, 0:1], None, ALU.add).then_inc(idx_ready, 1)
                    dve.wait_ge(summed, c + 1)

        @block.tensor
        def _(pe):
            with pe.Fori(0, PAIRS) as i:
                for a in range(2):
                    c = i * 2 + a
                    pe.wait_ge(eq_ready, c + 1)
                    if a:
                        pe.wait_ge(add_ready, c)
                    for t in range(C):
                        last = nc.tensor.matmul(pS[:, t * CW:(t + 1) * CW], eq[:, t, :], val[:, t, :], start=True, stop=True)
                    last.then_inc(summed, 1)
                pe.wait_ge(add_ready, i * 2 + 2)

        @block.scalar
        def _(act):
            with act.Fori(0, PAIRS) as i:
                for a in range(2):
                    c = i * 2 + a
                    act.wait_ge(summed, c + 1)
                    act.wait_ge(add_free, c + 1)
                    nc.scalar.copy(add[:, a].rearrange("p t w -> p (t w)"), pS[:, 0:C * CW]).then_inc(add_ready, 1)


def stage_third_layer(nc, g):
    st = "s9"
    with ExitStack() as ctx:
        sb = lambda name, shape: ctx.enter_context(nc.sbuf_tensor(f"{st}_{name}", shape, f32))
        S = lambda name: g.sem(f"{st}_{name}")
        w = Norm(nc, ctx, g, st, C, NC)
        x2 = sb("x2", [P, 3, C, F])
        x3 = sb("x3", [P, 2, C, F])
        sums = sb("sums", [P, 2, 3, C, CW])
        deg = sb("deg", [P, C])
        comb = sb("combined", [P, 2, C, F])
        tsb = sb("T", [P, Q * P])
        hid = sb("hid_T", [P, 2, Q * P])
        pb = lambda name: ctx.enter_context(nc.psum_tensor(f"{st}_{name}", [P, 1024], f32))
        pT, pH, pO = pb("pT"), [pb("pH0"), pb("pH1")], pb("pO")
        here = [S("here0"), S("here1")]
        comb_ready, turned, turned_sb, hid_done, hid_sb = (S(x) for x in ("comb_ready", "turned", "turned_sb", "hid_done", "hid_sb"))
        out_done, x3_ready, sums_used, x3_free = (S(x) for x in ("out_done", "x3_ready", "sums_used", "x3_free"))
        stored = S("stored")
        block = ctx.enter_context(nc.Block())
        HALF = NC // 2

        def cols(t, k, width):
            return t[0:NPAD, :].rearrange("(p t) f -> p (t f)", p=P)[:, bass.ds(k * (C * width), C * width)]

        @block.sync
        def _(sp):
            def load(k, b):
                sp.wait_ge(sums_used, k + 1)
                sp.dma_start(x2[:, b].rearrange("p t f -> p (t f)"), cols(g.X2, k, F)).then_inc(here[b], 16)
                for j, table in enumerate((g.sum_dst, g.sum_a, g.sum_b)):
                    sp.dma_start(sums[:, b, j].rearrange("p t f -> p (t f)"), cols(table, k, CW)).then_inc(here[b], 16)

            sp.sem_inc(x3_free, 2)
            load(0, 0)
            load(1, 1)

            def turn(i, more):
                for b in range(2):
                    k = i * 2 + b
                    sp.wait_ge(x3_ready, k + 1)
                    sp.dma_start(cols(g.out, k, F), x3[:, b].rearrange("p t f -> p (t f)")).then_inc(stored, 16)
                    if more:
                        load(k + 2, b)
                    sp.wait_ge(stored, k * 16 + 16)
                    sp.sem_inc(x3_free, 1)

            with sp.Fori(0, HALF - 1) as i:
                turn(i, True)
            turn(HALF - 1, False)

        @block.vector
        def _(dve):
            dve.sem_inc(sums_used, 2)

            def first(k, b, i):
                dve.wait_ge(here[b], i * 64 + 64)
                dve_norm(nc, dve, w, x2[:, b], comb[:, b, :, 0:CON], C, k, lo=0, hi=CON)
                nc.vector.tensor_tensor(x2[:, b], x2[:, b], bc_tile(g.b2out[:], C), ALU.add)
                for j in (1, 2):
                    nc.vector.tensor_tensor(sums[:, b, 0], sums[:, b, 0], sums[:, b, j], ALU.add)
                    dve.drain()
                nc.vector.tensor_scalar(deg[:].unsqueeze(2), sums[:, b, 0, :, CON:CW], 1.0, None, ALU.max)
                dve.drain()
                nc.vector.reciprocal(deg[:], deg[:])
                dve.drain()
                nc.vector.tensor_tensor(comb[:, b, :, CON:F], sums[:, b, 0, :, 0:CON], bc_feat(deg[:], CON), ALU.mult)
                dve.drain().then_inc(comb_ready, 1)

            def second(k, b):
                dve.wait_ge(out_done, k + 1)
                dve.wait_ge(x3_free, k + 1)
                nc.vector.tensor_tensor(x3[:, b], x2[:, b], pO[:, 0:C * F].rearrange("p (t f) -> p t f", f=F), ALU.add)
                dve.drain().then_inc(x3_ready, 1)
                dve.drain().then_inc(sums_used, 1)

            first(0, 0, 0)
            with dve.Fori(0, HALF - 1) as i:
                first(i * 2 + 1, 1, i)
                second(i * 2, 0)
                first(i * 2 + 2, 0, i + 1)
                second(i * 2 + 1, 1)
            first(NC - 1, 1, HALF - 1)
            second(NC - 2, 0)
            second(NC - 1, 1)

        @block.scalar
        def _(act):
            def turn(k):
                act.wait_ge(turned, k + 1)
                nc.scalar.copy(tsb[:], pT[:, 0:Q * P]).then_inc(turned_sb, 1)

            def hidden(k):
                for u in range(4):
                    act.wait_ge(hid_done, k * 4 + (u + 1))
                    nc.scalar.activation(hid[:, u % 2, :], pH[u % 2][:, 0:Q * P], ACT.Relu, bias=g.b2col[:, 0:1]).then_inc(hid_sb, 1)

            act_norm(nc, act, w, C, 0)
            turn(0)
            with act.Fori(0, NC - 1) as k:
                act_norm(nc, act, w, C, k + 1)
                hidden(k)
                turn(k + 1)
            hidden(NC - 1)

        @block.tensor
        def _(pe):
            def quads(k, b):
                pe.wait_ge(comb_ready, k + 1)
                pe_quads(nc, pT, comb[:, b], g.ident[:], Q, turned)

            def hidden(k, u):
                if u == 0:
                    pe.wait_ge(turned_sb, k + 1)
                else:
                    pe.wait_ge(hid_sb, k * 4 + u)
                for v in range(Q):
                    t = u * Q + v
                    q, j = t // 4, t % 4
                    last = nc.tensor.matmul(pH[u % 2][:, v * P:(v + 1) * P], g.w2in[:, j, :],
                                            tsb[:, q * P:(q + 1) * P], start=True, stop=True)
                last.then_inc(hid_done, 1)

            def body(k):
                hidden(k, 0)
                for u in range(4):
                    if u < 3:
                        hidden(k, u + 1)
                    pe.wait_ge(hid_sb, k * 4 + (u + 1))
                    for v in range(Q):
                        t = u * Q + v
                        last = nc.tensor.matmul(pO[:, t * F:(t + 1) * F], hid[:, u % 2, v * P:(v + 1) * P], g.w2out[:],
                                                start=True, stop=True)
                last.then_inc(out_done, 1)

            quads(0, 0)
            with pe.Fori(0, HALF - 1) as i:
                body(i * 2)
                quads(i * 2 + 1, 1)
                pe.wait_ge(x3_ready, i * 2 + 1)
                body(i * 2 + 1)
                quads(i * 2 + 2, 0)
                pe.wait_ge(x3_ready, i * 2 + 2)
            body(NC - 2)
            quads(NC - 1, 1)
            pe.wait_ge(x3_ready, NC - 1)
            body(NC - 1)


def stage_relations(nc, g):
    st = "s10"
    with ExitStack() as ctx:
        sb = lambda name, shape, dt=f32: ctx.enter_context(nc.sbuf_tensor(f"{st}_{name}", shape, dt))
        S = lambda name: g.sem(f"{st}_{name}")
        w = Norm(nc, ctx, g, st, C, 2 * EC)
        ring = sb("ring", [P, 2, 2, C, F])
        idx = sb("idx", [P, 2, 2, C], i32)
        h = sb("h", [P, 2, C, F])
        etype = sb("etype", [NREL, C * P], i32)
        onehot = etype[:].bitcast(f32)
        z = sb("z", [P, 4, NB, F])
        tsb = sb("h_T", [P, 2, Q * P])
        zT = sb("z_T", [P, 2, 4 * P])
        xc = sb("x_hat_curr", [P, C, 2 * F])
        prod = w.sq
        msg = sb("msg", [P, C, F])
        att = sb("att", [P, 2, C])
        run = sb("running", [P, 2, C, F])
        pT = ctx.enter_context(nc.psum_tensor("s10_pT", [P, 1024], f32))
        pR = [ctx.enter_context(nc.psum_tensor(f"s10_pR{a}", [P, 512], f32)) for a in range(2)]
        pZ = [ctx.enter_context(nc.psum_tensor(f"s10_pZ{a}", [P, 512], f32)) for a in range(2)]
        pM = ctx.enter_context(nc.psum_tensor("s10_pM", [P, 1024], f32))
        idx_here, rows = [S("idx_here0"), S("idx_here1")], [S("rows0"), S("rows1")]
        (ring_free, type_here, type_free, h_ready, hot_ready, turned, turned_sb, rel_done, rel_used, xc_sb, z_ready,
         z_turned, z_sb, msg_done, msg_sb, scored, squashed, run_ready, run_free) = (S(x) for x in (
             "ring_free", "type_here", "type_free", "h_ready", "hot_ready", "turned", "turned_sb", "rel_done", "rel_used",
             "xc_sb", "z_ready", "z_turned", "z_sb", "msg_done", "msg_sb", "scored", "squashed", "run_ready", "run_free"))
        block = ctx.enter_context(nc.Block())
        GAT = 2 * ONCE

        @block.sync
        def _(sp):
            def load_idx(c, a):
                sp.dma_start(idx[:, a, 0, :], g.src[:, bass.ds(c * C, C)]).then_inc(idx_here[a], 16)
                sp.dma_start(idx[:, a, 1, :], g.dst[:, bass.ds(c * C, C)]).then_inc(idx_here[a], 16)

            def load_type(c):
                sp.wait_ge(type_free, c + 1)
                sp.dma_start(etype[:], g.etype_rows[bass.ds(c * (C * P), C * P)].partition_broadcast(NREL)).then_inc(type_here, 16)

            sp.sem_inc(type_free, 1)
            for a in range(2):
                load_idx(a, a)
            with sp.Fori(0, PAIRS - 1) as i:
                for a in range(2):
                    load_type(i * 2 + a)
                    sp.wait_ge(rows[a], i * GAT + GAT)
                    load_idx(i * 2 + (a + 2), a)
            load_type(EC - 2)
            load_type(EC - 1)

        @block.gpsimd
        def _(pool):
            with pool.Fori(0, PAIRS) as i:
                for a in range(2):
                    pool_wait(g, pool, (idx_here[a], i * 32 + 32), (ring_free, i * 2 + (a + 1)))
                    for t in range(C):
                        for k in range(2):
                            pool.indirect_dma_start(
                                out=ring[:, a, k, t, :], out_offset=None, in_=g.out,
                                in_offset=bass.IndirectOffsetOnAxis(ap=idx[:, a, k, t:t + 1], axis=0),
                            ).then_inc(rows[a], 16)

        @block.vector
        def _(dve):
            nc.vector.memset(run[:, 1, C - 1, :], 0.0)
            dve.drain()
            with dve.Fori(0, PAIRS) as i:
                for a in range(2):
                    c = i * 2 + a
                    part = bass.ds(c * C, C)
                    dve.wait_ge(rows[a], i * GAT + GAT)
                    for k in range(2):
                        dve_norm(nc, dve, w, ring[:, a, k], h[:, k], C, c * 2 + k, h_ready)
                    dve.wait_ge(type_here, c * 16 + 16)
                    nc.vector.tensor_scalar(onehot, etype[:], g.relid[:, 0:1], None, ALU.is_equal).then_inc(hot_ready, 1)
                    for q in range(Q):
                        r = pR[q % 2][:, 0:4 * RT].rearrange("p (t c) -> p t c", c=RT)
                        ts = slice(4 * q, 4 * q + 4)
                        dve.wait_ge(xc_sb, c * Q + (q + 1))
                        if q:
                            dve.wait_ge(z_turned, c * C + 4 * q)
                        nc.vector.tensor_tensor(z[:], r[:, :, 0:NB].unsqueeze(3).to_broadcast([P, 4, NB, F]),
                                                h[:, 0, ts, :].unsqueeze(2).to_broadcast([P, 4, NB, F]), ALU.mult).then_inc(z_ready, 1)
                        nc.vector.tensor_tensor(prod[:, ts, :], r[:, :, NB:NB + F], xc[:, ts, 0:F], ALU.mult)
                        dve.drain().then_inc(rel_used, 1)
                    nc.vector.tensor_reduce(att[:, 0, :], prod[:], AX.X, ALU.add)
                    dve.drain()
                    nc.vector.tensor_scalar(att[:, 0, :], att[:, 0, :], 1.0 / float(F) ** 0.5, 0.0, ALU.mult, ALU.max).then_inc(scored, 1)
                    nc.vector.tensor_tensor(xc[:, :, F:2 * F], xc[:, :, F:2 * F], bc_feat(g.end[:, part]), ALU.mult)
                    dve.wait_ge(squashed, c + 1)
                    dve.wait_ge(msg_sb, c + 1)
                    nc.vector.tensor_tensor(msg[:], msg[:], bc_feat(att[:, 1, :]), ALU.mult)
                    dve.drain()
                    nc.vector.tensor_tensor(msg[:], msg[:], xc[:, :, F:2 * F], ALU.add)
                    dve.drain()
                    dve.wait_ge(run_free, c + 1)
                    for f in range(F):
                        nc.vector.tensor_tensor_scan(run[:, a, :, f], g.same[:, part], msg[:, :, f], run[:, 1 - a, C - 1, f:f + 1],
                                                     ALU.mult, ALU.add)
                    dve.drain().then_inc(run_ready, 1)

        @block.scalar
        def _(act):
            act.sem_inc(run_free, 2)
            act.sem_inc(ring_free, 2)
            with act.Fori(0, PAIRS) as i:
                for a in range(2):
                    c = i * 2 + a
                    for k in range(2):
                        act_norm(nc, act, w, C, c * 2 + k)
                        act.wait_ge(turned, c * 2 + (k + 1))
                        nc.scalar.copy(tsb[:, k, :], pT[:, 0:Q * P]).then_inc(turned_sb, 1)
                    nc.scalar.copy(g.xd[:, bass.ds(c * C, C), :], ring[:, a, 1])
                    act.drain().then_inc(ring_free, 1)
                    for q in range(Q):
                        r = pR[q % 2][:, 0:4 * RT].rearrange("p (t c) -> p t c", c=RT)
                        act.wait_ge(rel_done, c * Q + (q + 1))
                        nc.scalar.copy(xc[:, 4 * q:4 * q + 4, :], r[:, :, NB + F:RT]).then_inc(xc_sb, 1)
                        for j in range(4):
                            act.wait_ge(z_turned, c * C + (4 * q + j + 1))
                            nc.scalar.copy(zT[:, j % 2, :], pZ[j % 2][:]).then_inc(z_sb, 1)
                    act.wait_ge(scored, c + 1)
                    nc.scalar.activation(att[:, 1, :], att[:, 0, :], ACT.Tanh).then_inc(squashed, 1)
                    act.wait_ge(msg_done, c + 1)
                    nc.scalar.copy(msg[:], pM[:, 0:C * F].rearrange("p (t f) -> p t f", f=F)).then_inc(msg_sb, 1)
                    act.wait_ge(run_ready, c + 1)
                    nc.scalar.copy(g.agg[:, bass.ds(c * C, C), :], run[:, a]).then_inc(run_free, 1)

        def message(pe, c, t):
            pe.wait_ge(z_sb, c * C + (t + 1))
            for u in range(4):
                last = nc.tensor.matmul(pM[:, t * F:(t + 1) * F], zT[:, t % 2, u * P:(u + 1) * P], g.w3[:, u, :],
                                        start=(u == 0), stop=(u == 3))
            if t == C - 1:
                last.then_inc(msg_done, 1)

        @block.tensor
        def _(pe):
            with pe.Fori(0, PAIRS) as i:
                for a in range(2):
                    c = i * 2 + a
                    for k in range(2):
                        pe.wait_ge(h_ready, c * 2 + (k + 1))
                        pe_quads(nc, pT, h[:, k], g.ident[:], Q, turned)
                        pe.wait_ge(turned_sb, c * 2 + (k + 1))
                    pe.wait_ge(hot_ready, c + 1)

                    def relations(q):
                        for j in range(4):
                            t, o = 4 * q + j, pR[q % 2][:, j * RT:(j + 1) * RT]
                            cols_q = slice(q * P, (q + 1) * P)
                            nc.tensor.matmul(o, onehot[:, t * P:(t + 1) * P], g.relrow[:], start=True, stop=False)
                            nc.tensor.matmul(o[:, NB:NB + F], tsb[:, 1, cols_q], g.w3y[:, j, :], start=False, stop=False)
                            last = nc.tensor.matmul(o[:, NB + F:RT], tsb[:, 0, cols_q], g.w3x[:, j, :], start=False, stop=True)
                        last.then_inc(rel_done, 1)

                    relations(0)
                    for q in range(Q):
                        if q + 1 < Q:
                            if q:
                                pe.wait_ge(rel_used, c * Q + q)
                            relations(q + 1)
                            if q + 2 == Q:
                                pe.drain().then_inc(type_free, 1)
                        pe.wait_ge(z_ready, c * Q + (q + 1))
                        for j in range(4):
                            t = 4 * q + j
                            if j >= 2:
                                pe.wait_ge(z_sb, c * C + (t - 1))
                            for u in range(4):
                                last = nc.tensor.transpose(pZ[j % 2][:, u * P:(u + 1) * P],
                                                           z[:, j, 4 * u:4 * u + 4, :].rearrange("p b f -> p (b f)"), g.ident[:])
                            last.then_inc(z_turned, 1)
                            if j:
                                message(pe, c, t - 1)
                        message(pe, c, 4 * q + 3)
                    pe.wait_ge(msg_sb, c + 1)


def stage_scatter_out(nc, g):
    with ExitStack() as ctx:
        s = Scatter(nc, ctx, g, "s11")
        tmp = ctx.enter_context(nc.sbuf_tensor("s11_sum", [P, C, F], f32))
        block = ctx.enter_context(nc.Block())

        @block.sync
        def _(sp):
            sp_scatter(g, sp, s)

        @block.gpsimd
        def _(pool):
            pool_scatter(nc, g, pool, s, g.out)

        @block.vector
        def _(dve):
            with dve.Fori(0, PAIRS) as i:
                for a in range(2):
                    c = i * 2 + a
                    dve_true_sum(nc, dve, g, tmp[:], c)
                    s.wait_free(dve, c)
                    nc.vector.scalar_tensor_tensor(out=s.rows[:, a], in0=tmp[:], scalar=0.0, in1=g.xd[:, bass.ds(c * C, C), :],
                                                   op0=ALU.max, op1=ALU.add)
                    dve.drain().then_inc(s.ready, 1)


def build(nc, A, stages=99, dbg=()):
    g = Globals()
    g.x, g.src, g.dst, g.dst_flat, g.src_rows, g.etype_rows = (
        A[k] for k in ("x", "src", "dst", "dst_flat", "src_rows", "etype_rows"))
    g.W, g.WT, g.att_src, g.att_dst, g.bias = (A[k] for k in ("W", "WT", "att_src", "att_dst", "bias"))
    g.W1_lT, g.W1_rT, g.L1_b1, g.W2_lT, g.W2_rT, g.L1_b2 = (A[k] for k in ("W1_lT", "W1_rT", "L1_b1", "W2_lT", "W2_rT", "L1_b2"))
    g.L2_W1, g.L2_b1, g.L2_W2, g.L2_b2 = (A[k] for k in ("L2_W1", "L2_b1", "L2_W2", "L2_b2"))
    g.weight, g.w_comp, g.slw, g.A1_wT, g.A1_b, g.A2_wT, g.A2_b, g.rel_emb = (
        A[k] for k in ("weight", "w_comp", "slw", "A1_wT", "A1_b", "A2_wT", "A2_b", "rel_emb"))
    g.out = A["out"]
    dram = lambda name, shape, dt=f32: nc.dram_tensor(name, shape, dt, kind="ExternalOutput" if name in dbg else "Internal").ap()
    g.X1, g.X2, g.G = (dram(n, (NPAD, F)) for n in ("x1_table", "x2_table", "g_table"))
    g.sum_dst, g.sum_a, g.sum_b = (dram(n, (NTRASH, CW)) for n in ("sum_dst_table", "sum_a_table", "sum_b_table"))
    g.end_index = dram("end_index_table", (P, ET), i32)
    with ExitStack() as ctx:
        g.sem = lambda name: ctx.enter_context(nc.semaphore(name))
        sb = lambda name, shape, dt=f32: ctx.enter_context(nc.sbuf_tensor(name, shape, dt))
        g.pool_steps = g.sem("pool_steps")
        g.norm_sems = [g.sem(f"norm_{x}") for x in ("centered", "squared", "summed", "rooted")]
        g.carry_sems = [g.sem(f"carry_{x}") for x in ("copied", "turned", "scanned", "back")]
        g.scatter_sems = ([g.sem(f"scatter_idx_here{a}") for a in range(2)], [g.sem(f"scattered{a}") for a in range(2)],
                          g.sem("scatter_rows_ready"), g.sem("scatter_rows_free"))
        g.norms = g.carries = g.scatters = 0
        g.xd = sb("x_dst", [P, ET, F])
        g.agg = sb("agg", [P, ET, F])
        g.same, g.more, g.end = (sb(n, [P, ET]) for n in ("same_as_before", "same_as_after", "is_last"))
        g.pre, g.suf = sb("same_from_start", [P, ET]), sb("same_to_end", [P, ET])
        g.deg, g.rdeg = sb("deg", [P, ET]), sb("rdeg", [P, ET])
        g.e_edge, g.e_self = sb("e_edge", [P, ET]), sb("e_self", [P, ET])
        g.preall, g.sufall = sb("preall", [CARRY, P]), sb("sufall", [CARRY, P])
        g.carry, g.carry_back = sb("carry", [P, CARRY]), sb("carry_back", [P, CARRY])
        g.ident, g.before, g.ones = sb("ident", [P, P]), sb("before", [P, P]), sb("ones", [1, P])
        g.relid, g.relid_i, g.eps = sb("relid", [NREL, 1]), sb("relid_i", [NREL, 1], i32), sb("eps", [P, 1])
        g.w0, g.bias0, g.watt = sb("w0", [P, P]), sb("bias0", [1, P]), sb("watt", [P, 3, F])
        g.w1l, g.w1r, g.w1gr = sb("w1l", [P, 2, P]), sb("w1r", [P, 2, P]), sb("w1gr", [P, P])
        g.b1col, g.b1gr = sb("b1col", [P, 1]), sb("b1gr", [1, P])
        g.w2in, g.w2out, g.b2col, g.b2out = sb("w2in", [P, 4, P]), sb("w2out", [P, F]), sb("b2col", [P, 1]), sb("b2out", [P, F])
        g.w3, g.w3x, g.w3y, g.relrow = sb("w3", [P, 4, F]), sb("w3x", [P, 4, 2 * F]), sb("w3y", [P, 4, F]), sb("relrow", [NREL, RT])
        stage_setup(nc, g)
        if stages < 1: return
        stage_first_gather(nc, g)
        if stages < 2: return
        g.rden = sb("rden", [P, ET])
        stage_softmax(nc, g)
        stage_scatter_x1(nc, g)
        if stages < 3: return
        stage_gather(nc, g, "s3", g.X1, norm=True)
        stage_carry(nc, g, "s3c", [g.agg[:, ET - 1, :]])
        stage_scatter_g(nc, g)
        if stages < 4: return
        stage_gather(nc, g, "s5", g.G, norm=False)
        stage_carry(nc, g, "s5c", [g.agg[:, ET - 1, :]])
        with ExitStack() as con:
            g.con = con.enter_context(nc.sbuf_tensor("conical_dst", [P, ET, CON], f32))
            stage_scatter_x2(nc, g)
            if stages < 5: return

            def spread(dve):
                for f in range(CON):
                    nc.vector.tensor_tensor_scan(g.con[:, ::-1, f], g.more[:, ::-1], g.con[:, ::-1, f], 0.0, ALU.mult, ALU.add)
                dve.drain()

            stage_gather(nc, g, "s7", g.X2, norm=True, lo=CON, hi=F, first=spread)
            stage_carry(nc, g, "s7c", [g.agg[:, ET - 1, 0:CON]])
            stage_carry(nc, g, "s7r", [g.con[:, 0, :]], reverse=True)
            stage_symmetric(nc, g)
        if stages < 6: return
        stage_third_layer(nc, g)
        if stages < 7: return
        stage_relations(nc, g)
        stage_carry(nc, g, "s10c", [g.agg[:, ET - 1, :]])
        stage_scatter_out(nc, g)


def kernel(x, src, dst, edge_type_86, L0_gnn_W, L0_gnn_att_src, L0_gnn_att_dst, L0_gnn_bias, L1_gnn_W1_l, L1_gnn_W1_r,
           L1_gnn_b1, L1_gnn_W2_l, L1_gnn_W2_r, L1_gnn_b2, L2_gnn_W1, L2_gnn_b1, L2_gnn_W2, L2_gnn_b2, L3_gnn_weight,
           L3_gnn_w_comp, L3_gnn_self_loop_weight, L3_gnn_A1_w, L3_gnn_A1_b, L3_gnn_A2_w, L3_gnn_A2_b, L3_gnn_rel_emb,
           launch=None):
    import numpy as np

    def rows(a, fill):
        a = np.asarray(a)
        out = np.full((EPAD,), fill, a.dtype)
        out[:E] = a
        return out

    src_p, dst_p, et_p = rows(src, N), rows(dst, N), rows(edge_type_86, 0)
    xp = np.zeros((NPAD, F), np.float32)
    xp[:N] = np.asarray(x)
    flat = np.full((EPAD + 2,), -1, np.int32)
    flat[1:-1] = dst_p
    T = lambda a: np.ascontiguousarray(np.asarray(a).T)
    arrays = {
        "x": xp, "src": src_p.reshape(P, ET), "dst": dst_p.reshape(P, ET), "dst_flat": flat,
        "src_rows": T(src_p.reshape(P, ET)).reshape(-1), "etype_rows": T(et_p.reshape(P, ET)).reshape(-1),
        "W": L0_gnn_W, "WT": T(L0_gnn_W), "att_src": L0_gnn_att_src, "att_dst": L0_gnn_att_dst, "bias": L0_gnn_bias,
        "W1_lT": T(L1_gnn_W1_l), "W1_rT": T(L1_gnn_W1_r), "L1_b1": L1_gnn_b1, "W2_lT": T(L1_gnn_W2_l),
        "W2_rT": T(L1_gnn_W2_r), "L1_b2": L1_gnn_b2, "L2_W1": L2_gnn_W1, "L2_b1": L2_gnn_b1, "L2_W2": L2_gnn_W2,
        "L2_b2": L2_gnn_b2, "weight": L3_gnn_weight, "w_comp": L3_gnn_w_comp, "slw": L3_gnn_self_loop_weight,
        "A1_wT": T(L3_gnn_A1_w), "A1_b": L3_gnn_A1_b, "A2_wT": T(L3_gnn_A2_w), "A2_b": L3_gnn_A2_b,
        "rel_emb": L3_gnn_rel_emb,
    }
    arrays = {k: np.ascontiguousarray(np.asarray(a)) for k, a in arrays.items()}
    import concourse.bacc as bacc
    from concourse.bass_utils import run_bass_kernel_spmd

    nc = bacc.Bacc("TRN2", target_bir_lowering=False, num_devices=1)
    A = {k: nc.dram_tensor(f"in_{k}", a.shape, mybir.dt.from_np(a.dtype), kind="ExternalInput").ap() for k, a in arrays.items()}
    A["out"] = nc.dram_tensor("out_x", (NPAD, F), f32, kind="ExternalOutput").ap()
    if launch is not None:
        return launch(nc, A, arrays)
    build(nc, A)
    r = run_bass_kernel_spmd(nc, [{f"in_{k}": a for k, a in arrays.items()}], core_ids=[0])
    return r.results[0]["out_x"][:N]
```

```python
import concourse.bass as bass
from concourse import mybir
from contextlib import ExitStack

f32 = mybir.dt.float32
i32 = mybir.dt.int32
ALU = mybir.AluOpType
ACT = mybir.ActivationFunctionType
AX = mybir.AxisListType

P = 128
F = 32
N, E = 100000, 50000
C = 28
Q = C // 4
EC = 14
ET = EC * C
EPAD = P * ET
NC = 28
NT = NC * C
NPAD = P * NT
NTRASH = NPAD + P
PAIRS = EC // 2
CARRY = F + 1
OUTSIDE = 1 << 20
HID1, HID2 = 64, 128
CON = 16
CW = CON + 1
NREL, NB = 86, 16
RT = 3 * F + NB
EPS = 1e-5
NEG = -1.0e38


def bc_feat(ap, n=F):
    return ap.unsqueeze(2).to_broadcast([ap.shape[0], ap.shape[1], n])


def bc_tile(ap, n):
    return ap.unsqueeze(1).to_broadcast([ap.shape[0], n, ap.shape[1]])


def dve_norm(nc, dve, w, x, out, T, n, done=None, lo=0, hi=F):
    nc.vector.tensor_reduce(w.stat[:, 0, 0:T], x, AX.X, ALU.add)
    dve.drain()
    nc.vector.scalar_tensor_tensor(out=w.xc[:, 0:T, :], in0=bc_feat(w.stat[:, 0, 0:T]), scalar=-1.0 / F,
                                   in1=x, op0=ALU.mult, op1=ALU.add).then_inc(w.centered, 1)
    dve.wait_ge(w.squared, n + (w.base + 1))
    nc.vector.tensor_reduce(w.stat[:, 1, 0:T], w.sq[:, 0:T, :], AX.X, ALU.add).then_inc(w.summed, 1)
    dve.wait_ge(w.rooted, n + (w.base + 1))
    nc.vector.reciprocal(w.stat[:, 3, 0:T], w.stat[:, 2, 0:T])
    dve.drain()
    last = nc.vector.scalar_tensor_tensor(out=out, in0=w.xc[:, 0:T, lo:hi], scalar=0.0,
                                          in1=bc_feat(w.stat[:, 3, 0:T], hi - lo), op0=ALU.max, op1=ALU.mult)
    if done is not None:
        last.then_inc(done, 1)
    else:
        dve.drain()


def act_norm(nc, act, w, T, n):
    act.wait_ge(w.centered, n + (w.base + 1))
    nc.scalar.activation(w.sq[:, 0:T, :], w.xc[:, 0:T, :], ACT.Square).then_inc(w.squared, 1)
    act.wait_ge(w.summed, n + (w.base + 1))
    nc.scalar.activation(w.stat[:, 2, 0:T], w.stat[:, 1, 0:T], ACT.Sqrt, bias=w.eps[:, 0:1],
                         scale=1.0 / F).then_inc(w.rooted, 1)


def pool_wait(g, pool, *waits):
    for sem, value in waits:
        pool.wait_ge(sem, value)
    pool.sem_inc(g.pool_steps, 1)


class Norm:

    def __init__(self, nc, ctx, g, stage, T, norms):
        self.xc = ctx.enter_context(nc.sbuf_tensor(f"{stage}_xc", [P, T, F], f32))
        self.sq = ctx.enter_context(nc.sbuf_tensor(f"{stage}_sq", [P, T, F], f32))
        self.stat = ctx.enter_context(nc.sbuf_tensor(f"{stage}_stat", [P, 4, T], f32))
        self.eps = g.eps
        self.centered, self.squared, self.summed, self.rooted = g.norm_sems
        self.base = g.norms
        g.norms += norms


class Globals:
    pass


def pe_quads(nc, pt, src, ident, nquads, done):
    for q in range(nquads):
        last = nc.tensor.transpose(pt[:, q * P:(q + 1) * P], src[:, 4 * q:4 * q + 4, :].rearrange("p t f -> p (t f)"),
                                   ident)
    last.then_inc(done, 1)


def stage_setup(nc, g):
    with ExitStack() as ctx:
        sb = lambda name, shape, dt=f32: ctx.enter_context(nc.sbuf_tensor(name, shape, dt))
        dwin = sb("dst_windows", [P, 3, ET], i32)
        dwf = sb("dst_windows_f", [P, 3, ET])
        endf = sb("end_index_f", [P, ET])
        endi = sb("end_index", [P, ET], i32)
        att4 = sb("att_cols", [F, 3])
        wT = sb("W_T", [F, F])
        pw = ctx.enter_context(nc.psum_tensor("p_watt", [P, 512], f32))
        pa = ctx.enter_context(nc.psum_tensor("p_all", [P, 512], f32))
        loaded, flags, end_stored = (g.sem(n) for n in ("su_loaded", "su_flags", "su_end_stored"))
        padded, ident_set, watt_done = (g.sem(n) for n in ("su_padded", "su_ident", "su_watt"))
        att_loaded, att_sum, all_done, dst_loaded = (g.sem(n) for n in ("su_att", "su_att_sum", "su_all", "su_dst"))
        block = ctx.enter_context(nc.Block())

        @block.sync
        def _(sp):
            for k in range(3):
                sp.dma_start(dwin[:, k, :], g.dst_flat[k:k + EPAD].rearrange("(p t) -> p t", t=ET)).then_inc(dst_loaded, 16)
            sp.dma_start(att4[:, 0:1], g.att_src.unsqueeze(1)).then_inc(att_loaded, 16)
            sp.dma_start(att4[:, 1:2], g.att_dst.unsqueeze(1)).then_inc(att_loaded, 16)
            sp.dma_start(wT[:], g.WT).then_inc(att_loaded, 16)
            sp.wait_ge(padded, 1)
            n = 0

            def load(dst, src):
                nonlocal n
                n += 1
                sp.dma_start(dst, src).then_inc(loaded, 16)

            for j in range(4):
                load(g.w0[F * j:F * (j + 1), F * j:F * (j + 1)], g.W)
                r, jj = j // 2, j % 2
                load(g.w1l[F * j:F * (j + 1), r, HID1 * jj:HID1 * (jj + 1)], g.W1_lT)
                load(g.w1r[F * j:F * (j + 1), r, HID1 * jj:HID1 * (jj + 1)], g.W1_rT)
            for jj in range(2):
                k = HID1 * jj
                load(g.w1gr[k:k + HID1, k:k + F], g.W2_lT)
                load(g.w1gr[k:k + HID1, k + F:k + 2 * F], g.W2_rT)
                load(g.b1col[k:k + HID1, 0:1], g.L1_b1.unsqueeze(1))
            load(g.bias0[:], g.bias.partition_broadcast(P))
            load(g.b1out[:], g.L1_b2.partition_broadcast(P))
            sp.wait_ge(flags, 1)
            sp.dma_start(g.end_index, endi[:]).then_inc(end_stored, 16)
            sp.wait_ge(end_stored, 16)
            sp.wait_ge(loaded, 16 * n)

        @block.gpsimd
        def _(pool):
            nc.gpsimd.memset(g.ident[:], 0.0)
            nc.gpsimd.memset(g.before[:], 1.0)
            pool.drain()
            nc.gpsimd.affine_select(out=g.ident[:], in_=g.ident[:], compare_op=ALU.not_equal, fill=1.0, base=0,
                                    pattern=[[-1, P]], channel_multiplier=1)
            nc.gpsimd.affine_select(out=g.before[:], in_=g.before[:], compare_op=ALU.is_gt, fill=0.0, base=0,
                                    pattern=[[-1, P]], channel_multiplier=1)
            nc.gpsimd.iota(g.relid_i[:], pattern=[[0, 1]], base=0, channel_multiplier=1)
            pool.drain()
            nc.gpsimd.tensor_copy(g.relid[:], g.relid_i[:])
            pool.drain().then_inc(ident_set, 1)

        @block.vector
        def _(dve):
            dve.sem_inc(g.scatter_sems[3], 2)
            for t in (g.w0, g.w1l, g.w1r, g.w1gr):
                nc.vector.memset(t[:], 0.0)
            nc.vector.memset(g.eps[:], EPS)
            dve.drain().then_inc(padded, 1)
            dve.wait_ge(att_loaded, 48)
            nc.vector.tensor_tensor(att4[:, 2:3], att4[:, 0:1], att4[:, 1:2], ALU.add).then_inc(att_sum, 1)
            dve.wait_ge(dst_loaded, 48)
            nc.vector.tensor_copy(dwf[:], dwin[:])
            dve.drain()
            nc.vector.tensor_tensor(g.same[:], dwf[:, 1, :], dwf[:, 0, :], ALU.is_equal)
            nc.vector.tensor_tensor(g.more[:], dwf[:, 1, :], dwf[:, 2, :], ALU.is_equal)
            dve.drain()
            nc.vector.tensor_scalar(g.end[:], g.more[:], -1.0, 1.0, ALU.mult, ALU.add)
            nc.vector.tensor_tensor_scan(g.pre[:], g.same[:], g.same[:], 1.0, ALU.mult, ALU.mult)
            nc.vector.tensor_tensor_scan(g.suf[:, ::-1], g.more[:, ::-1], g.more[:, ::-1], 1.0, ALU.mult, ALU.mult)
            nc.vector.tensor_scalar(endf[:], g.more[:], float(OUTSIDE), None, ALU.mult)
            dve.drain()
            nc.vector.tensor_tensor(endf[:], endf[:], dwf[:, 1, :], ALU.add)
            nc.vector.memset(g.deg[:], 1.0)
            dve.drain()
            nc.vector.tensor_copy(endi[:], endf[:]).then_inc(flags, 1)
            nc.vector.tensor_tensor_scan(g.deg[:], g.same[:], g.deg[:], 0.0, ALU.mult, ALU.add)
            dve.drain().then_inc(flags, 1)
            dve.wait_ge(watt_done, 1)
            nc.vector.tensor_copy(g.watt[:], pw[:, 0:3 * F].rearrange("p (k f) -> p k f", f=F))
            dve.wait_ge(all_done, 1)
            nc.vector.tensor_copy(g.preall[:], pa[0:CARRY, 0:P])
            nc.vector.tensor_copy(g.sufall[:], pa[0:CARRY, P:2 * P])
            dve.drain().then_inc(flags, 1)

        @block.tensor
        def _(pe):
            pe.wait_ge(att_sum, 1)
            for k in range(3):
                last = nc.tensor.matmul(pw[:, k * F:(k + 1) * F], att4[:, k:k + 1].to_broadcast([F, P]), wT[:], start=True, stop=True)
            last.then_inc(watt_done, 1)
            pe.wait_ge(flags, 2)
            pe.wait_ge(ident_set, 1)
            nc.tensor.matmul(pa[0:CARRY, 0:P], g.pre[:, ET - 1:ET].to_broadcast([P, CARRY]), g.ident[:], start=True, stop=True)
            nc.tensor.matmul(pa[0:CARRY, P:2 * P], g.suf[:, 0:1].to_broadcast([P, CARRY]), g.ident[:], start=True,
                             stop=True).then_inc(all_done, 1)

    stage_carry(nc, g, "deg", [g.deg[:, ET - 1:ET]])
    with ExitStack() as ctx:
        block = ctx.enter_context(nc.Block())

        @block.vector
        def _(dve):
            nc.vector.scalar_tensor_tensor(out=g.deg[:], in0=g.pre[:], scalar=g.carry[:, 0:1], in1=g.deg[:],
                                           op0=ALU.mult, op1=ALU.add)
            dve.drain()
            nc.vector.reciprocal(g.rdeg[:], g.deg[:])


def stage_carry(nc, g, stage, parts, reverse=False, greatest=False):
    n = sum(p.shape[1] for p in parts)
    with ExitStack() as ctx:
        own = ctx.enter_context(nc.sbuf_tensor(f"{stage}_own", [P, n], f32))
        row = ctx.enter_context(nc.sbuf_tensor(f"{stage}_row", [n, P + 1], f32))
        cut = ctx.enter_context(nc.sbuf_tensor(f"{stage}_cut", [n, P], f32))
        pr = ctx.enter_context(nc.psum_tensor(f"{stage}_prow", [n, P], f32))
        pc = ctx.enter_context(nc.psum_tensor(f"{stage}_pcol", [P, n], f32))
        copied, turned, scanned, back = g.carry_sems
        g.carries += 1
        now = g.carries
        block = ctx.enter_context(nc.Block())

        @block.vector
        def _(dve):
            k = 0
            for part in parts:
                nc.vector.tensor_copy(own[:, k:k + part.shape[1]], part)
                k += part.shape[1]
            nc.vector.memset(row[:, P:P + 1] if reverse else row[:, 0:1], NEG if greatest else 0.0)
            if greatest:
                nc.vector.tensor_scalar(cut[:], g.preall[0:n, :], -NEG, NEG, ALU.mult, ALU.add)
            dve.drain().then_inc(copied, 1)
            dve.wait_ge(turned, now)
            if reverse:
                nc.vector.tensor_tensor_scan(row[:, 0:P][:, ::-1], g.sufall[0:n, ::-1], pr[:, ::-1], 0.0, ALU.mult, ALU.add)
            elif greatest:
                nc.vector.tensor_tensor_scan(row[:, 1:P + 1], cut[:], pr[:], NEG, ALU.add, ALU.max)
            else:
                nc.vector.tensor_tensor_scan(row[:, 1:P + 1], g.preall[0:n, :], pr[:], 0.0, ALU.mult, ALU.add)
            dve.drain().then_inc(scanned, 1)
            dve.wait_ge(back, now)
            nc.vector.tensor_copy((g.carry_back if reverse else g.carry)[:, 0:n], pc[:])

        @block.tensor
        def _(pe):
            pe.wait_ge(copied, now)
            nc.tensor.transpose(pr[:], own[:], g.ident[:]).then_inc(turned, 1)
            pe.wait_ge(scanned, now)
            nc.tensor.transpose(pc[:], row[:, 1:P + 1] if reverse else row[:, 0:P], g.ident[0:n, 0:n]).then_inc(back, 1)


def stage_first_gather(nc, g):
    st = "s1"
    with ExitStack() as ctx:
        sb = lambda name, shape, dt=f32: ctx.enter_context(nc.sbuf_tensor(f"{st}_{name}", shape, dt))
        pb = lambda name: ctx.enter_context(nc.psum_tensor(f"{st}_{name}", [P, 1024], f32))
        S = lambda name: g.sem(f"{st}_{name}")
        w = Norm(nc, ctx, g, st, C, 12 * PAIRS)
        ring = sb("ring", [P, 2, 2, C, F])
        idx = sb("idx", [P, 2, 2, C], i32)
        hedge = sb("h_edge", [P, 2 * C, F])
        dots = sb("dots", [P, 5, C])
        x0 = sb("x0", [P, 2, C, F])
        x1 = sb("x1", [P, 2, C, F])
        x2 = sb("x2", [P, 2, C, F])
        gt = sb("g", [P, 2, C, F])
        hd = sb("h_node", [P, 2, C, F])
        tsb = sb("h_T", [P, Q * P])
        hid = sb("hid_T", [P, 2, Q * P])
        pT, pW, pH, pG = pb("pT"), pb("pW"), pb("pH"), pb("pG")
        idx_here = [S("idx_here0"), S("idx_here1")]
        rows = [S("rows0"), S("rows1")]
        x0_here = [S("x0_here0"), S("x0_here1")]
        ring_free, h_edge_ready = S("ring_free"), S("h_edge_ready")
        h0_ready, h1_ready, turned, turned_sb = S("h0_ready"), S("h1_ready"), S("turned"), S("turned_sb")
        w_done, hid_done, hid_sb, gr_done = S("w_done"), S("hid_done"), S("hid_sb"), S("gr_done")
        x1_ready, x2_ready, stored, dense_free = S("x1_ready"), S("x2_ready"), S("stored"), S("dense_free")
        block = ctx.enter_context(nc.Block())
        GAT = 16 * 2 * C

        def cols(t, k, n=C * F):
            return t.rearrange("(p t) f -> p (t f)", p=P)[:, bass.ds(k * (C * F), n)]

        @block.sync
        def _(sp):
            def load_idx(c, a):
                sp.dma_start(idx[:, a, 0, :], g.src[:, bass.ds(c * C, C)]).then_inc(idx_here[a], 16)
                sp.dma_start(idx[:, a, 1, :], g.dst[:, bass.ds(c * C, C)]).then_inc(idx_here[a], 16)

            def load_x(k, b):
                sp.dma_start(x0[:, b].rearrange("p t f -> p (t f)"), cols(g.x, k)).then_inc(x0_here[b], 16)

            sp.sem_inc(dense_free, 2)
            for a in range(2):
                load_idx(a, a)
                load_x(a, a)

            def turn(i, more):
                for a in range(2):
                    for m in range(2):
                        k, b = i * 4 + (2 * a + m), m
                        sp.wait_ge(x1_ready, k + 1)
                        sp.dma_start(cols(g.X1, k), x1[:, b].rearrange("p t f -> p (t f)")).then_inc(stored, 16)
                        if more or a == 0:
                            load_x(k + 2, b)
                        sp.wait_ge(x2_ready, k + 1)
                        sp.dma_start(cols(g.X2, k), x2[:, b].rearrange("p t f -> p (t f)")).then_inc(stored, 16)
                        sp.dma_start(cols(g.G, k), gt[:, b].rearrange("p t f -> p (t f)")).then_inc(stored, 16)
                        sp.wait_ge(stored, (k + 1) * 48)
                        sp.sem_inc(dense_free, 1)
                    if more:
                        sp.wait_ge(rows[a], i * GAT + GAT)
                        load_idx(i * 2 + (a + 2), a)

            with sp.Fori(0, PAIRS - 1) as i:
                turn(i, True)
            turn(PAIRS - 1, False)

        @block.gpsimd
        def _(pool):
            with pool.Fori(0, PAIRS) as i:
                for a in range(2):
                    pool_wait(g, pool, (idx_here[a], i * 32 + 32), (ring_free, i * 2 + (a + 1)))
                    for t in range(C):
                        for k in range(2):
                            pool.indirect_dma_start(
                                out=ring[:, a, k, t, :], out_offset=None, in_=g.x,
                                in_offset=bass.IndirectOffsetOnAxis(ap=idx[:, a, k, t:t + 1], axis=0),
                            ).then_inc(rows[a], 16)

        @block.vector
        def _(dve):
            def node_a(b, turn, n):
                dve.wait_ge(x0_here[b], turn * 16 + 16)
                dve_norm(nc, dve, w, x0[:, b], hd[:, 0], C, n, h0_ready)
                nc.vector.tensor_tensor(x0[:, b], x0[:, b], bc_tile(g.bias0[:], C), ALU.add)
                dve.drain()

            def turn(i, more):
                for a in range(2):
                    n0 = i * 12 + (6 * a + 1)
                    def node_b(m):
                        b, k = m, i * 4 + (2 * a + m)
                        dve.wait_ge(dense_free, k + 1)
                        dve.wait_ge(w_done, k + 1)
                        nc.vector.tensor_tensor(x1[:, b], x0[:, b], pW[:, 0:C * F].rearrange("p (t f) -> p t f", f=F), ALU.add)
                        dve.drain().then_inc(x1_ready, 1)
                        dve_norm(nc, dve, w, x1[:, b], hd[:, 1], C, n0 + 3 * m, h1_ready)
                        nc.vector.tensor_tensor(x2[:, b], x1[:, b], bc_tile(g.b1out[:], C), ALU.add)

                    def node_c(m):
                        b, k = m, i * 4 + (2 * a + m)
                        for half in range(2):
                            dve.wait_ge(gr_done, k * 2 + (half + 1))
                            pv = (pG, pH)[half][:, 0:C // 2 * 2 * F].rearrange("p (t c) -> p t c", c=2 * F)
                            ts = slice(half * (C // 2), (half + 1) * (C // 2))
                            nc.vector.tensor_tensor(x2[:, b, ts, :], x2[:, b, ts, :], pv[:, :, F:2 * F], ALU.add)
                            nc.vector.tensor_copy(gt[:, b, ts, :], pv[:, :, 0:F])
                        dve.drain().then_inc(x2_ready, 1)

                    def edge_norm(half):
                        c = i * 2 + a
                        if half == 0:
                            dve.wait_ge(rows[a], i * GAT + GAT)
                            dve.wait_ge(ring_free, c + 2)
                        dve_norm(nc, dve, w, ring[:, a, half], hedge[:, half * C:(half + 1) * C, :], C, n0 + (2, 5 if more or a == 0 else 4)[half])

                    def edge_dots():
                        c = i * 2 + a
                        for k, (half, v) in enumerate(((0, 0), (1, 1), (1, 2))):
                            nc.vector.tensor_tensor(w.xc[:], hedge[:, half * C:(half + 1) * C, :],
                                                    bc_tile(g.watt[:, v, :], C), ALU.mult)
                            dve.drain()
                            nc.vector.tensor_reduce(dots[:, k, :], w.xc[:], AX.X, ALU.add)
                            dve.drain()
                        nc.vector.tensor_tensor(dots[:, 3, :], dots[:, 0, :], dots[:, 1, :], ALU.add)
                        dve.drain()
                        nc.vector.scalar_tensor_tensor(out=g.e_edge[:, bass.ds(c * C, C)], in0=dots[:, 3, :], scalar=0.2,
                                                       in1=dots[:, 3, :], op0=ALU.mult, op1=ALU.max)
                        nc.vector.scalar_tensor_tensor(out=g.e_self[:, bass.ds(c * C, C)], in0=dots[:, 2, :], scalar=0.2,
                                                       in1=dots[:, 2, :], op0=ALU.mult, op1=ALU.max)
                        dve.drain().then_inc(h_edge_ready, 1)

                    node_b(0)
                    node_a(1, i * 2 + a, n0 + 1)
                    edge_norm(0)
                    node_c(0)
                    node_b(1)
                    if more or a == 0:
                        node_a(0, i * 2 + (a + 1), n0 + 4)
                    edge_norm(1)
                    edge_dots()
                    node_c(1)

            node_a(0, 0, 0)
            with dve.Fori(0, PAIRS - 1) as i:
                turn(i, True)
            turn(PAIRS - 1, False)

        @block.scalar
        def _(act):
            act.sem_inc(ring_free, 2)

            def bring(n):
                act.wait_ge(turned, n + 1)
                nc.scalar.copy(tsb[:], pT[:, 0:Q * P]).then_inc(turned_sb, 1)

            def turn(i, more):
                for a in range(2):
                    n0 = i * 12 + (6 * a + 1)

                    def hidden(m):
                        k = i * 4 + (2 * a + m)
                        for half in range(2):
                            act.wait_ge(hid_done, k * 2 + (half + 1))
                            nc.scalar.activation(hid[:, half, :], pH[:, 0:Q * P], ACT.Relu,
                                                 bias=g.b1col[:, 0:1]).then_inc(hid_sb, 1)

                    act_norm(nc, act, w, C, n0)
                    bring(i * 8 + (4 * a + 1))
                    act_norm(nc, act, w, C, n0 + 1)
                    hidden(0)
                    act_norm(nc, act, w, C, n0 + 2)
                    bring(i * 8 + (4 * a + 2))
                    act_norm(nc, act, w, C, n0 + 3)
                    bring(i * 8 + (4 * a + 3))
                    if more or a == 0:
                        act_norm(nc, act, w, C, n0 + 4)
                    hidden(1)
                    act_norm(nc, act, w, C, n0 + (5 if more or a == 0 else 4))
                    if more or a == 0:
                        bring(i * 8 + (4 * a + 4))
                    act.wait_ge(h_edge_ready, i * 2 + (a + 1))
                    nc.scalar.copy(g.agg[:, bass.ds(i * (2 * C) + a * C, C), :], hedge[:, 0:C, :])
                    nc.scalar.copy(g.xd[:, bass.ds(i * (2 * C) + a * C, C), :], ring[:, a, 1])
                    act.drain().then_inc(ring_free, 1)

            act_norm(nc, act, w, C, 0)
            bring(0)
            with act.Fori(0, PAIRS - 1) as i:
                turn(i, True)
            turn(PAIRS - 1, False)

        @block.tensor
        def _(pe):
            def project(k):
                pe.wait_ge(h0_ready, k + 1)
                pe_quads(nc, pT, hd[:, 0], g.ident[:], Q, turned)
                pe.wait_ge(turned_sb, k * 2 + 1)
                for q in range(Q):
                    last = nc.tensor.matmul(pW[:, q * P:(q + 1) * P], tsb[:, q * P:(q + 1) * P], g.w0[:], start=True, stop=True)
                last.then_inc(w_done, 1)

            def second_layer(k):
                pe.wait_ge(h1_ready, k + 1)
                pe_quads(nc, pT, hd[:, 1], g.ident[:], Q, turned)
                pe.wait_ge(turned_sb, k * 2 + 2)
                for half in range(2):
                    if half:
                        pe.wait_ge(hid_sb, k * 2 + 1)
                    for s in range(Q):
                        r = half * Q + s
                        last = nc.tensor.matmul(pH[:, s * P:(s + 1) * P], g.w1r[:, r % 2, :],
                                                tsb[:, (r // 2) * P:(r // 2 + 1) * P], start=True, stop=True)
                    last.then_inc(hid_done, 1)
                for half in range(2):
                    pe.wait_ge(hid_sb, k * 2 + (half + 1))
                    for s in range(Q):
                        last = nc.tensor.matmul((pG, pH)[half][:, s * P:(s + 1) * P], hid[:, half, s * P:(s + 1) * P], g.w1gr[:],
                                                start=True, stop=True)
                    last.then_inc(gr_done, 1)

            project(0)
            with pe.Fori(0, NC - 1) as k:
                second_layer(k)
                project(k + 1)
            second_layer(NC - 1)


def stage_softmax(nc, g):
    with ExitStack() as ctx:
        sb = lambda name: ctx.enter_context(nc.sbuf_tensor(f"sm_{name}", [P, ET], f32))
        top, most, negcut, precut = sb("top"), sb("most"), sb("negcut"), sb("precut")
        with ExitStack() as inner:
            block = inner.enter_context(nc.Block())

            @block.vector
            def _(dve):
                nc.vector.tensor_scalar(negcut[:], g.same[:], -NEG, NEG, ALU.mult, ALU.add)
                nc.vector.tensor_scalar(precut[:], g.pre[:], -NEG, NEG, ALU.mult, ALU.add)
                nc.vector.tensor_tensor(top[:], g.e_edge[:], g.e_self[:], ALU.max)
                dve.drain()
                nc.vector.tensor_tensor_scan(most[:], negcut[:], top[:], NEG, ALU.add, ALU.max)

        stage_carry(nc, g, "sm_max", [most[:, ET - 1:ET]], greatest=True)
        with ExitStack() as inner:
            block = inner.enter_context(nc.Block())

            @block.vector
            def _(dve):
                nc.vector.scalar_tensor_tensor(out=most[:], in0=precut[:], scalar=g.carry[:, 0:1], in1=most[:],
                                               op0=ALU.add, op1=ALU.max)
                dve.drain()
                nc.vector.tensor_tensor(most[:], most[:], g.end[:], ALU.mult)
                dve.drain()
                nc.vector.tensor_tensor_scan(top[:, ::-1], g.more[:, ::-1], most[:, ::-1], 0.0, ALU.mult, ALU.add)

        stage_carry(nc, g, "sm_back", [top[:, 0:1]], reverse=True)
        less, raised = g.sem("sm_less"), g.sem("sm_raised")
        with ExitStack() as inner:
            block = inner.enter_context(nc.Block())

            @block.vector
            def _(dve):
                nc.vector.scalar_tensor_tensor(out=top[:], in0=g.suf[:], scalar=g.carry_back[:, 0:1], in1=top[:],
                                               op0=ALU.mult, op1=ALU.add)
                dve.drain()
                nc.vector.tensor_tensor(g.e_edge[:], g.e_edge[:], top[:], ALU.subtract)
                nc.vector.tensor_tensor(g.e_self[:], g.e_self[:], top[:], ALU.subtract).then_inc(less, 1)
                dve.wait_ge(raised, 2)
                nc.vector.tensor_tensor_scan(g.rden[:], g.same[:], g.e_edge[:], 0.0, ALU.mult, ALU.add)
                nc.vector.tensor_tensor(g.agg[:], g.agg[:], bc_feat(g.e_edge[:]), ALU.mult)
                dve.drain()
                for f in range(F):
                    nc.vector.tensor_tensor_scan(g.agg[:, :, f], g.same[:], g.agg[:, :, f], 0.0, ALU.mult, ALU.add)

            @block.scalar
            def _(act):
                act.wait_ge(less, 1)
                nc.scalar.activation(g.e_edge[:], g.e_edge[:], ACT.Exp).then_inc(raised, 1)
                nc.scalar.activation(g.e_self[:], g.e_self[:], ACT.Exp).then_inc(raised, 1)

        stage_carry(nc, g, "sm_sum", [g.agg[:, ET - 1, :], g.rden[:, ET - 1:ET]])
        with ExitStack() as inner:
            block = inner.enter_context(nc.Block())

            @block.vector
            def _(dve):
                nc.vector.scalar_tensor_tensor(out=g.rden[:], in0=g.pre[:], scalar=g.carry[:, F:F + 1], in1=g.rden[:],
                                               op0=ALU.mult, op1=ALU.add)
                dve.drain()
                nc.vector.tensor_tensor(g.rden[:], g.rden[:], g.e_self[:], ALU.add)
                dve.drain()
                nc.vector.reciprocal(g.rden[:], g.rden[:])
                dve.drain()
                nc.vector.tensor_tensor(g.e_self[:], g.e_self[:], g.rden[:], ALU.mult)


class Scatter:

    def __init__(self, nc, ctx, g, stage, width=F):
        self.rows = ctx.enter_context(nc.sbuf_tensor(f"{stage}_out_rows", [P, 2, C, width], f32))
        self.idx = ctx.enter_context(nc.sbuf_tensor(f"{stage}_out_idx", [P, 2, C], i32))
        self.idx_here, self.done, self.ready, self.free = g.scatter_sems
        self.n = g.scatters
        g.scatters += 1

    def wait_idx(self, eng, i, a):
        eng.wait_ge(self.idx_here[a], i * 16 + 16 * (PAIRS * self.n + 1))

    def wait_done(self, eng, i, a):
        eng.wait_ge(self.done[a], i * ONCE + ONCE * (PAIRS * self.n + 1))

    def wait_ready(self, eng, c):
        eng.wait_ge(self.ready, c + (EC * self.n + 1))

    def wait_free(self, eng, c):
        eng.wait_ge(self.free, c + (EC * self.n + 1))


ONCE = 16 * C


def sp_scatter(g, sp, s):

    def load(c, a):
        sp.dma_start(s.idx[:, a, :], g.end_index[:, bass.ds(c * C, C)]).then_inc(s.idx_here[a], 16)

    load(0, 0)
    load(1, 1)
    with sp.Fori(0, PAIRS - 1) as i:
        for a in range(2):
            s.wait_done(sp, i, a)
            sp.sem_inc(s.free, 1)
            load(i * 2 + (a + 2), a)
    for a in range(2):
        s.wait_done(sp, PAIRS - 1, a)
        sp.sem_inc(s.free, 1)


def pool_scatter(nc, g, pool, s, table):
    with pool.Fori(0, PAIRS) as i:
        for a in range(2):
            s.wait_idx(pool, i, a)
            s.wait_ready(pool, i * 2 + a)
            pool_wait(g, pool)
            for t in range(C):
                pool.indirect_dma_start(
                    out=table, out_offset=bass.IndirectOffsetOnAxis(ap=s.idx[:, a, t:t + 1], axis=0),
                    in_=s.rows[:, a, t, :], in_offset=None, bounds_check=NPAD - 1, oob_is_err=False,
                ).then_inc(s.done[a], 16)


def dve_true_sum(nc, dve, g, tmp, c, lo=0, hi=F):
    part = bass.ds(c * C, C)
    nc.vector.tensor_tensor(tmp, bc_tile(g.carry[:, lo:hi], C), bc_feat(g.pre[:, part], hi - lo), ALU.mult)
    dve.drain()
    nc.vector.tensor_tensor(tmp, tmp, g.agg[:, part, lo:hi], ALU.add)
    dve.drain()


def stage_scatter_x1(nc, g):
    st = "s2"
    with ExitStack() as ctx:
        w = Norm(nc, ctx, g, st, C, EC)
        s = Scatter(nc, ctx, g, st)
        z = ctx.enter_context(nc.sbuf_tensor("s2_z", [P, C, F], f32))
        hd = ctx.enter_context(nc.sbuf_tensor("s2_h_dst", [P, C, F], f32))
        tsb = ctx.enter_context(nc.sbuf_tensor("s2_z_T", [P, Q * P], f32))
        pT = ctx.enter_context(nc.psum_tensor("s2_pT", [P, 1024], f32))
        pW = ctx.enter_context(nc.psum_tensor("s2_pW", [P, 1024], f32))
        z_ready, turned, turned_sb, w_done = (g.sem(f"{st}_{x}") for x in ("z_ready", "turned", "turned_sb", "w_done"))
        block = ctx.enter_context(nc.Block())

        @block.sync
        def _(sp):
            sp_scatter(g, sp, s)

        @block.gpsimd
        def _(pool):
            pool_scatter(nc, g, pool, s, g.X1)

        @block.vector
        def _(dve):
            with dve.Fori(0, PAIRS) as i:
                for a in range(2):
                    c = i * 2 + a
                    part = bass.ds(c * C, C)
                    dve_norm(nc, dve, w, g.xd[:, part, :], hd[:], C, c)
                    nc.vector.tensor_tensor(hd[:], hd[:], bc_feat(g.e_self[:, part]), ALU.mult)
                    dve_true_sum(nc, dve, g, z[:], c)
                    nc.vector.tensor_tensor(z[:], z[:], bc_feat(g.rden[:, part]), ALU.mult)
                    dve.drain()
                    nc.vector.tensor_tensor(z[:], z[:], hd[:], ALU.add).then_inc(z_ready, 1)
                    s.wait_free(dve, c)
                    nc.vector.tensor_tensor(s.rows[:, a], g.xd[:, part, :], bc_tile(g.bias0[:], C), ALU.add)
                    dve.drain()
                    dve.wait_ge(w_done, c + 1)
                    nc.vector.tensor_tensor(s.rows[:, a], s.rows[:, a],
                                            pW[:, 0:C * F].rearrange("p (t f) -> p t f", f=F), ALU.add).then_inc(s.ready, 1)

        @block.scalar
        def _(act):
            with act.Fori(0, PAIRS) as i:
                for a in range(2):
                    c = i * 2 + a
                    act_norm(nc, act, w, C, c)
                    act.wait_ge(turned, c + 1)
                    nc.scalar.copy(tsb[:], pT[:, 0:Q * P]).then_inc(turned_sb, 1)
                    s.wait_ready(act, c)
                    nc.scalar.copy(g.xd[:, bass.ds(c * C, C), :], s.rows[:, a])

        @block.tensor
        def _(pe):
            with pe.Fori(0, PAIRS) as i:
                for a in range(2):
                    c = i * 2 + a
                    pe.wait_ge(z_ready, c + 1)
                    pe_quads(nc, pT, z, g.ident[:], Q, turned)
                    pe.wait_ge(turned_sb, c + 1)
                    for q in range(Q):
                        o = pW[:, q * P:(q + 1) * P]
                        last = nc.tensor.matmul(o, tsb[:, q * P:(q + 1) * P], g.w0[:], start=True, stop=True)
                    last.then_inc(w_done, 1)


def stage_gather(nc, g, st, table, norm, lo=0, hi=F, beside=None):
    K = hi - lo
    with ExitStack() as ctx:
        w = Norm(nc, ctx, g, st, C, EC) if norm else None
        sb = lambda name, shape, dt=f32: ctx.enter_context(nc.sbuf_tensor(f"{st}_{name}", shape, dt))
        ring = sb("ring", [P, 2, C, F])
        idx = sb("idx", [P, 2, C], i32)
        h = sb("h_src", [P, C, K]) if norm else None
        run = sb("running", [P, 2, C, K])
        idx_here = [g.sem(f"{st}_idx_here{a}") for a in range(2)]
        rows = [g.sem(f"{st}_rows{a}") for a in range(2)]
        ring_free, run_ready, run_free = (g.sem(f"{st}_{x}") for x in ("ring_free", "run_ready", "run_free"))
        block = ctx.enter_context(nc.Block())

        @block.sync
        def _(sp):
            def load(c, a):
                sp.dma_start(idx[:, a, :], g.src[:, bass.ds(c * C, C)]).then_inc(idx_here[a], 16)

            load(0, 0)
            load(1, 1)
            if beside is not None:
                beside.sp(sp)
            with sp.Fori(0, PAIRS - 1) as i:
                for a in range(2):
                    sp.wait_ge(rows[a], i * ONCE + ONCE)
                    load(i * 2 + (a + 2), a)
            if beside is not None:
                beside.sp_end(sp)

        @block.gpsimd
        def _(pool):
            with pool.Fori(0, PAIRS) as i:
                for a in range(2):
                    pool_wait(g, pool, (idx_here[a], i * 16 + 16), (ring_free, i * 2 + (a + 1)))
                    for t in range(C):
                        pool.indirect_dma_start(
                            out=ring[:, a, t, :], out_offset=None, in_=table,
                            in_offset=bass.IndirectOffsetOnAxis(ap=idx[:, a, t:t + 1], axis=0),
                        ).then_inc(rows[a], 16)

        @block.vector
        def _(dve):
            dve.sem_inc(ring_free, 2)
            nc.vector.memset(run[:, 1, C - 1, :], 0.0)
            dve.drain()
            if beside is not None:
                beside.dve(dve)
            with dve.Fori(0, PAIRS) as i:
                for a in range(2):
                    c = i * 2 + a
                    part = bass.ds(c * C, C)
                    dve.wait_ge(rows[a], i * ONCE + ONCE)
                    if norm:
                        dve_norm(nc, dve, w, ring[:, a], h[:], C, c, lo=lo, hi=hi)
                        dve.drain().then_inc(ring_free, 1)
                    dve.wait_ge(run_free, c + 1)
                    for f in range(K):
                        v = h[:, :, f] if norm else ring[:, a, :, lo + f]
                        nc.vector.tensor_tensor_scan(run[:, a, :, f], g.same[:, part], v, run[:, 1 - a, C - 1, f:f + 1],
                                                     ALU.mult, ALU.add)
                    dve.drain().then_inc(run_ready, 1)
                    if not norm:
                        dve.drain().then_inc(ring_free, 1)

        @block.scalar
        def _(act):
            act.sem_inc(run_free, 2)
            with act.Fori(0, PAIRS) as i:
                for a in range(2):
                    c = i * 2 + a
                    if norm:
                        act_norm(nc, act, w, C, c)
                    act.wait_ge(run_ready, c + 1)
                    nc.scalar.copy(g.agg[:, bass.ds(c * C, C), 0:K], run[:, a]).then_inc(run_free, 1)


class ClearTables:

    ROW = NTRASH * CW // P
    STEP = 2048

    def __init__(self, nc, ctx, g):
        assert self.ROW * P == NTRASH * CW
        self.nc, self.tables = nc, (g.sum_dst, g.sum_a, g.sum_b)
        self.zero = ctx.enter_context(nc.sbuf_tensor("zero", [P, self.STEP], f32))
        self.zero_set, self.cleared = g.sem("zero_set"), g.sem("tables_cleared")

    def dve(self, dve):
        self.nc.vector.memset(self.zero[:], 0.0).then_inc(self.zero_set, 1)

    def sp(self, sp):
        sp.wait_ge(self.zero_set, 1)
        self.n = 0
        for table in self.tables:
            flat = table.rearrange("n w -> (n w)").rearrange("(p k) -> p k", k=self.ROW)
            for k in range(0, self.ROW, self.STEP):
                m = min(self.STEP, self.ROW - k)
                sp.dma_start(flat[:, k:k + m], self.zero[:, 0:m]).then_inc(self.cleared, 16)
                self.n += 16

    def sp_end(self, sp):
        sp.wait_ge(self.cleared, self.n)


class LateWeights:

    def __init__(self, nc, ctx, g):
        self.nc, self.g, self.n = nc, g, 0
        sb = lambda name, shape: ctx.enter_context(nc.sbuf_tensor(name, shape, f32))
        g.w2in, g.w2out, g.b2col, g.b2out = sb("w2in", [P, 4, P]), sb("w2out", [P, F]), sb("b2col", [P, 1]), sb("b2out", [P, 1])
        g.w3, g.w3x, g.w3y = sb("w3", [P, 4, NB * F]), sb("w3x", [P, 4, 2 * F]), sb("w3y", [P, 4, F + NB])
        g.relrow, self.a2b = sb("relrow", [NREL, RT - F]), sb("A2_b_rows", [NREL, F])
        self.padded, self.loaded, self.rel_loaded = g.sem("late_padded"), g.sem("late_loaded"), g.sem("rel_loaded")

    def dve(self, dve):
        nc, g = self.nc, self.g
        for t in (g.w2in, g.w3, g.w3x, g.w3y):
            nc.vector.memset(t[:], 0.0)
        dve.drain().then_inc(self.padded, 1)
        for f in range(CON):
            nc.vector.tensor_tensor_scan(g.con[:, ::-1, f], g.more[:, ::-1], g.con[:, ::-1, f], 0.0, ALU.mult, ALU.add)
        dve.wait_ge(self.rel_loaded, 64)
        nc.vector.tensor_tensor(g.relrow[:, F:2 * F], g.relrow[:, F:2 * F], self.a2b[:], ALU.add)
        dve.drain()

    def load(self, sp, dst, src):
        sp.dma_start(dst, src).then_inc(self.loaded, 16)
        self.n += 16

    def sp(self, sp):
        g = self.g
        sp.dma_start(g.relrow[:, 2 * F:RT - F], g.w_comp).then_inc(self.rel_loaded, 16)
        sp.dma_start(g.relrow[:, F:2 * F], g.rel_emb).then_inc(self.rel_loaded, 16)
        sp.dma_start(g.relrow[:, 0:F], g.A1_b.partition_broadcast(NREL)).then_inc(self.rel_loaded, 16)
        sp.dma_start(self.a2b[:], g.A2_b.partition_broadcast(NREL)).then_inc(self.rel_loaded, 16)
        self.load(sp, g.w2out[:], g.L2_W2)
        self.load(sp, g.b2col[:], g.L2_b1.unsqueeze(1))
        sp.wait_ge(self.padded, 1)
        for j in range(4):
            rows = slice(F * j, F * (j + 1))
            self.load(sp, g.b2out[rows, :], g.L2_b2.unsqueeze(1))
            self.load(sp, g.w2in[rows, j, :], g.L2_W1)
            self.load(sp, g.w3[rows, j, :], g.weight)
            self.load(sp, g.w3x[rows, j, 0:F], g.slw)
            self.load(sp, g.w3x[rows, j, F:2 * F], g.A1_wT)
            self.load(sp, g.w3y[rows, j, 0:F], g.A2_wT)

    def sp_end(self, sp):
        sp.wait_ge(self.loaded, self.n)


def stage_scatter_g(nc, g):
    st = "s4"
    with ExitStack() as ctx:
        sb = lambda name, shape: ctx.enter_context(nc.sbuf_tensor(f"{st}_{name}", shape, f32))
        pb = lambda name: ctx.enter_context(nc.psum_tensor(f"{st}_{name}", [P, 1024], f32))
        S = lambda name: g.sem(f"{st}_{name}")
        w = Norm(nc, ctx, g, st, C, EC)
        s = Scatter(nc, ctx, g, st)
        mean, hd, tmp = sb("mean", [P, C, F]), sb("h_dst", [P, C, F]), sb("sum", [P, C, F])
        tsb, hid = sb("T", [P, 2, Q * P]), sb("hid_T", [P, 2, Q * P])
        pT, pU, pH, pG = pb("pT"), pb("pU"), pb("pH"), pb("pG")
        ready, turned, turned_sb, hid_done, hid_sb, gr_done = (
            S(x) for x in ("ready", "turned", "turned_sb", "hid_done", "hid_sb", "gr_done"))
        block = ctx.enter_context(nc.Block())

        @block.sync
        def _(sp):
            sp_scatter(g, sp, s)

        @block.gpsimd
        def _(pool):
            pool_scatter(nc, g, pool, s, g.G)

        @block.vector
        def _(dve):
            def front(c):
                dve_true_sum(nc, dve, g, tmp[:], c)
                dve.wait_ge(turned, c * 2 + 2)
                nc.vector.tensor_tensor(mean[:], tmp[:], bc_feat(g.rdeg[:, bass.ds(c * C, C)]), ALU.mult).then_inc(ready, 1)
                dve_norm(nc, dve, w, g.xd[:, bass.ds(c * C, C), :], hd[:], C, c, ready)

            def back(c, a):
                nc.vector.tensor_tensor(g.xd[:, bass.ds(c * C, C), :], g.xd[:, bass.ds(c * C, C), :],
                                        bc_tile(g.b1out[:], C), ALU.add)
                dve.drain()
                s.wait_free(dve, c)
                for half in range(2):
                    H = C // 2
                    part = bass.ds(c * C + half * H, H)
                    dve.wait_ge(gr_done, c * 2 + (half + 1))
                    pv = (pG, pH)[half][:, 0:H * 2 * F].rearrange("p (t c) -> p t c", c=2 * F)
                    nc.vector.tensor_copy(s.rows[:, a, half * H:(half + 1) * H, :], pv[:, :, 0:F])
                    nc.vector.tensor_tensor(g.xd[:, part, :], g.xd[:, part, :], pv[:, :, F:2 * F], ALU.add)
                dve.drain().then_inc(s.ready, 1)

            dve.sem_inc(turned, 2)
            front(0)
            with dve.Fori(0, PAIRS - 1) as i:
                for a in range(2):
                    front(i * 2 + (a + 1))
                    back(i * 2 + a, a)
            front(EC - 1)
            back(EC - 2, 0)
            back(EC - 1, 1)

        @block.scalar
        def _(act):
            def bring(c):
                for k, p in enumerate((pT, pU)):
                    act.wait_ge(turned, c * 2 + (k + 3))
                    nc.scalar.copy(tsb[:, k, :], p[:, 0:Q * P]).then_inc(turned_sb, 1)

            def hidden(c):
                for half in range(2):
                    act.wait_ge(hid_done, c * 2 + (half + 1))
                    nc.scalar.activation(hid[:, half, :], pH[:, 0:Q * P], ACT.Relu, bias=g.b1col[:, 0:1]).then_inc(hid_sb, 1)

            act_norm(nc, act, w, C, 0)
            bring(0)
            with act.Fori(0, EC - 1) as c:
                act_norm(nc, act, w, C, c + 1)
                hidden(c)
                bring(c + 1)
            hidden(EC - 1)

        @block.tensor
        def _(pe):
            with pe.Fori(0, EC) as c:
                pe.wait_ge(ready, c * 2 + 1)
                pe_quads(nc, pT, mean, g.ident[:], Q, turned)
                pe.wait_ge(ready, c * 2 + 2)
                pe_quads(nc, pU, hd, g.ident[:], Q, turned)
                pe.wait_ge(turned_sb, c * 2 + 2)
                s.wait_ready(pe, c - 1)
                for half in range(2):
                    if half:
                        pe.wait_ge(hid_sb, c * 2 + 1)
                    for k in range(Q):
                        r = half * Q + k
                        q = slice((r // 2) * P, (r // 2 + 1) * P)
                        o = pH[:, k * P:(k + 1) * P]
                        nc.tensor.matmul(o, g.w1l[:, r % 2, :], tsb[:, 0, q], start=True, stop=False)
                        last = nc.tensor.matmul(o, g.w1r[:, r % 2, :], tsb[:, 1, q], start=False, stop=True)
                    last.then_inc(hid_done, 1)
                for half in range(2):
                    pe.wait_ge(hid_sb, c * 2 + (half + 1))
                    for k in range(Q):
                        last = nc.tensor.matmul((pG, pH)[half][:, k * P:(k + 1) * P], hid[:, half, k * P:(k + 1) * P],
                                                g.w1gr[:], start=True, stop=True)
                    last.then_inc(gr_done, 1)


def stage_scatter_x2(nc, g):
    st = "s6"
    with ExitStack() as ctx:
        w = Norm(nc, ctx, g, st, C, EC)
        s = Scatter(nc, ctx, g, st)
        tmp = ctx.enter_context(nc.sbuf_tensor("s6_mean", [P, C, F], f32))
        block = ctx.enter_context(nc.Block())

        @block.sync
        def _(sp):
            sp_scatter(g, sp, s)

        @block.gpsimd
        def _(pool):
            pool_scatter(nc, g, pool, s, g.X2)

        @block.vector
        def _(dve):
            with dve.Fori(0, PAIRS) as i:
                for a in range(2):
                    c = i * 2 + a
                    part = bass.ds(c * C, C)
                    dve_true_sum(nc, dve, g, tmp[:], c)
                    nc.vector.tensor_tensor(tmp[:], tmp[:], bc_feat(g.rdeg[:, part]), ALU.mult)
                    dve.drain()
                    s.wait_free(dve, c)
                    nc.vector.tensor_tensor(s.rows[:, a], g.xd[:, part, :], tmp[:], ALU.add)
                    dve.drain().then_inc(s.ready, 1)
                    dve_norm(nc, dve, w, s.rows[:, a], tmp[:, :, CON:F], C, c, lo=CON, hi=F)
                    nc.vector.tensor_tensor(g.con[:, part, :], tmp[:, :, CON:F], bc_feat(g.end[:, part], CON), ALU.mult)
                    dve.drain()

        @block.scalar
        def _(act):
            with act.Fori(0, PAIRS) as i:
                for a in range(2):
                    act_norm(nc, act, w, C, i * 2 + a)


def stage_symmetric(nc, g):
    st = "s8"
    with ExitStack() as ctx:
        sb = lambda name, shape, dt=f32: ctx.enter_context(nc.sbuf_tensor(f"{st}_{name}", shape, dt))
        S = lambda name: g.sem(f"{st}_{name}")
        s = Scatter(nc, ctx, g, st, CW)
        srcb = sb("src_rows", [P, C, P], i32)
        srcc = sb("src_cols", [P, 2, C], i32)
        eq = sb("equal", [P, C, P])
        eqb = sb("equal_before", [P, C, P])
        val = sb("values", [P, C, CW])
        add = sb("add_rows", [P, 2, C, CW])
        aidx = sb("add_idx", [P, 2, C], i32)
        rank, srcf = sb("rank", [P, C]), sb("src_f", [P, C])
        trash, trash_i = sb("trash", [P, 1]), sb("trash_i", [P, 1], i32)
        pS = ctx.enter_context(nc.psum_tensor("s8_pS", [P, 512], f32))
        here, used, eq_ready, summed, add_ready, trash_set = (
            S(x) for x in ("src_here", "src_used", "eq_ready", "summed", "add_ready", "trash_set"))
        idx_ready, add_free = S("add_idx_ready"), S("add_free")
        added = [S("added_a"), S("added_b")]
        block = ctx.enter_context(nc.Block())
        tables = (g.sum_a, g.sum_b)
        PER = 16 * C

        @block.sync
        def _(sp):
            def load(c, a):
                sp.dma_start(s.idx[:, a, :], g.end_index[:, bass.ds(c * C, C)]).then_inc(s.idx_here[a], 16)

            def load_src(c, a):
                sp.wait_ge(used, c + 1)
                sp.dma_start(srcb[:].rearrange("p t k -> p (t k)"),
                             g.src_rows[bass.ds(c * (C * P), C * P)].partition_broadcast(P)).then_inc(here, 16)
                sp.dma_start(srcc[:, a, :], g.src[:, bass.ds(c * C, C)]).then_inc(here, 16)

            sp.sem_inc(add_free, 2)
            load(0, 0)
            load(1, 1)
            with sp.Fori(0, PAIRS - 1) as i:
                load_src(i * 2, 0)
                load_src(i * 2 + 1, 1)
                for a in range(2):
                    s.wait_done(sp, i, a)
                    sp.sem_inc(s.free, 1)
                    load(i * 2 + (a + 2), a)
                for b in range(2):
                    sp.wait_ge(added[b], i * PER + PER)
                sp.sem_inc(add_free, 2)
            load_src(EC - 2, 0)
            load_src(EC - 1, 1)
            for a in range(2):
                s.wait_done(sp, PAIRS - 1, a)
                sp.sem_inc(s.free, 1)
                sp.wait_ge(added[a], PAIRS * PER)

        @block.gpsimd
        def _(pool):
            nc.gpsimd.iota(trash_i[:], pattern=[[0, 1]], base=NPAD, channel_multiplier=1)
            pool.drain()
            nc.gpsimd.tensor_copy(trash[:], trash_i[:])
            pool.drain().then_inc(trash_set, 1)
            with pool.Fori(0, PAIRS) as i:
                for a in range(2):
                    c = i * 2 + a
                    s.wait_idx(pool, i, a)
                    s.wait_ready(pool, c)
                    pool_wait(g, pool)
                    for t in range(C):
                        pool.indirect_dma_start(
                            out=g.sum_dst, out_offset=bass.IndirectOffsetOnAxis(ap=s.idx[:, a, t:t + 1], axis=0),
                            in_=s.rows[:, a, t, :], in_offset=None, bounds_check=NPAD - 1, oob_is_err=False,
                        ).then_inc(s.done[a], 16)
                        if t == 0:
                            pool_wait(g, pool, (idx_ready, c + 1), (add_ready, c + 1))
                        b, turn = t % 2, (a * C + t) // 2
                        if turn:
                            pool_wait(g, pool, (added[b], i * PER + 16 * turn))
                        pool.indirect_dma_start(
                            out=tables[b], out_offset=bass.IndirectOffsetOnAxis(ap=aidx[:, a, t:t + 1], axis=0),
                            in_=add[:, a, t, :], in_offset=None, bounds_check=NTRASH - 1, oob_is_err=True,
                            compute_op=ALU.add,
                        ).then_inc(added[b], 16)
                for b in range(2):
                    pool.wait_ge(added[b], i * PER + PER)

        @block.vector
        def _(dve):
            dve.sem_inc(used, 1)
            nc.vector.memset(val[:], 1.0)
            dve.drain()
            dve.wait_ge(trash_set, 1)
            with dve.Fori(0, PAIRS) as i:
                for a in range(2):
                    c = i * 2 + a
                    part = bass.ds(c * C, C)
                    s.wait_free(dve, c)
                    dve_true_sum(nc, dve, g, s.rows[:, a, :, 0:CON], c, 0, CON)
                    nc.vector.tensor_copy(s.rows[:, a, :, CON:CW], g.deg[:, part].unsqueeze(2))
                    dve.drain().then_inc(s.ready, 1)
                    nc.vector.tensor_tensor(val[:, :, 0:CON], bc_tile(g.carry_back[:, 0:CON], C),
                                            bc_feat(g.suf[:, part], CON), ALU.mult)
                    dve.drain()
                    nc.vector.tensor_tensor(val[:, :, 0:CON], val[:, :, 0:CON], g.con[:, part, :], ALU.add)
                    dve.wait_ge(here, c * 32 + 32)
                    nc.vector.tensor_copy(srcf[:], srcc[:, a, :])
                    dve.drain()
                    nc.vector.tensor_tensor(eq[:], srcb[:], bc_feat(srcf[:], P), ALU.is_equal)
                    dve.drain().then_inc(eq_ready, 1)
                    dve.drain().then_inc(used, 1)
                    nc.vector.tensor_tensor(eqb[:], eq[:], bc_tile(g.before[:], C), ALU.mult)
                    dve.drain()
                    nc.vector.tensor_reduce(rank[:], eqb[:], AX.X, ALU.add)
                    dve.drain()
                    nc.vector.tensor_scalar(srcf[:], srcf[:], trash[:, 0:1], None, ALU.subtract)
                    dve.drain()
                    nc.vector.scalar_tensor_tensor(out=srcf[:], in0=rank[:], scalar=0.0, in1=srcf[:], op0=ALU.is_equal,
                                                   op1=ALU.mult)
                    dve.drain()
                    dve.wait_ge(add_free, c + 1)
                    nc.vector.tensor_scalar(aidx[:, a, :], srcf[:], trash[:, 0:1], None, ALU.add).then_inc(idx_ready, 1)
                    dve.wait_ge(summed, c + 1)

        @block.tensor
        def _(pe):
            with pe.Fori(0, PAIRS) as i:
                for a in range(2):
                    c = i * 2 + a
                    pe.wait_ge(eq_ready, c + 1)
                    if a:
                        pe.wait_ge(add_ready, c)
                    for t in range(C):
                        last = nc.tensor.matmul(pS[:, t * CW:(t + 1) * CW], eq[:, t, :], val[:, t, :], start=True, stop=True)
                    last.then_inc(summed, 1)
                pe.wait_ge(add_ready, i * 2 + 2)

        @block.scalar
        def _(act):
            with act.Fori(0, PAIRS) as i:
                for a in range(2):
                    c = i * 2 + a
                    act.wait_ge(summed, c + 1)
                    act.wait_ge(add_free, c + 1)
                    nc.scalar.copy(add[:, a].rearrange("p t w -> p (t w)"), pS[:, 0:C * CW]).then_inc(add_ready, 1)


def stage_third_layer(nc, g):
    st = "s9"
    with ExitStack() as ctx:
        sb = lambda name, shape: ctx.enter_context(nc.sbuf_tensor(f"{st}_{name}", shape, f32))
        S = lambda name: g.sem(f"{st}_{name}")
        w = Norm(nc, ctx, g, st, C, NC)
        x2 = sb("x2", [P, 3, C, F])
        x3 = sb("x3", [P, 2, C, F])
        sums = sb("sums", [P, 2, 3, C, CW])
        deg = sb("deg", [P, C])
        comb = sb("combined", [P, 2, C, F])
        tsb = sb("T", [P, Q * P])
        hid = sb("hid_T", [P, 4, 512])
        osb = sb("out_T", [P, Q * P])
        pb = lambda name, n=1: ctx.enter_context(nc.psum_tensor(f"{st}_{name}", [P, 512 * n], f32))
        pT, pH, pO, pB = pb("pT", 2), [pb("pH0"), pb("pH1")], pb("pO", 2), pb("pB", 2)
        GROUPS = ((0, 4), (4, 3))
        here = [S("here0"), S("here1")]
        comb_ready, turned, turned_sb, hid_done, hid_sb = (S(x) for x in ("comb_ready", "turned", "turned_sb", "hid_done", "hid_sb"))
        out_done, out_sb, out_back, x3_ready, sums_used, x3_free = (
            S(x) for x in ("out_done", "out_sb", "out_back", "x3_ready", "sums_used", "x3_free"))
        stored = S("stored")
        block = ctx.enter_context(nc.Block())
        HALF = NC // 2

        def cols(t, k, width):
            return t[0:NPAD, :].rearrange("(p t) f -> p (t f)", p=P)[:, bass.ds(k * (C * width), C * width)]

        @block.sync
        def _(sp):
            def load(k, b):
                sp.wait_ge(sums_used, k + 1)
                sp.dma_start(x2[:, b].rearrange("p t f -> p (t f)"), cols(g.X2, k, F)).then_inc(here[b], 16)
                for j, table in enumerate((g.sum_dst, g.sum_a, g.sum_b)):
                    sp.dma_start(sums[:, b, j].rearrange("p t f -> p (t f)"), cols(table, k, CW)).then_inc(here[b], 16)

            sp.sem_inc(x3_free, 2)
            load(0, 0)
            load(1, 1)

            def turn(i, more):
                for b in range(2):
                    k = i * 2 + b
                    sp.wait_ge(x3_ready, k + 1)
                    sp.dma_start(cols(g.out, k, F), x3[:, b].rearrange("p t f -> p (t f)")).then_inc(stored, 16)
                    if more:
                        load(k + 2, b)
                    sp.wait_ge(stored, k * 16 + 16)
                    sp.sem_inc(x3_free, 1)

            with sp.Fori(0, HALF - 1) as i:
                turn(i, True)
            turn(HALF - 1, False)

        @block.vector
        def _(dve):
            dve.sem_inc(sums_used, 2)

            def first(k, b, i):
                dve.wait_ge(here[b], i * 64 + 64)
                dve_norm(nc, dve, w, x2[:, b], comb[:, b, :, 0:CON], C, k, lo=0, hi=CON)
                for j in (1, 2):
                    nc.vector.tensor_tensor(sums[:, b, 0], sums[:, b, 0], sums[:, b, j], ALU.add)
                    dve.drain()
                nc.vector.tensor_scalar(deg[:].unsqueeze(2), sums[:, b, 0, :, CON:CW], 1.0, None, ALU.max)
                dve.drain()
                nc.vector.reciprocal(deg[:], deg[:])
                dve.drain()
                nc.vector.tensor_tensor(comb[:, b, :, CON:F], sums[:, b, 0, :, 0:CON], bc_feat(deg[:], CON), ALU.mult)
                dve.drain().then_inc(comb_ready, 1)

            def second(k, b):
                dve.wait_ge(out_back, k + 1)
                dve.wait_ge(x3_free, k + 1)
                nc.vector.tensor_tensor(x3[:, b], x2[:, b], pB[:, 0:C * F].rearrange("p (t f) -> p t f", f=F), ALU.add)
                dve.drain().then_inc(x3_ready, 1)
                dve.drain().then_inc(sums_used, 1)

            first(0, 0, 0)
            with dve.Fori(0, HALF - 1) as i:
                first(i * 2 + 1, 1, i)
                second(i * 2, 0)
                first(i * 2 + 2, 0, i + 1)
                second(i * 2 + 1, 1)
            first(NC - 1, 1, HALF - 1)
            second(NC - 2, 0)
            second(NC - 1, 1)

        @block.scalar
        def _(act):
            def turn(k):
                act.wait_ge(turned, k + 1)
                nc.scalar.copy(tsb[:], pT[:, 0:Q * P]).then_inc(turned_sb, 1)

            def hidden(k):
                for n in range(8):
                    _, m = GROUPS[n // 4]
                    act.wait_ge(hid_done, k * 8 + (n + 1))
                    nc.scalar.activation(hid[:, n % 4, 0:m * P], pH[n % 2][:, 0:m * P], ACT.Relu, bias=g.b2col[:, 0:1]).then_inc(hid_sb, 1)

            def out(k):
                act.wait_ge(out_done, k + 1)
                nc.scalar.activation(osb[:], pO[:, 0:Q * P], ACT.Identity, bias=g.b2out[:, 0:1]).then_inc(out_sb, 1)

            act_norm(nc, act, w, C, 0)
            turn(0)
            with act.Fori(0, NC - 1) as k:
                hidden(k)
                act_norm(nc, act, w, C, k + 1)
                out(k)
                turn(k + 1)
            hidden(NC - 1)
            out(NC - 1)

        @block.tensor
        def _(pe):
            def quads(k, b):
                pe.wait_ge(comb_ready, k + 1)
                pe_quads(nc, pT, comb[:, b], g.ident[:], Q, turned)

            def hidden(k, n):
                (q, m), j = GROUPS[n // 4], n % 4
                if n == 0:
                    pe.wait_ge(turned_sb, k + 1)
                elif n > 1:
                    pe.wait_ge(hid_sb, k * 8 + (n - 1))
                nc.tensor.matmul(pH[n % 2][:, 0:m * P], g.w2in[:, j, :], tsb[:, q * P:(q + m) * P], start=True,
                                 stop=True).then_inc(hid_done, 1)

            def body(k):
                for n in range(8):
                    (q, m), j = GROUPS[n // 4], n % 4
                    hidden(k, n)
                    if j == 3:
                        pe.wait_ge(hid_sb, k * 8 + (n + 1))
                        for i in range(4):
                            last = nc.tensor.matmul(pO[F * i:F * (i + 1), q * P:(q + m) * P], g.w2out[:], hid[:, i, 0:m * P],
                                                    start=True, stop=True)
                last.then_inc(out_done, 1)

            def back(k):
                pe.wait_ge(out_sb, k + 1)
                for q in range(Q):
                    last = nc.tensor.transpose(pB[:, q * P:(q + 1) * P], osb[:, q * P:(q + 1) * P], g.ident[:])
                last.then_inc(out_back, 1)

            quads(0, 0)
            body(0)
            quads(1, 1)
            back(0)
            with pe.Fori(0, HALF - 1) as i:
                for b in range(2):
                    body(i * 2 + (b + 1))
                    quads(i * 2 + (b + 2), b)
                    pe.wait_ge(x3_ready, i * 2 + (b + 1))
                    back(i * 2 + (b + 1))
            body(NC - 1)
            pe.wait_ge(x3_ready, NC - 1)
            back(NC - 1)


def stage_relations(nc, g):
    st = "s10"
    with ExitStack() as ctx:
        sb = lambda name, shape, dt=f32: ctx.enter_context(nc.sbuf_tensor(f"{st}_{name}", shape, dt))
        pb = lambda name, n=1: ctx.enter_context(nc.psum_tensor(f"{st}_{name}", [P, 512 * n], f32))
        S = lambda name: g.sem(f"{st}_{name}")
        w = Norm(nc, ctx, g, st, C, 2 * EC)
        ring = sb("ring", [P, 2, 2, C, F])
        idx = sb("idx", [P, 2, 2, C], i32)
        h = sb("h", [P, 2, C, F])
        etype = sb("etype", [NREL, C * P], i32)
        onehot = etype[:].bitcast(f32)
        tsb = sb("h_T", [P, 2, Q * P])
        rel = sb("rel", [P, C, RT])
        bases = sb("bases", [P, 2, 2, F, NB])
        msg = w.sq
        att = sb("att", [P, 2, C])
        run = sb("running", [P, 2, C, F])
        pT = pb("pT", 2)
        pR = [pb(f"pR{a}") for a in range(2)]
        pX = [pb(f"pX{a}", 2) for a in range(2)]
        idx_here, rows = [S("idx_here0"), S("idx_here1")], [S("rows0"), S("rows1")]
        (ring_free, type_here, type_free, h_ready, hot_ready, turned, turned_sb, rel_done, rel_sb, bases_done, bases_used,
         scored, squashed, run_ready, run_free) = (S(x) for x in (
             "ring_free", "type_here", "type_free", "h_ready", "hot_ready", "turned", "turned_sb", "rel_done", "rel_sb",
             "bases_done", "bases_used", "scored", "squashed", "run_ready", "run_free"))
        block = ctx.enter_context(nc.Block())
        GAT = 2 * ONCE
        D = C // 2

        @block.sync
        def _(sp):
            def load_idx(c, a):
                sp.dma_start(idx[:, a, 0, :], g.src[:, bass.ds(c * C, C)]).then_inc(idx_here[a], 16)
                sp.dma_start(idx[:, a, 1, :], g.dst[:, bass.ds(c * C, C)]).then_inc(idx_here[a], 16)

            def load_type(c):
                sp.wait_ge(type_free, c + 1)
                sp.dma_start(etype[:], g.etype_rows[bass.ds(c * (C * P), C * P)].partition_broadcast(NREL)).then_inc(type_here, 16)

            sp.sem_inc(type_free, 1)
            for a in range(2):
                load_idx(a, a)
            load_type(0)
            with sp.Fori(0, PAIRS - 1) as i:
                for a in range(2):
                    sp.wait_ge(rows[a], i * GAT + GAT)
                    load_idx(i * 2 + (a + 2), a)
                    load_type(i * 2 + (a + 1))
            load_type(EC - 1)

        @block.gpsimd
        def _(pool):
            with pool.Fori(0, PAIRS) as i:
                for a in range(2):
                    pool_wait(g, pool, (idx_here[a], i * 32 + 32), (ring_free, i * 2 + (a + 1)))
                    for k in range(2):
                        for t in range(C):
                            pool.indirect_dma_start(
                                out=ring[:, a, k, t, :], out_offset=None, in_=g.out,
                                in_offset=bass.IndirectOffsetOnAxis(ap=idx[:, a, k, t:t + 1], axis=0),
                            ).then_inc(rows[a], 16)

        @block.vector
        def _(dve):
            nc.vector.memset(run[:, 1, C - 1, :], 0.0)
            dve.drain()
            with dve.Fori(0, PAIRS) as i:
                for a in range(2):
                    c = i * 2 + a
                    part = bass.ds(c * C, C)
                    dve.wait_ge(type_here, c * 16 + 16)
                    nc.vector.tensor_scalar(onehot, etype[:], g.relid[:, 0:1], None, ALU.is_equal).then_inc(hot_ready, 1)
                    dve.wait_ge(rows[a], i * GAT + GAT)
                    for k in range(2):
                        dve_norm(nc, dve, w, ring[:, a, k], h[:, k], C, c * 2 + k, h_ready)
                    for d in range(D):
                        ts = slice(2 * d, 2 * d + 2)
                        if d % 2 == 0:
                            dve.wait_ge(rel_sb, c * Q + (d // 2 + 1))
                        dve.wait_ge(bases_done, c * D + (d + 1))
                        nc.vector.tensor_tensor(bases[:, d % 2], pX[d % 2][:].rearrange("p (t o b) -> p t o b", t=2, b=NB),
                                                rel[:, ts, RT - NB:RT].unsqueeze(2).to_broadcast([P, 2, F, NB]), ALU.mult)
                        dve.drain().then_inc(bases_used, 1)
                        nc.vector.tensor_reduce(msg[:, ts, :], bases[:, d % 2], AX.X, ALU.add)
                    prod = w.xc
                    nc.vector.tensor_tensor(prod[:], rel[:, :, F:2 * F], rel[:, :, 2 * F:3 * F], ALU.mult)
                    dve.drain()
                    nc.vector.tensor_reduce(att[:, 0, :], prod[:], AX.X, ALU.add)
                    dve.drain()
                    nc.vector.tensor_scalar(att[:, 0, :], att[:, 0, :], 1.0 / float(F) ** 0.5, 0.0, ALU.mult, ALU.max).then_inc(scored, 1)
                    nc.vector.tensor_tensor(rel[:, :, 0:F], rel[:, :, 0:F], bc_feat(g.end[:, part]), ALU.mult)
                    dve.wait_ge(squashed, c + 1)
                    nc.vector.tensor_tensor(msg[:], msg[:], bc_feat(att[:, 1, :]), ALU.mult)
                    dve.drain()
                    nc.vector.tensor_tensor(msg[:], msg[:], rel[:, :, 0:F], ALU.add)
                    dve.drain()
                    dve.wait_ge(run_free, c + 1)
                    for f in range(F):
                        nc.vector.tensor_tensor_scan(run[:, a, :, f], g.same[:, part], msg[:, :, f], run[:, 1 - a, C - 1, f:f + 1],
                                                     ALU.mult, ALU.add)
                    dve.drain().then_inc(run_ready, 1)

        @block.scalar
        def _(act):
            act.sem_inc(run_free, 2)
            act.sem_inc(ring_free, 2)
            with act.Fori(0, PAIRS) as i:
                for a in range(2):
                    c = i * 2 + a
                    for k in range(2):
                        act_norm(nc, act, w, C, c * 2 + k)
                        act.wait_ge(turned, c * 2 + (k + 1))
                        nc.scalar.copy(tsb[:, k, :], pT[:, 0:Q * P]).then_inc(turned_sb, 1)
                    nc.scalar.copy(g.xd[:, bass.ds(c * C, C), :], ring[:, a, 1])
                    act.drain().then_inc(ring_free, 1)
                    for q in range(Q):
                        act.wait_ge(rel_done, c * Q + (q + 1))
                        nc.scalar.copy(rel[:, 4 * q:4 * q + 4, :].rearrange("p t c -> p (t c)"), pR[q % 2][:, 0:4 * RT]).then_inc(rel_sb, 1)
                    act.wait_ge(scored, c + 1)
                    nc.scalar.activation(att[:, 1, :], att[:, 0, :], ACT.Tanh).then_inc(squashed, 1)
                    act.wait_ge(run_ready, c + 1)
                    nc.scalar.copy(g.agg[:, bass.ds(c * C, C), :], run[:, a]).then_inc(run_free, 1)

        @block.tensor
        def _(pe):
            with pe.Fori(0, PAIRS) as i:
                for a in range(2):
                    c = i * 2 + a
                    for k in range(2):
                        pe.wait_ge(h_ready, c * 2 + (k + 1))
                        pe_quads(nc, pT, h[:, k], g.ident[:], Q, turned)
                        pe.wait_ge(turned_sb, c * 2 + (k + 1))
                    pe.wait_ge(hot_ready, c + 1)
                    for q in range(Q):
                        quad = slice(q * P, (q + 1) * P)
                        o = pR[q % 2][:, 0:4 * RT].rearrange("p (t c) -> p t c", c=RT)
                        if q > 1:
                            pe.wait_ge(rel_sb, c * Q + (q - 1))
                        nc.tensor.matmul(o[:, :, 0:2 * F], tsb[:, 0, quad], g.w3x[:], start=True, stop=False)
                        nc.tensor.matmul(o[:, :, 2 * F:RT], tsb[:, 1, quad], g.w3y[:], start=False, stop=False)
                        for j in range(4):
                            t = 4 * q + j
                            last = nc.tensor.matmul(o[:, j, F:RT], onehot[:, t * P:(t + 1) * P], g.relrow[:], start=False,
                                                    stop=(j == 3))
                        last.then_inc(rel_done, 1)
                        for d in (2 * q, 2 * q + 1):
                            if d > 1:
                                pe.wait_ge(bases_used, c * D + (d - 1))
                            for j in range(2):
                                last = nc.tensor.matmul(pX[d % 2][:, j * 512:(j + 1) * 512], tsb[:, 0, quad],
                                                        g.w3[:, (2 * d + j) % 4, :], start=True, stop=True)
                            last.then_inc(bases_done, 1)
                    pe.drain().then_inc(type_free, 1)
                    pe.wait_ge(bases_used, c * D + D)


def stage_scatter_out(nc, g):
    with ExitStack() as ctx:
        s = Scatter(nc, ctx, g, "s11")
        tmp = ctx.enter_context(nc.sbuf_tensor("s11_sum", [P, C, F], f32))
        block = ctx.enter_context(nc.Block())

        @block.sync
        def _(sp):
            sp_scatter(g, sp, s)

        @block.gpsimd
        def _(pool):
            pool_scatter(nc, g, pool, s, g.out)

        @block.vector
        def _(dve):
            with dve.Fori(0, PAIRS) as i:
                for a in range(2):
                    c = i * 2 + a
                    dve_true_sum(nc, dve, g, tmp[:], c)
                    s.wait_free(dve, c)
                    nc.vector.scalar_tensor_tensor(out=s.rows[:, a], in0=tmp[:], scalar=0.0, in1=g.xd[:, bass.ds(c * C, C), :],
                                                   op0=ALU.max, op1=ALU.add)
                    dve.drain().then_inc(s.ready, 1)


def build(nc, A, stages=99, dbg=()):
    g = Globals()
    g.x, g.src, g.dst, g.dst_flat, g.src_rows, g.etype_rows = (
        A[k] for k in ("x", "src", "dst", "dst_flat", "src_rows", "etype_rows"))
    g.W, g.WT, g.att_src, g.att_dst, g.bias = (A[k] for k in ("W", "WT", "att_src", "att_dst", "bias"))
    g.W1_lT, g.W1_rT, g.L1_b1, g.W2_lT, g.W2_rT, g.L1_b2 = (A[k] for k in ("W1_lT", "W1_rT", "L1_b1", "W2_lT", "W2_rT", "L1_b2"))
    g.L2_W1, g.L2_b1, g.L2_W2, g.L2_b2 = (A[k] for k in ("L2_W1", "L2_b1", "L2_W2", "L2_b2"))
    g.weight, g.w_comp, g.slw, g.A1_wT, g.A1_b, g.A2_wT, g.A2_b, g.rel_emb = (
        A[k] for k in ("weight", "w_comp", "slw", "A1_wT", "A1_b", "A2_wT", "A2_b", "rel_emb"))
    g.out = A["out"]
    dram = lambda name, shape, dt=f32: nc.dram_tensor(name, shape, dt, kind="ExternalOutput" if name in dbg else "Internal").ap()
    g.X1, g.X2, g.G = (dram(n, (NPAD, F)) for n in ("x1_table", "x2_table", "g_table"))
    g.sum_dst, g.sum_a, g.sum_b = (dram(n, (NTRASH, CW)) for n in ("sum_dst_table", "sum_a_table", "sum_b_table"))
    g.end_index = dram("end_index_table", (P, ET), i32)
    with ExitStack() as ctx:
        g.sem = lambda name: ctx.enter_context(nc.semaphore(name))
        sb = lambda name, shape, dt=f32: ctx.enter_context(nc.sbuf_tensor(name, shape, dt))
        g.pool_steps = g.sem("pool_steps")
        g.norm_sems = [g.sem(f"norm_{x}") for x in ("centered", "squared", "summed", "rooted")]
        g.carry_sems = [g.sem(f"carry_{x}") for x in ("copied", "turned", "scanned", "back")]
        g.scatter_sems = ([g.sem(f"scatter_idx_here{a}") for a in range(2)], [g.sem(f"scattered{a}") for a in range(2)],
                          g.sem("scatter_rows_ready"), g.sem("scatter_rows_free"))
        g.norms = g.carries = g.scatters = 0
        g.xd = sb("x_dst", [P, ET, F])
        g.agg = sb("agg", [P, ET, F])
        g.same, g.more, g.end = (sb(n, [P, ET]) for n in ("same_as_before", "same_as_after", "is_last"))
        g.pre, g.suf = sb("same_from_start", [P, ET]), sb("same_to_end", [P, ET])
        g.deg, g.rdeg = sb("deg", [P, ET]), sb("rdeg", [P, ET])
        g.preall, g.sufall = sb("preall", [CARRY, P]), sb("sufall", [CARRY, P])
        g.carry, g.carry_back = sb("carry", [P, CARRY]), sb("carry_back", [P, CARRY])
        g.ident, g.before = sb("ident", [P, P]), sb("before", [P, P])
        g.relid, g.relid_i, g.eps = sb("relid", [NREL, 1]), sb("relid_i", [NREL, 1], i32), sb("eps", [P, 1])
        g.w0, g.bias0, g.watt = sb("w0", [P, P]), sb("bias0", [P, F]), sb("watt", [P, 3, F])
        g.w1l, g.w1r, g.w1gr = sb("w1l", [P, 2, P]), sb("w1r", [P, 2, P]), sb("w1gr", [P, P])
        g.b1col, g.b1out = sb("b1col", [P, 1]), sb("b1out", [P, F])
        stage_setup(nc, g)
        if stages < 1: return
        with ExitStack() as attention:
            g.e_edge, g.e_self = (attention.enter_context(nc.sbuf_tensor(n, [P, ET], f32)) for n in ("e_edge", "e_self"))
            stage_first_gather(nc, g)
            if stages < 2: return
            g.rden = attention.enter_context(nc.sbuf_tensor("rden", [P, ET], f32))
            stage_softmax(nc, g)
            stage_scatter_x1(nc, g)
        if stages < 3: return
        with ExitStack() as zeros:
            stage_gather(nc, g, "s3", g.X1, norm=True, beside=ClearTables(nc, zeros, g))
        stage_carry(nc, g, "s3c", [g.agg[:, ET - 1, :]])
        stage_scatter_g(nc, g)
        if stages < 4: return
        stage_gather(nc, g, "s5", g.G, norm=False)
        stage_carry(nc, g, "s5c", [g.agg[:, ET - 1, :]])
        late_space = ctx.enter_context(ExitStack())
        late = LateWeights(nc, late_space, g)
        with ExitStack() as con:
            g.con = con.enter_context(nc.sbuf_tensor("conical_dst", [P, ET, CON], f32))
            stage_scatter_x2(nc, g)
            if stages < 5: return
            stage_gather(nc, g, "s7", g.X2, norm=True, lo=CON, hi=F, beside=late)
            stage_carry(nc, g, "s7c", [g.agg[:, ET - 1, 0:CON]])
            stage_carry(nc, g, "s7r", [g.con[:, 0, :]], reverse=True)
            stage_symmetric(nc, g)
        if stages < 6: return
        stage_third_layer(nc, g)
        if stages < 7: return
        stage_relations(nc, g)
        stage_carry(nc, g, "s10c", [g.agg[:, ET - 1, :]])
        stage_scatter_out(nc, g)


def kernel(x, src, dst, edge_type_86, L0_gnn_W, L0_gnn_att_src, L0_gnn_att_dst, L0_gnn_bias, L1_gnn_W1_l, L1_gnn_W1_r,
           L1_gnn_b1, L1_gnn_W2_l, L1_gnn_W2_r, L1_gnn_b2, L2_gnn_W1, L2_gnn_b1, L2_gnn_W2, L2_gnn_b2, L3_gnn_weight,
           L3_gnn_w_comp, L3_gnn_self_loop_weight, L3_gnn_A1_w, L3_gnn_A1_b, L3_gnn_A2_w, L3_gnn_A2_b, L3_gnn_rel_emb,
           launch=None):
    import numpy as np

    def rows(a, fill):
        a = np.asarray(a)
        out = np.full((EPAD,), fill, a.dtype)
        out[:E] = a
        return out

    src_p, dst_p, et_p = rows(src, N), rows(dst, N), rows(edge_type_86, 0)
    xp = np.zeros((NPAD, F), np.float32)
    xp[:N] = np.asarray(x)
    flat = np.full((EPAD + 2,), -1, np.int32)
    flat[1:-1] = dst_p
    T = lambda a: np.ascontiguousarray(np.asarray(a).T)
    arrays = {
        "x": xp, "src": src_p.reshape(P, ET), "dst": dst_p.reshape(P, ET), "dst_flat": flat,
        "src_rows": T(src_p.reshape(P, ET)).reshape(-1), "etype_rows": T(et_p.reshape(P, ET)).reshape(-1),
        "W": L0_gnn_W, "WT": T(L0_gnn_W), "att_src": L0_gnn_att_src, "att_dst": L0_gnn_att_dst, "bias": L0_gnn_bias,
        "W1_lT": T(L1_gnn_W1_l), "W1_rT": T(L1_gnn_W1_r), "L1_b1": L1_gnn_b1, "W2_lT": T(L1_gnn_W2_l),
        "W2_rT": T(L1_gnn_W2_r), "L1_b2": L1_gnn_b2, "L2_W1": L2_gnn_W1, "L2_b1": L2_gnn_b1, "L2_W2": L2_gnn_W2,
        "L2_b2": L2_gnn_b2, "weight": np.transpose(np.asarray(L3_gnn_weight), (1, 2, 0)).reshape(F, NB * F), "w_comp": L3_gnn_w_comp, "slw": L3_gnn_self_loop_weight,
        "A1_wT": T(L3_gnn_A1_w), "A1_b": L3_gnn_A1_b, "A2_wT": T(L3_gnn_A2_w), "A2_b": L3_gnn_A2_b,
        "rel_emb": L3_gnn_rel_emb,
    }
    arrays = {k: np.ascontiguousarray(np.asarray(a)) for k, a in arrays.items()}
    import concourse.bacc as bacc
    from concourse.bass_utils import run_bass_kernel_spmd

    nc = bacc.Bacc("TRN2", target_bir_lowering=False, num_devices=1)
    A = {k: nc.dram_tensor(f"in_{k}", a.shape, mybir.dt.from_np(a.dtype), kind="ExternalInput").ap() for k, a in arrays.items()}
    A["out"] = nc.dram_tensor("out_x", (NPAD, F), f32, kind="ExternalOutput").ap()
    if launch is not None:
        return launch(nc, A, arrays)
    build(nc, A)
    r = run_bass_kernel_spmd(nc, [{f"in_{k}": a for k, a in arrays.items()}], core_ids=[0])
    return r.results[0]["out_x"][:N]
```

```python
import concourse.bass as bass
from concourse import mybir
from contextlib import ExitStack

f32 = mybir.dt.float32
i32 = mybir.dt.int32
ALU = mybir.AluOpType
ACT = mybir.ActivationFunctionType
AX = mybir.AxisListType

P = 128
F = 32
N, E = 100000, 50000
C = 28
Q = C // 4
EC = 14
ET = EC * C
EPAD = P * ET
NC = 28
NT = NC * C
NPAD = P * NT
NTRASH = NPAD + P
PAIRS = EC // 2
CARRY = F + 1
OUTSIDE = 1 << 20
HID1, HID2 = 64, 128
CON = 16
CW = CON + 1
NREL, NB = 86, 16
RT = 3 * F + NB
EPS = 1e-5
NEG = -1.0e38


def bc_feat(ap, n=F):
    return ap.unsqueeze(2).to_broadcast([ap.shape[0], ap.shape[1], n])


def bc_tile(ap, n):
    return ap.unsqueeze(1).to_broadcast([ap.shape[0], n, ap.shape[1]])


def dve_norm(nc, dve, w, x, out, T, n, done=None, lo=0, hi=F, meanwhile=(None, None)):
    nc.vector.tensor_reduce(w.stat[:, 0, 0:T], x, AX.X, ALU.add)
    dve.drain()
    nc.vector.scalar_tensor_tensor(out=w.xc[:, 0:T, :], in0=bc_feat(w.stat[:, 0, 0:T]), scalar=-1.0 / F,
                                   in1=x, op0=ALU.mult, op1=ALU.add).then_inc(w.centered, 1)
    if meanwhile[0] is not None:
        meanwhile[0]()
    dve.wait_ge(w.squared, n + (w.base + 1))
    nc.vector.tensor_reduce(w.stat[:, 1, 0:T], w.sq[:, 0:T, :], AX.X, ALU.add).then_inc(w.summed, 1)
    if meanwhile[1] is not None:
        meanwhile[1]()
    dve.wait_ge(w.rooted, n + (w.base + 1))
    nc.vector.reciprocal(w.stat[:, 3, 0:T], w.stat[:, 2, 0:T])
    dve.drain()
    last = nc.vector.scalar_tensor_tensor(out=out, in0=w.xc[:, 0:T, lo:hi], scalar=0.0,
                                          in1=bc_feat(w.stat[:, 3, 0:T], hi - lo), op0=ALU.max, op1=ALU.mult)
    if done is not None:
        last.then_inc(done, 1)
    else:
        dve.drain()


def act_norm(nc, act, w, T, n):
    act_square(nc, act, w, T, n)
    act_root(nc, act, w, T, n)


def act_square(nc, act, w, T, n):
    act.wait_ge(w.centered, n + (w.base + 1))
    nc.scalar.activation(w.sq[:, 0:T, :], w.xc[:, 0:T, :], ACT.Square).then_inc(w.squared, 1)


def act_root(nc, act, w, T, n):
    act.wait_ge(w.summed, n + (w.base + 1))
    nc.scalar.activation(w.stat[:, 2, 0:T], w.stat[:, 1, 0:T], ACT.Sqrt, bias=w.eps[:, 0:1],
                         scale=1.0 / F).then_inc(w.rooted, 1)


def pool_wait(g, pool, *waits):
    for sem, value in waits:
        pool.wait_ge(sem, value)
    pool.sem_inc(g.pool_steps, 1)


class Norm:

    def __init__(self, nc, ctx, g, stage, T, norms):
        self.xc = ctx.enter_context(nc.sbuf_tensor(f"{stage}_xc", [P, T, F], f32))
        self.sq = ctx.enter_context(nc.sbuf_tensor(f"{stage}_sq", [P, T, F], f32))
        self.stat = ctx.enter_context(nc.sbuf_tensor(f"{stage}_stat", [P, 4, T], f32))
        self.eps = g.eps
        self.centered, self.squared, self.summed, self.rooted = g.norm_sems
        self.base, self.norms = g.norms, norms
        g.norms += norms


class Globals:
    pass


def pe_quads(nc, pt, src, ident, nquads, done):
    for q in range(nquads):
        last = nc.tensor.transpose(pt[:, q * P:(q + 1) * P], src[:, 4 * q:4 * q + 4, :].rearrange("p t f -> p (t f)"),
                                   ident)
    last.then_inc(done, 1)


class Ends:

    EARLY = 7

    def __init__(self, nc, ctx, g):
        self.g = g
        self.ring = ctx.enter_context(nc.sbuf_tensor("ends_ring", [P, 2, 2, C, F], f32))
        self.idx = ctx.enter_context(nc.sbuf_tensor("ends_idx", [P, 2, 2, C], i32))
        self.idx_here = [g.sem(f"ends_idx_here{a}") for a in range(2)]
        self.rows = [g.sem(f"ends_rows{a}") for a in range(2)]

    def load_idx(self, sp, c, a):
        sp.dma_start(self.idx[:, a, 0, :], self.g.src[:, bass.ds(c * C, C)]).then_inc(self.idx_here[a], 16)
        sp.dma_start(self.idx[:, a, 1, :], self.g.dst[:, bass.ds(c * C, C)]).then_inc(self.idx_here[a], 16)

    def gather(self, pool, a, tiles):
        for t in tiles:
            for k in range(2):
                pool.indirect_dma_start(
                    out=self.ring[:, a, k, t, :], out_offset=None, in_=self.g.x,
                    in_offset=bass.IndirectOffsetOnAxis(ap=self.idx[:, a, k, t:t + 1], axis=0),
                ).then_inc(self.rows[a], 16)


def stage_setup(nc, g, ends):
    with ExitStack() as ctx:
        sb = lambda name, shape, dt=f32: ctx.enter_context(nc.sbuf_tensor(name, shape, dt))
        dwin = sb("dst_windows", [P, 3, ET], i32)
        dwf = sb("dst_windows_f", [P, 3, ET])
        endf = sb("end_index_f", [P, ET])
        endi = sb("end_index", [P, ET], i32)
        att4 = sb("att_cols", [F, 3])
        wT = sb("W_T", [F, F])
        pw = ctx.enter_context(nc.psum_tensor("p_watt", [P, 512], f32))
        pa = ctx.enter_context(nc.psum_tensor("p_all", [P, 512], f32))
        loaded, flags, end_stored = (g.sem(n) for n in ("su_loaded", "su_flags", "su_end_stored"))
        padded, ident_set, watt_done = (g.sem(n) for n in ("su_padded", "su_ident", "su_watt"))
        att_loaded, att_sum, all_done, dst_loaded = (g.sem(n) for n in ("su_att", "su_att_sum", "su_all", "su_dst"))
        block = ctx.enter_context(nc.Block())

        @block.sync
        def _(sp):
            ends.load_idx(sp, 0, 0)
            for k in range(3):
                sp.dma_start(dwin[:, k, :], g.dst_flat[k:k + EPAD].rearrange("(p t) -> p t", t=ET)).then_inc(dst_loaded, 16)
            sp.dma_start(att4[:, 0:1], g.att_src.unsqueeze(1)).then_inc(att_loaded, 16)
            sp.dma_start(att4[:, 1:2], g.att_dst.unsqueeze(1)).then_inc(att_loaded, 16)
            sp.dma_start(wT[:], g.WT).then_inc(att_loaded, 16)
            sp.wait_ge(padded, 1)
            n = 0

            def load(dst, src):
                nonlocal n
                n += 1
                sp.dma_start(dst, src).then_inc(loaded, 16)

            for j in range(4):
                load(g.w0[F * j:F * (j + 1), F * j:F * (j + 1)], g.W)
                r, jj = j // 2, j % 2
                load(g.w1l[F * j:F * (j + 1), r, HID1 * jj:HID1 * (jj + 1)], g.W1_lT)
                load(g.w1r[F * j:F * (j + 1), r, HID1 * jj:HID1 * (jj + 1)], g.W1_rT)
            for jj in range(2):
                k = HID1 * jj
                load(g.w1gr[k:k + HID1, k:k + F], g.W2_lT)
                load(g.w1gr[k:k + HID1, k + F:k + 2 * F], g.W2_rT)
                load(g.b1col[k:k + HID1, 0:1], g.L1_b1.unsqueeze(1))
            load(g.bias0[:], g.bias.partition_broadcast(P))
            load(g.b1out[:], g.L1_b2.partition_broadcast(P))
            sp.wait_ge(flags, 1)
            sp.dma_start(g.end_index, endi[:]).then_inc(end_stored, 16)
            sp.wait_ge(end_stored, 16)
            sp.wait_ge(loaded, 16 * n)

        @block.gpsimd
        def _(pool):
            nc.gpsimd.memset(g.ident[:], 0.0)
            nc.gpsimd.memset(g.before[:], 1.0)
            pool.drain()
            nc.gpsimd.affine_select(out=g.ident[:], in_=g.ident[:], compare_op=ALU.not_equal, fill=1.0, base=0,
                                    pattern=[[-1, P]], channel_multiplier=1)
            nc.gpsimd.affine_select(out=g.before[:], in_=g.before[:], compare_op=ALU.is_gt, fill=0.0, base=0,
                                    pattern=[[-1, P]], channel_multiplier=1)
            nc.gpsimd.iota(g.relid_i[:], pattern=[[0, 1]], base=0, channel_multiplier=1)
            pool.drain()
            nc.gpsimd.tensor_copy(g.relid[:], g.relid_i[:])
            pool.drain().then_inc(ident_set, 1)
            pool_wait(g, pool, (ends.idx_here[0], 32))
            ends.gather(pool, 0, range(Ends.EARLY))

        @block.vector
        def _(dve):
            dve.sem_inc(g.scatter_sems[3], 2)
            for t in (g.w0, g.w1l, g.w1r, g.w1gr):
                nc.vector.memset(t[:], 0.0)
            nc.vector.memset(g.eps[:], EPS)
            dve.drain().then_inc(padded, 1)
            dve.wait_ge(att_loaded, 48)
            nc.vector.tensor_tensor(att4[:, 2:3], att4[:, 0:1], att4[:, 1:2], ALU.add).then_inc(att_sum, 1)
            dve.wait_ge(dst_loaded, 48)
            nc.vector.tensor_copy(dwf[:], dwin[:])
            dve.drain()
            nc.vector.tensor_tensor(g.same[:], dwf[:, 1, :], dwf[:, 0, :], ALU.is_equal)
            nc.vector.tensor_tensor(g.more[:], dwf[:, 1, :], dwf[:, 2, :], ALU.is_equal)
            dve.drain()
            nc.vector.tensor_scalar(g.end[:], g.more[:], -1.0, 1.0, ALU.mult, ALU.add)
            nc.vector.tensor_tensor_scan(g.pre[:], g.same[:], g.same[:], 1.0, ALU.mult, ALU.mult)
            nc.vector.tensor_tensor_scan(g.suf[:, ::-1], g.more[:, ::-1], g.more[:, ::-1], 1.0, ALU.mult, ALU.mult)
            nc.vector.tensor_scalar(endf[:], g.more[:], float(OUTSIDE), None, ALU.mult)
            dve.drain()
            nc.vector.tensor_tensor(endf[:], endf[:], dwf[:, 1, :], ALU.add)
            nc.vector.memset(g.deg[:], 1.0)
            dve.drain()
            nc.vector.tensor_copy(endi[:], endf[:]).then_inc(flags, 1)
            nc.vector.tensor_tensor_scan(g.deg[:], g.same[:], g.deg[:], 0.0, ALU.mult, ALU.add)
            dve.drain().then_inc(flags, 1)
            dve.wait_ge(watt_done, 1)
            nc.vector.tensor_copy(g.watt[:], pw[:, 0:3 * F].rearrange("p (k f) -> p k f", f=F))
            dve.wait_ge(all_done, 1)
            nc.vector.tensor_copy(g.preall[:], pa[0:CARRY, 0:P])
            nc.vector.tensor_copy(g.sufall[:], pa[0:CARRY, P:2 * P])
            dve.drain().then_inc(flags, 1)

        @block.tensor
        def _(pe):
            pe.wait_ge(att_sum, 1)
            for k in range(3):
                last = nc.tensor.matmul(pw[:, k * F:(k + 1) * F], att4[:, k:k + 1].to_broadcast([F, P]), wT[:], start=True, stop=True)
            last.then_inc(watt_done, 1)
            pe.wait_ge(flags, 2)
            pe.wait_ge(ident_set, 1)
            nc.tensor.matmul(pa[0:CARRY, 0:P], g.pre[:, ET - 1:ET].to_broadcast([P, CARRY]), g.ident[:], start=True, stop=True)
            nc.tensor.matmul(pa[0:CARRY, P:2 * P], g.suf[:, 0:1].to_broadcast([P, CARRY]), g.ident[:], start=True,
                             stop=True).then_inc(all_done, 1)

    stage_carry(nc, g, "deg", [g.deg[:, ET - 1:ET]])
    with ExitStack() as ctx:
        block = ctx.enter_context(nc.Block())

        @block.vector
        def _(dve):
            nc.vector.scalar_tensor_tensor(out=g.deg[:], in0=g.pre[:], scalar=g.carry[:, 0:1], in1=g.deg[:],
                                           op0=ALU.mult, op1=ALU.add)
            dve.drain()
            nc.vector.reciprocal(g.rdeg[:], g.deg[:])


def stage_carry(nc, g, stage, parts, reverse=False, greatest=False):
    n = sum(p.shape[1] for p in parts)
    with ExitStack() as ctx:
        own = ctx.enter_context(nc.sbuf_tensor(f"{stage}_own", [P, n], f32))
        row = ctx.enter_context(nc.sbuf_tensor(f"{stage}_row", [n, P + 1], f32))
        cut = ctx.enter_context(nc.sbuf_tensor(f"{stage}_cut", [n, P], f32))
        pr = ctx.enter_context(nc.psum_tensor(f"{stage}_prow", [n, P], f32))
        pc = ctx.enter_context(nc.psum_tensor(f"{stage}_pcol", [P, n], f32))
        copied, turned, scanned, back = g.carry_sems
        g.carries += 1
        now = g.carries
        block = ctx.enter_context(nc.Block())

        @block.vector
        def _(dve):
            k = 0
            for part in parts:
                nc.vector.tensor_copy(own[:, k:k + part.shape[1]], part)
                k += part.shape[1]
            nc.vector.memset(row[:, P:P + 1] if reverse else row[:, 0:1], NEG if greatest else 0.0)
            if greatest:
                nc.vector.tensor_scalar(cut[:], g.preall[0:n, :], -NEG, NEG, ALU.mult, ALU.add)
            dve.drain().then_inc(copied, 1)
            dve.wait_ge(turned, now)
            if reverse:
                nc.vector.tensor_tensor_scan(row[:, 0:P][:, ::-1], g.sufall[0:n, ::-1], pr[:, ::-1], 0.0, ALU.mult, ALU.add)
            elif greatest:
                nc.vector.tensor_tensor_scan(row[:, 1:P + 1], cut[:], pr[:], NEG, ALU.add, ALU.max)
            else:
                nc.vector.tensor_tensor_scan(row[:, 1:P + 1], g.preall[0:n, :], pr[:], 0.0, ALU.mult, ALU.add)
            dve.drain().then_inc(scanned, 1)
            dve.wait_ge(back, now)
            nc.vector.tensor_copy((g.carry_back if reverse else g.carry)[:, 0:n], pc[:])

        @block.tensor
        def _(pe):
            pe.wait_ge(copied, now)
            nc.tensor.transpose(pr[:], own[:], g.ident[:]).then_inc(turned, 1)
            pe.wait_ge(scanned, now)
            nc.tensor.transpose(pc[:], row[:, 1:P + 1] if reverse else row[:, 0:P], g.ident[0:n, 0:n]).then_inc(back, 1)


def stage_first_gather(nc, g, ends):
    st = "s1"
    with ExitStack() as ctx:
        sb = lambda name, shape, dt=f32: ctx.enter_context(nc.sbuf_tensor(f"{st}_{name}", shape, dt))
        pb = lambda name: ctx.enter_context(nc.psum_tensor(f"{st}_{name}", [P, 1024], f32))
        S = lambda name: g.sem(f"{st}_{name}")
        w = Norm(nc, ctx, g, st, C, 12 * PAIRS)
        ring = ends.ring
        hedge = sb("h_edge", [P, 2 * C, F])
        dots = sb("dots", [P, 5, C])
        x0 = sb("x0", [P, 2, C, F])
        x1 = sb("x1", [P, 2, C, F])
        x2 = sb("x2", [P, 2, C, F])
        gt = sb("g", [P, 2, C, F])
        hd = sb("h_node", [P, 2, C, F])
        tsb = sb("h_T", [P, Q * P])
        hid = sb("hid_T", [P, 2, Q * P])
        pT, pW, pH, pG = pb("pT"), pb("pW"), pb("pH"), pb("pG")
        rows = ends.rows
        x0_here = [S("x0_here0"), S("x0_here1")]
        ring_free, h_edge_ready = S("ring_free"), S("h_edge_ready")
        h0_ready, h1_ready, turned, turned_sb = S("h0_ready"), S("h1_ready"), S("turned"), S("turned_sb")
        w_done, hid_done, hid_sb, gr_done = S("w_done"), S("hid_done"), S("hid_sb"), S("gr_done")
        x1_ready, x2_ready, stored, dense_free = S("x1_ready"), S("x2_ready"), S("stored"), S("dense_free")
        block = ctx.enter_context(nc.Block())
        GAT = 16 * 2 * C

        def norms_before(i, a):
            return i * 12 + (6 * a + 5)

        def cols(t, k, n=C * F):
            return t.rearrange("(p t) f -> p (t f)", p=P)[:, bass.ds(k * (C * F), n)]

        @block.sync
        def _(sp):
            def load_x(k, b):
                sp.dma_start(x0[:, b].rearrange("p t f -> p (t f)"), cols(g.x, k)).then_inc(x0_here[b], 16)

            sp.sem_inc(dense_free, 2)
            ends.load_idx(sp, 1, 1)
            for a in range(2):
                load_x(a, a)

            def turn(i, more):
                for a in range(2):
                    for m in range(2):
                        k, b = i * 4 + (2 * a + m), m
                        sp.wait_ge(x1_ready, k + 1)
                        sp.dma_start(cols(g.X1, k), x1[:, b].rearrange("p t f -> p (t f)")).then_inc(stored, 16)
                        if more or a == 0:
                            load_x(k + 2, b)
                        sp.wait_ge(x2_ready, k + 1)
                        sp.dma_start(cols(g.X2, k), x2[:, b].rearrange("p t f -> p (t f)")).then_inc(stored, 16)
                        sp.dma_start(cols(g.G, k), gt[:, b].rearrange("p t f -> p (t f)")).then_inc(stored, 16)
                        sp.wait_ge(stored, (k + 1) * 48)
                        sp.sem_inc(dense_free, 1)
                    if more:
                        sp.wait_ge(rows[a], i * GAT + GAT)
                        ends.load_idx(sp, i * 2 + (a + 2), a)

            with sp.Fori(0, PAIRS - 1) as i:
                turn(i, True)
            turn(PAIRS - 1, False)

        @block.gpsimd
        def _(pool):
            pool_wait(g, pool)
            ends.gather(pool, 0, range(Ends.EARLY, C))
            pool_wait(g, pool, (ends.idx_here[1], 32))
            ends.gather(pool, 1, range(C))
            with pool.Fori(1, PAIRS) as i:
                for a in range(2):
                    pool_wait(g, pool, (ends.idx_here[a], i * 32 + 32), (ring_free, i * 2 + (a + 1)))
                    ends.gather(pool, a, range(C))

        @block.vector
        def _(dve):
            def node_a(b, turn, n):
                dve.wait_ge(x0_here[b], turn * 16 + 16)
                bias = lambda: nc.vector.tensor_tensor(x0[:, b], x0[:, b], bc_tile(g.bias0[:], C), ALU.add)
                dve_norm(nc, dve, w, x0[:, b], hd[:, 0], C, n, h0_ready, meanwhile=(None, bias))

            def node_b(k, b, n):
                dve.wait_ge(dense_free, k + 1)
                dve.wait_ge(w_done, k + 1)
                nc.vector.tensor_tensor(x1[:, b], x0[:, b], pW[:, 0:C * F].rearrange("p (t f) -> p t f", f=F), ALU.add)
                dve.drain().then_inc(x1_ready, 1)
                bias = lambda: nc.vector.tensor_tensor(x2[:, b], x1[:, b], bc_tile(g.b1out[:], C), ALU.add)
                dve_norm(nc, dve, w, x1[:, b], hd[:, 1], C, n, h1_ready, meanwhile=(bias, None))

            def node_c(k, b):
                for half in range(2):
                    dve.wait_ge(gr_done, k * 2 + (half + 1))
                    pv = (pG, pH)[half][:, 0:C // 2 * 2 * F].rearrange("p (t c) -> p t c", c=2 * F)
                    ts = slice(half * (C // 2), (half + 1) * (C // 2))
                    nc.vector.tensor_tensor(x2[:, b, ts, :], x2[:, b, ts, :], pv[:, :, F:2 * F], ALU.add)
                    nc.vector.tensor_copy(gt[:, b, ts, :], pv[:, :, 0:F])
                dve.drain().then_inc(x2_ready, 1)

            def edge_norm(i, a, half, n):
                if half == 0:
                    dve.wait_ge(rows[a], i * GAT + GAT)
                    dve.wait_ge(ring_free, i * 2 + (a + 2))
                dve_norm(nc, dve, w, ring[:, a, half], hedge[:, half * C:(half + 1) * C, :], C, n)

            def edge_dots(c):
                for k, (half, v) in enumerate(((0, 0), (1, 1), (1, 2))):
                    nc.vector.tensor_tensor(w.xc[:], hedge[:, half * C:(half + 1) * C, :],
                                            bc_tile(g.watt[:, v, :], C), ALU.mult)
                    dve.drain()
                    nc.vector.tensor_reduce(dots[:, k, :], w.xc[:], AX.X, ALU.add)
                    dve.drain()
                nc.vector.tensor_tensor(dots[:, 3, :], dots[:, 0, :], dots[:, 1, :], ALU.add)
                dve.drain()
                nc.vector.scalar_tensor_tensor(out=g.e_edge[:, bass.ds(c * C, C)], in0=dots[:, 3, :], scalar=0.2,
                                               in1=dots[:, 3, :], op0=ALU.mult, op1=ALU.max)
                nc.vector.scalar_tensor_tensor(out=g.e_self[:, bass.ds(c * C, C)], in0=dots[:, 2, :], scalar=0.2,
                                               in1=dots[:, 2, :], op0=ALU.mult, op1=ALU.max)
                dve.drain().then_inc(h_edge_ready, 1)

            node_a(0, 0, 0)
            node_b(0, 0, 1)
            node_a(1, 0, 2)
            node_c(0, 0)
            node_b(1, 1, 3)
            node_a(0, 1, 4)
            node_c(1, 1)

            def step(i, a, more):
                c, k, n0 = i * 2 + a, i * 4 + (2 * a + 2), norms_before(i, a)
                node_b(k, 0, n0)
                node_a(1, c + 1, n0 + 1)
                edge_norm(i, a, 0, n0 + 2)
                node_c(k, 0)
                node_b(k + 1, 1, n0 + 3)
                if more:
                    node_a(0, c + 2, n0 + 4)
                edge_norm(i, a, 1, n0 + (5 if more else 4))
                edge_dots(c)
                node_c(k + 1, 1)

            with dve.Fori(0, PAIRS - 1) as i:
                for a in range(2):
                    step(i, a, True)
            step(PAIRS - 1, 0, False)
            edge_norm(PAIRS - 1, 1, 0, w.norms - 2)
            edge_norm(PAIRS - 1, 1, 1, w.norms - 1)
            edge_dots(EC - 1)

        @block.scalar
        def _(act):
            act.sem_inc(ring_free, 2)

            def bring(n):
                act.wait_ge(turned, n + 1)
                nc.scalar.copy(tsb[:], pT[:, 0:Q * P]).then_inc(turned_sb, 1)

            def hidden(k):
                for half in range(2):
                    act.wait_ge(hid_done, k * 2 + (half + 1))
                    nc.scalar.activation(hid[:, half, :], pH[:, 0:Q * P], ACT.Relu, bias=g.b1col[:, 0:1]).then_inc(hid_sb, 1)

            def keep_edges(c, a):
                act.wait_ge(h_edge_ready, c + 1)
                nc.scalar.copy(g.agg[:, bass.ds(c * C, C), :], hedge[:, 0:C, :])
                nc.scalar.copy(g.xd[:, bass.ds(c * C, C), :], ring[:, a, 1])
                act.drain().then_inc(ring_free, 1)

            act_norm(nc, act, w, C, 0)
            bring(0)
            act_norm(nc, act, w, C, 1)
            bring(1)
            act_norm(nc, act, w, C, 2)
            hidden(0)
            bring(2)
            act_norm(nc, act, w, C, 3)
            bring(3)
            act_norm(nc, act, w, C, 4)
            hidden(1)
            bring(4)

            def step(i, a, more):
                c, k, n0 = i * 2 + a, i * 4 + (2 * a + 2), norms_before(i, a)
                act_norm(nc, act, w, C, n0)
                bring(k * 2 + 1)
                act_norm(nc, act, w, C, n0 + 1)
                hidden(k)
                act_norm(nc, act, w, C, n0 + 2)
                bring(k * 2 + 2)
                act_norm(nc, act, w, C, n0 + 3)
                bring(k * 2 + 3)
                if more:
                    act_norm(nc, act, w, C, n0 + 4)
                hidden(k + 1)
                act_norm(nc, act, w, C, n0 + (5 if more else 4))
                if more:
                    bring(k * 2 + 4)
                keep_edges(c, a)

            with act.Fori(0, PAIRS - 1) as i:
                for a in range(2):
                    step(i, a, True)
            step(PAIRS - 1, 0, False)
            act_norm(nc, act, w, C, w.norms - 2)
            act_norm(nc, act, w, C, w.norms - 1)
            keep_edges(EC - 1, 1)

        @block.tensor
        def _(pe):
            def project(k):
                pe.wait_ge(h0_ready, k + 1)
                pe_quads(nc, pT, hd[:, 0], g.ident[:], Q, turned)
                pe.wait_ge(turned_sb, k * 2 + 1)
                for q in range(Q):
                    last = nc.tensor.matmul(pW[:, q * P:(q + 1) * P], tsb[:, q * P:(q + 1) * P], g.w0[:], start=True, stop=True)
                last.then_inc(w_done, 1)

            def second_layer(k):
                pe.wait_ge(h1_ready, k + 1)
                pe_quads(nc, pT, hd[:, 1], g.ident[:], Q, turned)
                pe.wait_ge(turned_sb, k * 2 + 2)
                for half in range(2):
                    if half:
                        pe.wait_ge(hid_sb, k * 2 + 1)
                    for s in range(Q):
                        r = half * Q + s
                        last = nc.tensor.matmul(pH[:, s * P:(s + 1) * P], g.w1r[:, r % 2, :],
                                                tsb[:, (r // 2) * P:(r // 2 + 1) * P], start=True, stop=True)
                    last.then_inc(hid_done, 1)
                for half in range(2):
                    pe.wait_ge(hid_sb, k * 2 + (half + 1))
                    for s in range(Q):
                        last = nc.tensor.matmul((pG, pH)[half][:, s * P:(s + 1) * P], hid[:, half, s * P:(s + 1) * P], g.w1gr[:],
                                                start=True, stop=True)
                    last.then_inc(gr_done, 1)

            project(0)
            with pe.Fori(0, NC - 1) as k:
                second_layer(k)
                project(k + 1)
            second_layer(NC - 1)


def stage_softmax(nc, g):
    with ExitStack() as ctx:
        sb = lambda name: ctx.enter_context(nc.sbuf_tensor(f"sm_{name}", [P, ET], f32))
        top, most, negcut, precut = sb("top"), sb("most"), sb("negcut"), sb("precut")
        with ExitStack() as inner:
            block = inner.enter_context(nc.Block())

            @block.vector
            def _(dve):
                nc.vector.tensor_scalar(negcut[:], g.same[:], -NEG, NEG, ALU.mult, ALU.add)
                nc.vector.tensor_scalar(precut[:], g.pre[:], -NEG, NEG, ALU.mult, ALU.add)
                nc.vector.tensor_tensor(top[:], g.e_edge[:], g.e_self[:], ALU.max)
                dve.drain()
                nc.vector.tensor_tensor_scan(most[:], negcut[:], top[:], NEG, ALU.add, ALU.max)

        stage_carry(nc, g, "sm_max", [most[:, ET - 1:ET]], greatest=True)
        with ExitStack() as inner:
            block = inner.enter_context(nc.Block())

            @block.vector
            def _(dve):
                nc.vector.scalar_tensor_tensor(out=most[:], in0=precut[:], scalar=g.carry[:, 0:1], in1=most[:],
                                               op0=ALU.add, op1=ALU.max)
                dve.drain()
                nc.vector.tensor_tensor(most[:], most[:], g.end[:], ALU.mult)
                dve.drain()
                nc.vector.tensor_tensor_scan(top[:, ::-1], g.more[:, ::-1], most[:, ::-1], 0.0, ALU.mult, ALU.add)

        stage_carry(nc, g, "sm_back", [top[:, 0:1]], reverse=True)
        less, raised = g.sem("sm_less"), g.sem("sm_raised")
        with ExitStack() as inner:
            block = inner.enter_context(nc.Block())

            @block.vector
            def _(dve):
                nc.vector.scalar_tensor_tensor(out=top[:], in0=g.suf[:], scalar=g.carry_back[:, 0:1], in1=top[:],
                                               op0=ALU.mult, op1=ALU.add)
                dve.drain()
                nc.vector.tensor_tensor(g.e_edge[:], g.e_edge[:], top[:], ALU.subtract)
                nc.vector.tensor_tensor(g.e_self[:], g.e_self[:], top[:], ALU.subtract).then_inc(less, 1)
                dve.wait_ge(raised, 2)
                nc.vector.tensor_tensor_scan(g.rden[:], g.same[:], g.e_edge[:], 0.0, ALU.mult, ALU.add)
                nc.vector.tensor_tensor(g.agg[:], g.agg[:], bc_feat(g.e_edge[:]), ALU.mult)
                dve.drain()
                for f in range(F):
                    nc.vector.tensor_tensor_scan(g.agg[:, :, f], g.same[:], g.agg[:, :, f], 0.0, ALU.mult, ALU.add)

            @block.scalar
            def _(act):
                act.wait_ge(less, 1)
                nc.scalar.activation(g.e_edge[:], g.e_edge[:], ACT.Exp).then_inc(raised, 1)
                nc.scalar.activation(g.e_self[:], g.e_self[:], ACT.Exp).then_inc(raised, 1)

        stage_carry(nc, g, "sm_sum", [g.agg[:, ET - 1, :], g.rden[:, ET - 1:ET]])
        with ExitStack() as inner:
            block = inner.enter_context(nc.Block())

            @block.vector
            def _(dve):
                nc.vector.scalar_tensor_tensor(out=g.rden[:], in0=g.pre[:], scalar=g.carry[:, F:F + 1], in1=g.rden[:],
                                               op0=ALU.mult, op1=ALU.add)
                dve.drain()
                nc.vector.tensor_tensor(g.rden[:], g.rden[:], g.e_self[:], ALU.add)
                dve.drain()
                nc.vector.reciprocal(g.rden[:], g.rden[:])
                dve.drain()
                nc.vector.tensor_tensor(g.e_self[:], g.e_self[:], g.rden[:], ALU.mult)


class Scatter:

    def __init__(self, nc, ctx, g, stage, width=F):
        self.rows = ctx.enter_context(nc.sbuf_tensor(f"{stage}_out_rows", [P, 2, C, width], f32))
        self.idx = ctx.enter_context(nc.sbuf_tensor(f"{stage}_out_idx", [P, 2, C], i32))
        self.idx_here, self.done, self.ready, self.free = g.scatter_sems
        self.n = g.scatters
        g.scatters += 1

    def wait_idx(self, eng, i, a):
        eng.wait_ge(self.idx_here[a], i * 16 + 16 * (PAIRS * self.n + 1))

    def wait_done(self, eng, i, a):
        eng.wait_ge(self.done[a], i * ONCE + ONCE * (PAIRS * self.n + 1))

    def wait_ready(self, eng, c):
        eng.wait_ge(self.ready, c + (EC * self.n + 1))

    def wait_free(self, eng, c):
        eng.wait_ge(self.free, c + (EC * self.n + 1))


ONCE = 16 * C


def sp_scatter(g, sp, s):

    def load(c, a):
        sp.dma_start(s.idx[:, a, :], g.end_index[:, bass.ds(c * C, C)]).then_inc(s.idx_here[a], 16)

    load(0, 0)
    load(1, 1)
    with sp.Fori(0, PAIRS - 1) as i:
        for a in range(2):
            s.wait_done(sp, i, a)
            sp.sem_inc(s.free, 1)
            load(i * 2 + (a + 2), a)
    for a in range(2):
        s.wait_done(sp, PAIRS - 1, a)
        sp.sem_inc(s.free, 1)


def pool_scatter(nc, g, pool, s, table):
    with pool.Fori(0, PAIRS) as i:
        for a in range(2):
            s.wait_idx(pool, i, a)
            s.wait_ready(pool, i * 2 + a)
            pool_wait(g, pool)
            for t in range(C):
                pool.indirect_dma_start(
                    out=table, out_offset=bass.IndirectOffsetOnAxis(ap=s.idx[:, a, t:t + 1], axis=0),
                    in_=s.rows[:, a, t, :], in_offset=None, bounds_check=NPAD - 1, oob_is_err=False,
                ).then_inc(s.done[a], 16)


def dve_true_sum(nc, dve, g, tmp, c, lo=0, hi=F):
    part = bass.ds(c * C, C)
    nc.vector.tensor_tensor(tmp, bc_tile(g.carry[:, lo:hi], C), bc_feat(g.pre[:, part], hi - lo), ALU.mult)
    dve.drain()
    nc.vector.tensor_tensor(tmp, tmp, g.agg[:, part, lo:hi], ALU.add)
    dve.drain()


def stage_scatter_x1(nc, g):
    st = "s2"
    with ExitStack() as ctx:
        w = Norm(nc, ctx, g, st, C, EC)
        s = Scatter(nc, ctx, g, st)
        z = ctx.enter_context(nc.sbuf_tensor("s2_z", [P, C, F], f32))
        hd = ctx.enter_context(nc.sbuf_tensor("s2_h_dst", [P, C, F], f32))
        tsb = ctx.enter_context(nc.sbuf_tensor("s2_z_T", [P, Q * P], f32))
        pT = ctx.enter_context(nc.psum_tensor("s2_pT", [P, 1024], f32))
        pW = ctx.enter_context(nc.psum_tensor("s2_pW", [P, 1024], f32))
        z_ready, turned, turned_sb, w_done = (g.sem(f"{st}_{x}") for x in ("z_ready", "turned", "turned_sb", "w_done"))
        block = ctx.enter_context(nc.Block())

        @block.sync
        def _(sp):
            sp_scatter(g, sp, s)

        @block.gpsimd
        def _(pool):
            pool_scatter(nc, g, pool, s, g.X1)

        @block.vector
        def _(dve):
            with dve.Fori(0, PAIRS) as i:
                for a in range(2):
                    c = i * 2 + a
                    part = bass.ds(c * C, C)
                    true_sum = lambda: dve_true_sum(nc, dve, g, z[:], c)
                    divide = lambda: nc.vector.tensor_tensor(z[:], z[:], bc_feat(g.rden[:, part]), ALU.mult)
                    dve_norm(nc, dve, w, g.xd[:, part, :], hd[:], C, c, meanwhile=(true_sum, divide))
                    nc.vector.tensor_tensor(hd[:], hd[:], bc_feat(g.e_self[:, part]), ALU.mult)
                    dve.drain()
                    nc.vector.tensor_tensor(z[:], z[:], hd[:], ALU.add).then_inc(z_ready, 1)
                    s.wait_free(dve, c)
                    nc.vector.tensor_tensor(s.rows[:, a], g.xd[:, part, :], bc_tile(g.bias0[:], C), ALU.add)
                    dve.drain()
                    dve.wait_ge(w_done, c + 1)
                    nc.vector.tensor_tensor(s.rows[:, a], s.rows[:, a],
                                            pW[:, 0:C * F].rearrange("p (t f) -> p t f", f=F), ALU.add).then_inc(s.ready, 1)

        @block.scalar
        def _(act):
            with act.Fori(0, PAIRS) as i:
                for a in range(2):
                    c = i * 2 + a
                    act_norm(nc, act, w, C, c)
                    act.wait_ge(turned, c + 1)
                    nc.scalar.copy(tsb[:], pT[:, 0:Q * P]).then_inc(turned_sb, 1)
                    s.wait_ready(act, c)
                    nc.scalar.copy(g.xd[:, bass.ds(c * C, C), :], s.rows[:, a])

        @block.tensor
        def _(pe):
            with pe.Fori(0, PAIRS) as i:
                for a in range(2):
                    c = i * 2 + a
                    pe.wait_ge(z_ready, c + 1)
                    pe_quads(nc, pT, z, g.ident[:], Q, turned)
                    pe.wait_ge(turned_sb, c + 1)
                    for q in range(Q):
                        o = pW[:, q * P:(q + 1) * P]
                        last = nc.tensor.matmul(o, tsb[:, q * P:(q + 1) * P], g.w0[:], start=True, stop=True)
                    last.then_inc(w_done, 1)


def stage_gather(nc, g, st, table, norm, lo=0, hi=F, beside=None, radial=None):
    K = hi - lo
    NORMS = 3 if radial is not None else 1
    with ExitStack() as ctx:
        w = Norm(nc, ctx, g, st, C, NORMS * EC) if norm else None
        sb = lambda name, shape, dt=f32: ctx.enter_context(nc.sbuf_tensor(f"{st}_{name}", shape, dt))
        ring = sb("ring", [P, 2, C, F])
        idx = sb("idx", [P, 2, C], i32)
        h = sb("h_src", [P, C, K]) if norm else None
        run = sb("running", [P, 2, C, K])
        if radial is not None:
            node = sb("nodes", [P, 2, C, F])
            nodes_here = [g.sem(f"{st}_nodes_here{m}") for m in range(2)]
        idx_here = [g.sem(f"{st}_idx_here{a}") for a in range(2)]
        rows = [g.sem(f"{st}_rows{a}") for a in range(2)]
        ring_free, run_ready, run_free = (g.sem(f"{st}_{x}") for x in ("ring_free", "run_ready", "run_free"))
        block = ctx.enter_context(nc.Block())

        @block.sync
        def _(sp):
            def load(c, a):
                sp.dma_start(idx[:, a, :], g.src[:, bass.ds(c * C, C)]).then_inc(idx_here[a], 16)

            def load_nodes(k, m):
                sp.dma_start(node[:, m].rearrange("p t f -> p (t f)"),
                             table.rearrange("(p t) f -> p (t f)", p=P)[:, bass.ds(k * (C * F), C * F)]).then_inc(nodes_here[m], 16)

            def more_nodes(c):
                for m in range(2):
                    sp.wait_ge(w.centered, c * NORMS + (w.base + m + 1))
                    load_nodes(c * 2 + (m + 2), m)

            load(0, 0)
            load(1, 1)
            if radial is not None:
                load_nodes(0, 0)
                load_nodes(1, 1)
            if beside is not None:
                beside.sp(sp)
            with sp.Fori(0, PAIRS - 1) as i:
                for a in range(2):
                    sp.wait_ge(rows[a], i * ONCE + ONCE)
                    load(i * 2 + (a + 2), a)
                    if radial is not None:
                        more_nodes(i * 2 + a)
                if beside is not None:
                    beside.sp_turn(sp, i)
            if radial is not None:
                more_nodes(EC - 2)
            if beside is not None:
                beside.sp_end(sp)

        @block.gpsimd
        def _(pool):
            with pool.Fori(0, PAIRS) as i:
                for a in range(2):
                    pool_wait(g, pool, (idx_here[a], i * 16 + 16), (ring_free, i * 2 + (a + 1)))
                    for t in range(C):
                        pool.indirect_dma_start(
                            out=ring[:, a, t, :], out_offset=None, in_=table,
                            in_offset=bass.IndirectOffsetOnAxis(ap=idx[:, a, t:t + 1], axis=0),
                        ).then_inc(rows[a], 16)

        @block.vector
        def _(dve):
            dve.sem_inc(ring_free, 2)
            nc.vector.memset(run[:, 1, C - 1, :], 0.0)
            dve.drain()
            if beside is not None:
                beside.dve(dve)
            with dve.Fori(0, PAIRS) as i:
                for a in range(2):
                    c = i * 2 + a
                    part = bass.ds(c * C, C)
                    if radial is not None:
                        for m in range(2):
                            dve.wait_ge(nodes_here[m], c * 16 + 16)
                            dve_norm(nc, dve, w, node[:, m], radial[:, bass.ds(c * (2 * C) + m * C, C), :], C,
                                     c * NORMS + m, lo=0, hi=radial.shape[2])
                    dve.wait_ge(rows[a], i * ONCE + ONCE)
                    if norm:
                        dve_norm(nc, dve, w, ring[:, a], h[:], C, c * NORMS + (NORMS - 1), lo=lo, hi=hi)
                        dve.drain().then_inc(ring_free, 1)
                    dve.wait_ge(run_free, c + 1)
                    for f in range(K):
                        v = h[:, :, f] if norm else ring[:, a, :, lo + f]
                        nc.vector.tensor_tensor_scan(run[:, a, :, f], g.same[:, part], v, run[:, 1 - a, C - 1, f:f + 1],
                                                     ALU.mult, ALU.add)
                    dve.drain().then_inc(run_ready, 1)
                    if not norm:
                        dve.drain().then_inc(ring_free, 1)

        @block.scalar
        def _(act):
            act.sem_inc(run_free, 2)
            with act.Fori(0, PAIRS) as i:
                for a in range(2):
                    c = i * 2 + a
                    for m in range(NORMS if norm else 0):
                        act_norm(nc, act, w, C, c * NORMS + m)
                    act.wait_ge(run_ready, c + 1)
                    nc.scalar.copy(g.agg[:, bass.ds(c * C, C), 0:K], run[:, a]).then_inc(run_free, 1)


class ClearTables:

    ROW = NTRASH * CW // P
    TURNS = PAIRS - 1
    STEP = ROW // (TURNS + 1)
    REST = ROW - TURNS * STEP

    def __init__(self, nc, ctx, g):
        assert self.ROW * P == NTRASH * CW
        self.nc, self.tables = nc, (g.sum_dst, g.sum_a, g.sum_b)
        self.zero = ctx.enter_context(nc.sbuf_tensor("zero", [P, self.REST], f32))
        self.zero_set, self.cleared = g.sem("zero_set"), g.sem("tables_cleared")

    def dve(self, dve):
        self.nc.vector.memset(self.zero[:], 0.0).then_inc(self.zero_set, 1)

    def sp(self, sp):
        sp.wait_ge(self.zero_set, 1)

    def clear(self, sp, first, n):
        for table in self.tables:
            flat = table.rearrange("n w -> (n w)").rearrange("(p k) -> p k", k=self.ROW)
            sp.dma_start(flat[:, bass.ds(first, n)], self.zero[:, 0:n]).then_inc(self.cleared, 16)

    def sp_turn(self, sp, i):
        self.clear(sp, i * self.STEP, self.STEP)

    def sp_end(self, sp):
        self.clear(sp, self.TURNS * self.STEP, self.REST)
        sp.wait_ge(self.cleared, 16 * len(self.tables) * (self.TURNS + 1))


class LateWeights:

    def __init__(self, nc, ctx, third_ctx, g):
        self.nc, self.g, self.n = nc, g, 0
        sb = lambda name, shape: ctx.enter_context(nc.sbuf_tensor(name, shape, f32))
        sb3 = lambda name, shape: third_ctx.enter_context(nc.sbuf_tensor(name, shape, f32))
        g.w3, g.w3x, g.w3y = sb("w3", [P, 4, NB * F]), sb("w3x", [P, 4, 2 * F]), sb("w3y", [P, 4, F + NB])
        g.relrow, self.a2b = sb("relrow", [NREL, RT - F]), sb("A2_b_rows", [NREL, F])
        g.w2in, g.w2out, g.b2col, g.b2out = sb3("w2in", [P, 4, P]), sb3("w2out", [P, F]), sb3("b2col", [P, 1]), sb3("b2out", [P, 1])
        self.padded, self.loaded, self.rel_loaded = g.sem("late_padded"), g.sem("late_loaded"), g.sem("rel_loaded")

    def dve(self, dve):
        nc, g = self.nc, self.g
        for t in (g.w2in, g.w3, g.w3x, g.w3y):
            nc.vector.memset(t[:], 0.0)
        dve.drain().then_inc(self.padded, 1)
        for f in range(CON):
            nc.vector.tensor_tensor_scan(g.con[:, ::-1, f], g.more[:, ::-1], g.con[:, ::-1, f], 0.0, ALU.mult, ALU.add)
        dve.wait_ge(self.rel_loaded, 64)
        nc.vector.tensor_tensor(g.relrow[:, F:2 * F], g.relrow[:, F:2 * F], self.a2b[:], ALU.add)
        dve.drain()

    def load(self, sp, dst, src):
        sp.dma_start(dst, src).then_inc(self.loaded, 16)
        self.n += 16

    def sp(self, sp):
        g = self.g
        sp.dma_start(g.relrow[:, 2 * F:RT - F], g.w_comp).then_inc(self.rel_loaded, 16)
        sp.dma_start(g.relrow[:, F:2 * F], g.rel_emb).then_inc(self.rel_loaded, 16)
        sp.dma_start(g.relrow[:, 0:F], g.A1_b.partition_broadcast(NREL)).then_inc(self.rel_loaded, 16)
        sp.dma_start(self.a2b[:], g.A2_b.partition_broadcast(NREL)).then_inc(self.rel_loaded, 16)
        self.load(sp, g.w2out[:], g.L2_W2)
        self.load(sp, g.b2col[:], g.L2_b1.unsqueeze(1))
        sp.wait_ge(self.padded, 1)
        for j in range(4):
            rows = slice(F * j, F * (j + 1))
            self.load(sp, g.b2out[rows, :], g.L2_b2.unsqueeze(1))
            self.load(sp, g.w2in[rows, j, :], g.L2_W1)
            self.load(sp, g.w3[rows, j, :], g.weight)
            self.load(sp, g.w3x[rows, j, 0:F], g.slw)
            self.load(sp, g.w3x[rows, j, F:2 * F], g.A1_wT)
            self.load(sp, g.w3y[rows, j, 0:F], g.A2_wT)

    def sp_turn(self, sp, i):
        pass

    def sp_end(self, sp):
        sp.wait_ge(self.loaded, self.n)


def stage_scatter_g(nc, g):
    st = "s4"
    with ExitStack() as ctx:
        sb = lambda name, shape: ctx.enter_context(nc.sbuf_tensor(f"{st}_{name}", shape, f32))
        pb = lambda name: ctx.enter_context(nc.psum_tensor(f"{st}_{name}", [P, 1024], f32))
        S = lambda name: g.sem(f"{st}_{name}")
        w = Norm(nc, ctx, g, st, C, EC)
        s = Scatter(nc, ctx, g, st)
        mean, hd, tmp = sb("mean", [P, C, F]), sb("h_dst", [P, C, F]), sb("sum", [P, C, F])
        tsb, hid = sb("T", [P, 2, Q * P]), sb("hid_T", [P, 2, Q * P])
        pT, pU, pH, pG = pb("pT"), pb("pU"), pb("pH"), pb("pG")
        ready, turned, turned_sb, hid_done, hid_sb, gr_done = (
            S(x) for x in ("ready", "turned", "turned_sb", "hid_done", "hid_sb", "gr_done"))
        block = ctx.enter_context(nc.Block())

        @block.sync
        def _(sp):
            sp_scatter(g, sp, s)

        @block.gpsimd
        def _(pool):
            pool_scatter(nc, g, pool, s, g.G)

        @block.vector
        def _(dve):
            def front(c):
                dve_true_sum(nc, dve, g, tmp[:], c)
                dve.wait_ge(turned, c * 2 + 2)
                nc.vector.tensor_tensor(mean[:], tmp[:], bc_feat(g.rdeg[:, bass.ds(c * C, C)]), ALU.mult).then_inc(ready, 1)
                dve_norm(nc, dve, w, g.xd[:, bass.ds(c * C, C), :], hd[:], C, c, ready)

            def back(c, a):
                nc.vector.tensor_tensor(g.xd[:, bass.ds(c * C, C), :], g.xd[:, bass.ds(c * C, C), :],
                                        bc_tile(g.b1out[:], C), ALU.add)
                dve.drain()
                s.wait_free(dve, c)
                for half in range(2):
                    H = C // 2
                    part = bass.ds(c * C + half * H, H)
                    dve.wait_ge(gr_done, c * 2 + (half + 1))
                    pv = (pG, pH)[half][:, 0:H * 2 * F].rearrange("p (t c) -> p t c", c=2 * F)
                    nc.vector.tensor_copy(s.rows[:, a, half * H:(half + 1) * H, :], pv[:, :, 0:F])
                    nc.vector.tensor_tensor(g.xd[:, part, :], g.xd[:, part, :], pv[:, :, F:2 * F], ALU.add)
                dve.drain().then_inc(s.ready, 1)

            dve.sem_inc(turned, 2)
            front(0)
            with dve.Fori(0, PAIRS - 1) as i:
                for a in range(2):
                    front(i * 2 + (a + 1))
                    back(i * 2 + a, a)
            front(EC - 1)
            back(EC - 2, 0)
            back(EC - 1, 1)

        @block.scalar
        def _(act):
            def bring(c):
                for k, p in enumerate((pT, pU)):
                    act.wait_ge(turned, c * 2 + (k + 3))
                    nc.scalar.copy(tsb[:, k, :], p[:, 0:Q * P]).then_inc(turned_sb, 1)

            def hidden(c):
                for half in range(2):
                    act.wait_ge(hid_done, c * 2 + (half + 1))
                    nc.scalar.activation(hid[:, half, :], pH[:, 0:Q * P], ACT.Relu, bias=g.b1col[:, 0:1]).then_inc(hid_sb, 1)

            act_norm(nc, act, w, C, 0)
            bring(0)
            with act.Fori(0, EC - 1) as c:
                act_norm(nc, act, w, C, c + 1)
                hidden(c)
                bring(c + 1)
            hidden(EC - 1)

        @block.tensor
        def _(pe):
            with pe.Fori(0, EC) as c:
                pe.wait_ge(ready, c * 2 + 1)
                pe_quads(nc, pT, mean, g.ident[:], Q, turned)
                pe.wait_ge(ready, c * 2 + 2)
                pe_quads(nc, pU, hd, g.ident[:], Q, turned)
                pe.wait_ge(turned_sb, c * 2 + 2)
                s.wait_ready(pe, c - 1)
                for half in range(2):
                    if half:
                        pe.wait_ge(hid_sb, c * 2 + 1)
                    for k in range(Q):
                        r = half * Q + k
                        q = slice((r // 2) * P, (r // 2 + 1) * P)
                        o = pH[:, k * P:(k + 1) * P]
                        nc.tensor.matmul(o, g.w1l[:, r % 2, :], tsb[:, 0, q], start=True, stop=False)
                        last = nc.tensor.matmul(o, g.w1r[:, r % 2, :], tsb[:, 1, q], start=False, stop=True)
                    last.then_inc(hid_done, 1)
                for half in range(2):
                    pe.wait_ge(hid_sb, c * 2 + (half + 1))
                    for k in range(Q):
                        last = nc.tensor.matmul((pG, pH)[half][:, k * P:(k + 1) * P], hid[:, half, k * P:(k + 1) * P],
                                                g.w1gr[:], start=True, stop=True)
                    last.then_inc(gr_done, 1)


def stage_scatter_x2(nc, g):
    st = "s6"
    with ExitStack() as ctx:
        w = Norm(nc, ctx, g, st, C, EC)
        s = Scatter(nc, ctx, g, st)
        tmp = ctx.enter_context(nc.sbuf_tensor("s6_mean", [P, C, F], f32))
        block = ctx.enter_context(nc.Block())

        @block.sync
        def _(sp):
            sp_scatter(g, sp, s)

        @block.gpsimd
        def _(pool):
            pool_scatter(nc, g, pool, s, g.X2)

        @block.vector
        def _(dve):
            with dve.Fori(0, PAIRS) as i:
                for a in range(2):
                    c = i * 2 + a
                    part = bass.ds(c * C, C)
                    dve_true_sum(nc, dve, g, tmp[:], c)
                    nc.vector.tensor_tensor(tmp[:], tmp[:], bc_feat(g.rdeg[:, part]), ALU.mult)
                    dve.drain()
                    s.wait_free(dve, c)
                    nc.vector.tensor_tensor(s.rows[:, a], g.xd[:, part, :], tmp[:], ALU.add)
                    dve.drain().then_inc(s.ready, 1)
                    dve_norm(nc, dve, w, s.rows[:, a], tmp[:, :, CON:F], C, c, lo=CON, hi=F)
                    nc.vector.tensor_tensor(g.con[:, part, :], tmp[:, :, CON:F], bc_feat(g.end[:, part], CON), ALU.mult)
                    dve.drain()

        @block.scalar
        def _(act):
            with act.Fori(0, PAIRS) as i:
                for a in range(2):
                    act_norm(nc, act, w, C, i * 2 + a)


def stage_symmetric(nc, g):
    st = "s8"
    with ExitStack() as ctx:
        sb = lambda name, shape, dt=f32: ctx.enter_context(nc.sbuf_tensor(f"{st}_{name}", shape, dt))
        S = lambda name: g.sem(f"{st}_{name}")
        s = Scatter(nc, ctx, g, st, CW)
        srcc = sb("src", [P, 2, C], i32)
        eq = sb("equal", [P, C, P])
        eqb = sb("equal_before", [P, C, P])
        val = sb("values", [P, C, CW])
        add = sb("add_rows", [P, 2, C, CW])
        aidx = sb("add_idx", [P, 2, C], i32)
        rank, srcf = sb("rank", [P, C]), sb("src_f", [P, C])
        trash, trash_i = sb("trash", [P, 1]), sb("trash_i", [P, 1], i32)
        pB = ctx.enter_context(nc.psum_tensor("s8_pB", [P, C * P], f32))
        pS = ctx.enter_context(nc.psum_tensor("s8_pS", [P, 512], f32))
        here = [S("src_here0"), S("src_here1")]
        src_ready, spread, eq_ready, summed, add_ready, trash_set = (
            S(x) for x in ("src_ready", "src_spread", "eq_ready", "summed", "add_ready", "trash_set"))
        idx_ready, add_free = S("add_idx_ready"), S("add_free")
        added = [S("added_a"), S("added_b")]
        block = ctx.enter_context(nc.Block())
        tables = (g.sum_a, g.sum_b)
        PER = 16 * C
        LAG = 1

        @block.sync
        def _(sp):
            def load(c, a):
                sp.dma_start(s.idx[:, a, :], g.end_index[:, bass.ds(c * C, C)]).then_inc(s.idx_here[a], 16)

            def load_src(c, a):
                sp.dma_start(srcc[:, a, :], g.src[:, bass.ds(c * C, C)]).then_inc(here[a], 16)

            sp.sem_inc(add_free, 2)
            for a in range(2):
                load_src(a, a)
                load(a, a)

            def turn(i, more):
                for a in range(2):
                    s.wait_done(sp, i, a)
                    sp.sem_inc(s.free, 1)
                    if more:
                        load(i * 2 + (a + 2), a)
                        sp.wait_ge(src_ready, i * 2 + (a + 1))
                        load_src(i * 2 + (a + 2), a)
                    for b in range(2):
                        sp.wait_ge(added[b], i * PER + (a + 1) * (PER // 2))
                    sp.sem_inc(add_free, 1)

            with sp.Fori(0, PAIRS - 1) as i:
                turn(i, True)
            turn(PAIRS - 1, False)

        @block.gpsimd
        def _(pool):
            nc.gpsimd.iota(trash_i[:], pattern=[[0, 1]], base=NPAD, channel_multiplier=1)
            pool.drain()
            nc.gpsimd.tensor_copy(trash[:], trash_i[:])
            pool.drain().then_inc(trash_set, 1)
            with pool.Fori(0, PAIRS) as i:
                for a in range(2):
                    c = i * 2 + a
                    s.wait_idx(pool, i, a)
                    s.wait_ready(pool, c)
                    pool_wait(g, pool)
                    for n in range(C + LAG):
                        if n < C:
                            pool.indirect_dma_start(
                                out=g.sum_dst, out_offset=bass.IndirectOffsetOnAxis(ap=s.idx[:, a, n:n + 1], axis=0),
                                in_=s.rows[:, a, n, :], in_offset=None, bounds_check=NPAD - 1, oob_is_err=False,
                            ).then_inc(s.done[a], 16)
                        t = n - LAG
                        if t < 0:
                            continue
                        if t == 0:
                            pool_wait(g, pool, (idx_ready, c + 1), (add_ready, c + 1))
                        b, turn = t % 2, (a * C + t) // 2
                        if turn:
                            pool_wait(g, pool, (added[b], i * PER + 16 * turn))
                        elif b == 0:
                            pool_wait(g, pool, (add_free, i * 2 + 2))
                        pool.indirect_dma_start(
                            out=tables[b], out_offset=bass.IndirectOffsetOnAxis(ap=aidx[:, a, t:t + 1], axis=0),
                            in_=add[:, a, t, :], in_offset=None, bounds_check=NTRASH - 1, oob_is_err=True,
                            compute_op=ALU.add,
                        ).then_inc(added[b], 16)

        @block.vector
        def _(dve):
            nc.vector.memset(val[:], 1.0)
            dve.drain()
            dve.wait_ge(trash_set, 1)
            with dve.Fori(0, PAIRS) as i:
                for a in range(2):
                    c = i * 2 + a
                    part = bass.ds(c * C, C)
                    dve.wait_ge(here[a], i * 16 + 16)
                    nc.vector.tensor_copy(srcf[:], srcc[:, a, :])
                    dve.drain().then_inc(src_ready, 1)
                    s.wait_free(dve, c)
                    dve_true_sum(nc, dve, g, s.rows[:, a, :, 0:CON], c, 0, CON)
                    nc.vector.tensor_copy(s.rows[:, a, :, CON:CW], g.deg[:, part].unsqueeze(2))
                    dve.drain().then_inc(s.ready, 1)
                    nc.vector.tensor_tensor(val[:, :, 0:CON], bc_tile(g.carry_back[:, 0:CON], C),
                                            bc_feat(g.suf[:, part], CON), ALU.mult)
                    dve.drain()
                    nc.vector.tensor_tensor(val[:, :, 0:CON], val[:, :, 0:CON], g.con[:, part, :], ALU.add)
                    dve.wait_ge(spread, c + 1)
                    nc.vector.tensor_tensor(eq[:], pB[:].rearrange("p (t k) -> p t k", k=P), bc_feat(srcf[:], P), ALU.is_equal)
                    dve.drain().then_inc(eq_ready, 1)
                    nc.vector.tensor_tensor(eqb[:], eq[:], bc_tile(g.before[:], C), ALU.mult)
                    dve.drain()
                    nc.vector.tensor_reduce(rank[:], eqb[:], AX.X, ALU.add)
                    dve.drain()
                    nc.vector.tensor_scalar(srcf[:], srcf[:], trash[:, 0:1], None, ALU.subtract)
                    dve.drain()
                    nc.vector.scalar_tensor_tensor(out=srcf[:], in0=rank[:], scalar=0.0, in1=srcf[:], op0=ALU.is_equal,
                                                   op1=ALU.mult)
                    dve.drain()
                    dve.wait_ge(add_free, c + 1)
                    nc.vector.tensor_scalar(aidx[:, a, :], srcf[:], trash[:, 0:1], None, ALU.add)
                    dve.drain().then_inc(idx_ready, 1)
                    dve.wait_ge(summed, c + 1)

        @block.tensor
        def _(pe):
            with pe.Fori(0, PAIRS) as i:
                for a in range(2):
                    c = i * 2 + a
                    pe.wait_ge(src_ready, c + 1)
                    for t in range(C):
                        last = nc.tensor.transpose(pB[:, t * P:(t + 1) * P], srcf[:, t:t + 1].to_broadcast([P, P]), g.ident[:])
                    last.then_inc(spread, 1)
                    pe.wait_ge(eq_ready, c + 1)
                    if a:
                        pe.wait_ge(add_ready, c)
                    for t in range(C):
                        last = nc.tensor.matmul(pS[:, t * CW:(t + 1) * CW], eq[:, t, :], val[:, t, :], start=True, stop=True)
                    last.then_inc(summed, 1)
                pe.wait_ge(add_ready, i * 2 + 2)

        @block.scalar
        def _(act):
            with act.Fori(0, PAIRS) as i:
                for a in range(2):
                    c = i * 2 + a
                    act.wait_ge(summed, c + 1)
                    act.wait_ge(add_free, c + 1)
                    nc.scalar.copy(add[:, a].rearrange("p t w -> p (t w)"), pS[:, 0:C * CW]).then_inc(add_ready, 1)


def stage_third_layer(nc, g):
    st = "s9"
    with ExitStack() as ctx:
        sb = lambda name, shape: ctx.enter_context(nc.sbuf_tensor(f"{st}_{name}", shape, f32))
        S = lambda name: g.sem(f"{st}_{name}")
        W = C * F
        x2 = sb("x2", [P, 4, C, F])
        x3 = sb("x3", [P, 2, C, F])
        sums = sb("sums", [P, 2, 3, C, CW])
        deg = sb("deg", [P, C])
        comb = sb("combined", [P, C, F])
        tsb = sb("T", [P, 2, W])
        hid = sb("hid_T", [P, 8, 512])
        osb = sb("out_T", [P, W])
        pb = lambda name, n=1: ctx.enter_context(nc.psum_tensor(f"{st}_{name}", [P, 512 * n], f32))
        pH, pO = [pb(f"pH{n}") for n in range(4)], pb("pO", 2)
        PARTS = ((0, 512), (512, W - 512))
        here = [S("here0"), S("here1")]
        turned, hid_done, hid_sb, out_done, out_sb, out_used, x3_ready, x3_free, stored = (
            S(x) for x in ("turned", "hid_done", "hid_sb", "out_done", "out_sb", "out_used", "x3_ready", "x3_free", "stored"))
        block = ctx.enter_context(nc.Block())
        TURNS = NC // 4
        assert NC % 4 == 0

        def cols(t, k, width):
            return t[0:NPAD, :].rearrange("(p t) f -> p (t f)", p=P)[:, bass.ds(k * (C * width), C * width)]

        @block.sync
        def _(sp):
            def load(k, m):
                b = m % 2
                sp.dma_start(x2[:, m].rearrange("p t f -> p (t f)"), cols(g.X2, k, F)).then_inc(here[b], 16)
                for j, table in enumerate((g.sum_dst, g.sum_a, g.sum_b)):
                    sp.dma_start(sums[:, b, j].rearrange("p t f -> p (t f)"), cols(table, k, CW)).then_inc(here[b], 16)

            def step(k, m, ahead):
                sp.wait_ge(x3_ready, k + 1)
                if ahead:
                    load(k + 4, m)
                sp.dma_start(cols(g.out, k, F), x3[:, m % 2].rearrange("p t f -> p (t f)")).then_inc(stored, 16)
                sp.wait_ge(stored, k * 16 + 16)
                sp.sem_inc(x3_free, 1)

            sp.sem_inc(x3_free, 2)
            load(0, 0)
            load(1, 1)
            for m in (2, 3):
                sp.wait_ge(turned, m - 1)
                load(m, m)
            with sp.Fori(0, TURNS - 1) as i:
                for m in range(4):
                    step(i * 4 + m, m, True)
            for m in range(4):
                step(NC - 4 + m, m, False)

        @block.vector
        def _(dve):
            def first(k, m, pair, start=False):
                b = m % 2
                dve.wait_ge(here[b], pair * 64 + 64)
                for j in (1, 2):
                    nc.vector.tensor_tensor(sums[:, b, 0], sums[:, b, 0], sums[:, b, j], ALU.add)
                    dve.drain()
                nc.vector.tensor_scalar(deg[:].unsqueeze(2), sums[:, b, 0, :, CON:CW], 1.0, None, ALU.max)
                dve.drain()
                nc.vector.reciprocal(deg[:], deg[:])
                nc.vector.tensor_copy(comb[:, :, 0:CON], g.radial[:, bass.ds(k * C, C), :])
                dve.drain()
                nc.vector.tensor_tensor(comb[:, :, CON:F], sums[:, b, 0, :, 0:CON], bc_feat(deg[:], CON), ALU.mult)
                dve.drain()
                if not start:
                    dve.wait_ge(hid_done, k * 8 - 8)
                nc.vector.transpose(tsb[:, b, :], comb[:].rearrange("p t f -> p (t f)")).then_inc(turned, 1)

            def second(k, m):
                out = x3[:, m % 2]
                dve.wait_ge(x3_free, k + 1)
                dve.wait_ge(out_sb, k + 1)
                nc.vector.transpose(out.rearrange("p t f -> p (t f)"), osb[:]).then_inc(out_used, 1)
                dve.drain()
                nc.vector.tensor_tensor(out, out, x2[:, m], ALU.add).then_inc(x3_ready, 1)

            first(0, 0, 0, start=True)
            first(1, 1, 0, start=True)
            with dve.Fori(0, TURNS - 1) as i:
                for m in range(4):
                    first(i * 4 + (m + 2), (m + 2) % 4, i * 2 + (m + 2) // 2)
                    second(i * 4 + m, m)
            for m in range(2):
                first(NC - 2 + m, m + 2, NC // 2 - 1)
                second(NC - 4 + m, m)
            for m in (2, 3):
                second(NC - 4 + m, m)

        @block.scalar
        def _(act):
            def hidden(k, ns):
                for n in ns:
                    width = PARTS[n // 4][1]
                    act.wait_ge(hid_done, k * 8 + (n + 1))
                    nc.scalar.activation(hid[:, n, 0:width], pH[n % 4][:, 0:width], ACT.Relu, bias=g.b2col[:, 0:1]).then_inc(hid_sb, 1)

            def out(k, start=False):
                act.wait_ge(out_done, k + 1)
                if not start:
                    act.wait_ge(out_used, k)
                nc.scalar.activation(osb[:], pO[:, 0:W], ACT.Identity, bias=g.b2out[:, 0:1]).then_inc(out_sb, 1)

            def step(k, start=False):
                hidden(k, range(2, 8))
                hidden(k + 1, range(2))
                out(k, start)

            hidden(0, range(2))
            step(0, start=True)
            with act.Fori(1, NC - 1) as k:
                step(k)
            hidden(NC - 1, range(2, 8))
            out(NC - 1)

        @block.tensor
        def _(pe):
            def hidden(k, b, ns, start=False):
                for n in ns:
                    (c0, width), j = PARTS[n // 4], n % 4
                    if n == 0:
                        pe.wait_ge(turned, k + 1)
                    if n >= 4 or not start:
                        pe.wait_ge(hid_sb, k * 8 + (n - 3))
                    nc.tensor.matmul(pH[n % 4][:, 0:width], g.w2in[:, j, :], tsb[:, b, c0:c0 + width], start=True,
                                     stop=True).then_inc(hid_done, 1)

            def out(k, part):
                c0, width = PARTS[part]
                pe.wait_ge(hid_sb, k * 8 + (part * 4 + 4))
                for j in range(4):
                    last = nc.tensor.matmul(pO[F * j:F * (j + 1), c0:c0 + width], g.w2out[:], hid[:, part * 4 + j, 0:width],
                                            start=True, stop=True)
                return last

            def step(k, b, start=False, more=True):
                hidden(k, b, range(2, 6), start=start)
                if not start:
                    pe.wait_ge(out_sb, k)
                out(k, 0)
                hidden(k, b, range(6, 8), start=start)
                if more:
                    hidden(k + 1, 1 - b, range(2))
                out(k, 1).then_inc(out_done, 1)

            hidden(0, 0, range(2), start=True)
            step(0, 0, start=True)
            with pe.Fori(0, NC // 2 - 1) as i:
                step(i * 2 + 1, 1)
                step(i * 2 + 2, 0)
            step(NC - 1, 1, more=False)


def stage_relations(nc, g):
    st = "s10"
    with ExitStack() as ctx:
        sb = lambda name, shape, dt=f32: ctx.enter_context(nc.sbuf_tensor(f"{st}_{name}", shape, dt))
        pb = lambda name, n=1: ctx.enter_context(nc.psum_tensor(f"{st}_{name}", [P, 512 * n], f32))
        S = lambda name: g.sem(f"{st}_{name}")
        w = Norm(nc, ctx, g, st, C, 2 * EC)
        ring = sb("ring", [P, 2, 2, C, F])
        idx = sb("idx", [P, 2, 2, C], i32)
        h = (sb("h", [P, C, F]), w.xc)
        etype = sb("etype", [NREL, C * P], i32)
        onehot = etype[:].bitcast(f32)
        tsb = sb("h_T", [P, 2, Q * P])
        rel = sb("rel", [P, 2, C, RT])
        bases = sb("bases", [P, 2, 2, F, NB])
        msg = sb("message", [P, C, F])
        att = sb("att", [P, 2, C])
        run, reached = sb("running", [P, C, F]), sb("reached", [P, F])
        pT = pb("pT", 2)
        pR = [pb(f"pR{a}") for a in range(2)]
        pX = [pb(f"pX{a}", 2) for a in range(2)]
        idx_here, rows = [S("idx_here0"), S("idx_here1")], [S("rows0"), S("rows1")]
        (ring_free, type_here, h_ready, hot_ready, turned, turned_sb, rel_done, rel_sb, bases_done, bases_used,
         scored, squashed, run_ready, run_free) = (S(x) for x in (
             "ring_free", "type_here", "h_ready", "hot_ready", "turned", "turned_sb", "rel_done", "rel_sb",
             "bases_done", "bases_used", "scored", "squashed", "run_ready", "run_free"))
        block = ctx.enter_context(nc.Block())
        GAT = 2 * ONCE
        D = C // 2

        @block.sync
        def _(sp):
            def load_idx(c, a):
                sp.dma_start(idx[:, a, 0, :], g.src[:, bass.ds(c * C, C)]).then_inc(idx_here[a], 16)
                sp.dma_start(idx[:, a, 1, :], g.dst[:, bass.ds(c * C, C)]).then_inc(idx_here[a], 16)

            def load_type(c, first=False):
                if not first:
                    sp.wait_ge(rel_done, c * Q)
                sp.dma_start(etype[:], g.etype_rows[bass.ds(c * (C * P), C * P)].partition_broadcast(NREL)).then_inc(type_here, 16)

            load_type(0, first=True)
            for a in range(2):
                load_idx(a, a)
            with sp.Fori(0, PAIRS - 1) as i:
                for a in range(2):
                    sp.wait_ge(rows[a], i * GAT + GAT)
                    load_idx(i * 2 + (a + 2), a)
                    load_type(i * 2 + (a + 1))
            load_type(EC - 1)

        @block.gpsimd
        def _(pool):
            with pool.Fori(0, PAIRS) as i:
                for a in range(2):
                    pool_wait(g, pool, (idx_here[a], i * 32 + 32), (ring_free, i * 2 + (a + 1)))
                    for k in range(2):
                        for t in range(C):
                            pool.indirect_dma_start(
                                out=ring[:, a, k, t, :], out_offset=None, in_=g.out,
                                in_offset=bass.IndirectOffsetOnAxis(ap=idx[:, a, k, t:t + 1], axis=0),
                            ).then_inc(rows[a], 16)

        @block.vector
        def _(dve):
            def norm(c, i, a, k, meanwhile=(None, None)):
                if k == 0:
                    dve.wait_ge(rows[a], i * GAT + GAT)
                dve_norm(nc, dve, w, ring[:, a, k], h[k][:], C, c * 2 + k, h_ready, meanwhile=meanwhile)

            def one_hot(c):
                dve.wait_ge(type_here, c * 16 + 16)
                nc.vector.tensor_scalar(onehot, etype[:], g.relid[:, 0:1], None, ALU.is_equal).then_inc(hot_ready, 1)

            def pairs(c, a, ds):
                for d in ds:
                    ts = slice(2 * d, 2 * d + 2)
                    if d % 2 == 0:
                        dve.wait_ge(rel_sb, c * Q + (d // 2 + 1))
                    dve.wait_ge(bases_done, c * D + (d + 1))
                    nc.vector.tensor_tensor(bases[:, d % 2], pX[d % 2][:].rearrange("p (t o b) -> p t o b", t=2, b=NB),
                                            rel[:, a, ts, RT - NB:RT].unsqueeze(2).to_broadcast([P, 2, F, NB]), ALU.mult)
                    dve.drain().then_inc(bases_used, 1)
                    nc.vector.tensor_reduce(msg[:, ts, :], bases[:, d % 2], AX.X, ALU.add)

            def messages(c, a, more):
                part = bass.ds(c * C, C)
                prod = bases[:, 0].rearrange("p t o b -> p (t o b)")[:, 0:C * F].rearrange("p (t f) -> p t f", f=F)
                nc.vector.tensor_tensor(prod, rel[:, a, :, F:2 * F], rel[:, a, :, 2 * F:3 * F], ALU.mult)
                dve.drain()
                nc.vector.tensor_reduce(att[:, 0, :], prod, AX.X, ALU.add)
                dve.drain()
                nc.vector.tensor_scalar(att[:, 0, :], att[:, 0, :], 1.0 / float(F) ** 0.5, 0.0, ALU.mult, ALU.max).then_inc(scored, 1)
                nc.vector.tensor_tensor(rel[:, a, :, 0:F], rel[:, a, :, 0:F], bc_feat(g.end[:, part]), ALU.mult)
                if more:
                    one_hot(c + 1)
                dve.wait_ge(squashed, c + 1)
                nc.vector.tensor_tensor(msg[:], msg[:], bc_feat(att[:, 1, :]), ALU.mult)
                dve.drain()
                nc.vector.tensor_tensor(msg[:], msg[:], rel[:, a, :, 0:F], ALU.add)
                dve.drain()
                dve.wait_ge(run_free, c + 1)
                for f in range(F):
                    nc.vector.tensor_tensor_scan(run[:, :, f], g.same[:, part], msg[:, :, f], reached[:, f:f + 1],
                                                 ALU.mult, ALU.add)
                dve.drain().then_inc(run_ready, 1)
                nc.vector.tensor_copy(reached[:], run[:, C - 1, :])
                dve.drain()

            def step(c, i, a):
                pairs(c, a, range(0, 8))
                after = (c + 1, i + a, 1 - a)
                norm(*after, 0, (lambda: pairs(c, a, (8,)), lambda: pairs(c, a, (9,))))
                norm(*after, 1, (lambda: pairs(c, a, (10,)), lambda: pairs(c, a, (11,))))
                pairs(c, a, range(12, D))
                messages(c, a, True)

            nc.vector.memset(reached[:], 0.0)
            one_hot(0)
            norm(0, 0, 0, 0)
            norm(0, 0, 0, 1)
            with dve.Fori(0, PAIRS - 1) as i:
                for a in range(2):
                    step(i * 2 + a, i, a)
            step(EC - 2, PAIRS - 1, 0)
            pairs(EC - 1, 1, range(D))
            messages(EC - 1, 1, False)

        @block.scalar
        def _(act):
            def turn(c, k):
                act.wait_ge(turned, c * 2 + (k + 1))
                nc.scalar.copy(tsb[:, k, :], pT[:, 0:Q * P]).then_inc(turned_sb, 1)

            def norm(c, k):
                act_norm(nc, act, w, C, c * 2 + k)

            def keep_rows(c, a):
                nc.scalar.copy(g.xd[:, bass.ds(c * C, C), :], ring[:, a, 1])
                act.drain().then_inc(ring_free, 1)

            def quad(c, a, qs):
                for q in qs:
                    act.wait_ge(rel_done, c * Q + (q + 1))
                    nc.scalar.copy(rel[:, a, 4 * q:4 * q + 4, :].rearrange("p t c -> p (t c)"), pR[q % 2][:, 0:4 * RT]).then_inc(rel_sb, 1)

            def tanh(c):
                act.wait_ge(scored, c + 1)
                nc.scalar.activation(att[:, 1, :], att[:, 0, :], ACT.Tanh).then_inc(squashed, 1)

            def keep_sums(c):
                act.wait_ge(run_ready, c + 1)
                nc.scalar.copy(g.agg[:, bass.ds(c * C, C), :], run[:]).then_inc(run_free, 1)

            def step(c, a, before):
                if before:
                    keep_sums(c - 1)
                quad(c, a, range(2, 5))
                norm(c + 1, 0)
                quad(c, a, (5,))
                norm(c + 1, 1)
                quad(c, a, (6,))
                keep_rows(c + 1, 1 - a)
                turn(c + 1, 0)
                turn(c + 1, 1)
                tanh(c)
                quad(c + 1, 1 - a, (0, 1))

            act.sem_inc(run_free, 1)
            act.sem_inc(ring_free, 2)
            norm(0, 0)
            turn(0, 0)
            norm(0, 1)
            keep_rows(0, 0)
            turn(0, 1)
            quad(0, 0, (0, 1))
            step(0, 0, False)
            step(1, 1, True)
            with act.Fori(1, PAIRS - 1) as i:
                for a in range(2):
                    step(i * 2 + a, a, True)
            step(EC - 2, 0, True)
            keep_sums(EC - 2)
            quad(EC - 1, 1, range(2, Q))
            tanh(EC - 1)
            keep_sums(EC - 1)

        @block.tensor
        def _(pe):
            def quads(c):
                for k in range(2):
                    pe.wait_ge(h_ready, c * 2 + (k + 1))
                    pe_quads(nc, pT, h[k], g.ident[:], Q, turned)
                    pe.wait_ge(turned_sb, c * 2 + (k + 1))

            def body(c, start):
                pe.wait_ge(hot_ready, c + 1)
                for q in range(Q):
                    quad = slice(q * P, (q + 1) * P)
                    o = pR[q % 2][:, 0:4 * RT].rearrange("p (t c) -> p t c", c=RT)
                    if q > 1 or not start:
                        pe.wait_ge(rel_sb, c * Q + (q - 1))
                    nc.tensor.matmul(o[:, :, 0:2 * F], tsb[:, 0, quad], g.w3x[:], start=True, stop=False)
                    nc.tensor.matmul(o[:, :, 2 * F:RT], tsb[:, 1, quad], g.w3y[:], start=False, stop=False)
                    for j in range(4):
                        t = 4 * q + j
                        last = nc.tensor.matmul(o[:, j, F:RT], onehot[:, t * P:(t + 1) * P], g.relrow[:], start=False,
                                                stop=(j == 3))
                    last.then_inc(rel_done, 1)
                    for d in (2 * q, 2 * q + 1):
                        if d > 1 or not start:
                            pe.wait_ge(bases_used, c * D + (d - 1))
                        for j in range(2):
                            last = nc.tensor.matmul(pX[d % 2][:, j * 512:(j + 1) * 512], tsb[:, 0, quad],
                                                    g.w3[:, (2 * d + j) % 4, :], start=True, stop=True)
                        last.then_inc(bases_done, 1)

            quads(0)
            body(0, True)
            with pe.Fori(1, EC) as c:
                quads(c)
                body(c, False)


def stage_scatter_out(nc, g):
    with ExitStack() as ctx:
        s = Scatter(nc, ctx, g, "s11")
        tmp = ctx.enter_context(nc.sbuf_tensor("s11_sum", [P, C, F], f32))
        block = ctx.enter_context(nc.Block())

        @block.sync
        def _(sp):
            sp_scatter(g, sp, s)

        @block.gpsimd
        def _(pool):
            pool_scatter(nc, g, pool, s, g.out)

        @block.vector
        def _(dve):
            with dve.Fori(0, PAIRS) as i:
                for a in range(2):
                    c = i * 2 + a
                    dve_true_sum(nc, dve, g, tmp[:], c)
                    s.wait_free(dve, c)
                    nc.vector.scalar_tensor_tensor(out=s.rows[:, a], in0=tmp[:], scalar=0.0, in1=g.xd[:, bass.ds(c * C, C), :],
                                                   op0=ALU.max, op1=ALU.add)
                    dve.drain().then_inc(s.ready, 1)


def build(nc, A, stages=99, dbg=()):
    g = Globals()
    g.x, g.src, g.dst, g.dst_flat, g.etype_rows = (
        A[k] for k in ("x", "src", "dst", "dst_flat", "etype_rows"))
    g.W, g.WT, g.att_src, g.att_dst, g.bias = (A[k] for k in ("W", "WT", "att_src", "att_dst", "bias"))
    g.W1_lT, g.W1_rT, g.L1_b1, g.W2_lT, g.W2_rT, g.L1_b2 = (A[k] for k in ("W1_lT", "W1_rT", "L1_b1", "W2_lT", "W2_rT", "L1_b2"))
    g.L2_W1, g.L2_b1, g.L2_W2, g.L2_b2 = (A[k] for k in ("L2_W1", "L2_b1", "L2_W2", "L2_b2"))
    g.weight, g.w_comp, g.slw, g.A1_wT, g.A1_b, g.A2_wT, g.A2_b, g.rel_emb = (
        A[k] for k in ("weight", "w_comp", "slw", "A1_wT", "A1_b", "A2_wT", "A2_b", "rel_emb"))
    g.out = A["out"]
    dram = lambda name, shape, dt=f32: nc.dram_tensor(name, shape, dt, kind="ExternalOutput" if name in dbg else "Internal").ap()
    g.X1, g.X2, g.G = (dram(n, (NPAD, F)) for n in ("x1_table", "x2_table", "g_table"))
    g.sum_dst, g.sum_a, g.sum_b = (dram(n, (NTRASH, CW)) for n in ("sum_dst_table", "sum_a_table", "sum_b_table"))
    g.end_index = dram("end_index_table", (P, ET), i32)
    with ExitStack() as ctx:
        g.sem = lambda name: ctx.enter_context(nc.semaphore(name))
        sb = lambda name, shape, dt=f32: ctx.enter_context(nc.sbuf_tensor(name, shape, dt))
        g.pool_steps = g.sem("pool_steps")
        g.norm_sems = [g.sem(f"norm_{x}") for x in ("centered", "squared", "summed", "rooted")]
        g.carry_sems = [g.sem(f"carry_{x}") for x in ("copied", "turned", "scanned", "back")]
        g.scatter_sems = ([g.sem(f"scatter_idx_here{a}") for a in range(2)], [g.sem(f"scattered{a}") for a in range(2)],
                          g.sem("scatter_rows_ready"), g.sem("scatter_rows_free"))
        g.norms = g.carries = g.scatters = 0
        g.xd = sb("x_dst", [P, ET, F])
        g.radial = g.xd[:].rearrange("p t f -> p (t f)").rearrange("p (n k) -> p n k", k=CON)
        g.agg = sb("agg", [P, ET, F])
        g.same, g.more, g.end = (sb(n, [P, ET]) for n in ("same_as_before", "same_as_after", "is_last"))
        g.pre, g.suf = sb("same_from_start", [P, ET]), sb("same_to_end", [P, ET])
        g.deg, g.rdeg = sb("deg", [P, ET]), sb("rdeg", [P, ET])
        g.preall, g.sufall = sb("preall", [CARRY, P]), sb("sufall", [CARRY, P])
        g.carry, g.carry_back = sb("carry", [P, CARRY]), sb("carry_back", [P, CARRY])
        g.ident, g.before = sb("ident", [P, P]), sb("before", [P, P])
        g.relid, g.relid_i, g.eps = sb("relid", [NREL, 1]), sb("relid_i", [NREL, 1], i32), sb("eps", [P, 1])
        first_weights = ctx.enter_context(ExitStack())
        sb1 = lambda name, shape: first_weights.enter_context(nc.sbuf_tensor(name, shape, f32))
        g.w0, g.bias0, g.watt = sb1("w0", [P, P]), sb1("bias0", [P, F]), sb1("watt", [P, 3, F])
        g.w1l, g.w1r, g.w1gr = sb1("w1l", [P, 2, P]), sb1("w1r", [P, 2, P]), sb1("w1gr", [P, P])
        g.b1col, g.b1out = sb1("b1col", [P, 1]), sb1("b1out", [P, F])
        with ExitStack() as attention:
            g.e_edge, g.e_self = (attention.enter_context(nc.sbuf_tensor(n, [P, ET], f32)) for n in ("e_edge", "e_self"))
            with ExitStack() as ring:
                ends = Ends(nc, ring, g)
                stage_setup(nc, g, ends)
                if stages < 1: return
                stage_first_gather(nc, g, ends)
            if stages < 2: return
            g.rden = attention.enter_context(nc.sbuf_tensor("rden", [P, ET], f32))
            stage_softmax(nc, g)
            stage_scatter_x1(nc, g)
        if stages < 3: return
        with ExitStack() as zeros:
            stage_gather(nc, g, "s3", g.X1, norm=True, beside=ClearTables(nc, zeros, g))
        stage_carry(nc, g, "s3c", [g.agg[:, ET - 1, :]])
        stage_scatter_g(nc, g)
        first_weights.close()
        if stages < 4: return
        stage_gather(nc, g, "s5", g.G, norm=False)
        stage_carry(nc, g, "s5c", [g.agg[:, ET - 1, :]])
        late_space = ctx.enter_context(ExitStack())
        third_weights = ctx.enter_context(ExitStack())
        late = LateWeights(nc, late_space, third_weights, g)
        with ExitStack() as con:
            g.con = con.enter_context(nc.sbuf_tensor("conical_dst", [P, ET, CON], f32))
            stage_scatter_x2(nc, g)
            if stages < 5: return
            stage_gather(nc, g, "s7", g.X2, norm=True, lo=CON, hi=F, beside=late, radial=g.radial)
            stage_carry(nc, g, "s7c", [g.agg[:, ET - 1, 0:CON]])
            stage_carry(nc, g, "s7r", [g.con[:, 0, :]], reverse=True)
            stage_symmetric(nc, g)
        if stages < 6: return
        stage_third_layer(nc, g)
        third_weights.close()
        if stages < 7: return
        stage_relations(nc, g)
        stage_carry(nc, g, "s10c", [g.agg[:, ET - 1, :]])
        stage_scatter_out(nc, g)


def kernel(x, src, dst, edge_type_86, L0_gnn_W, L0_gnn_att_src, L0_gnn_att_dst, L0_gnn_bias, L1_gnn_W1_l, L1_gnn_W1_r,
           L1_gnn_b1, L1_gnn_W2_l, L1_gnn_W2_r, L1_gnn_b2, L2_gnn_W1, L2_gnn_b1, L2_gnn_W2, L2_gnn_b2, L3_gnn_weight,
           L3_gnn_w_comp, L3_gnn_self_loop_weight, L3_gnn_A1_w, L3_gnn_A1_b, L3_gnn_A2_w, L3_gnn_A2_b, L3_gnn_rel_emb,
           launch=None):
    import numpy as np

    def rows(a, fill):
        a = np.asarray(a)
        out = np.full((EPAD,), fill, a.dtype)
        out[:E] = a
        return out

    src_p, dst_p, et_p = rows(src, N), rows(dst, N), rows(edge_type_86, 0)
    xp = np.zeros((NPAD, F), np.float32)
    xp[:N] = np.asarray(x)
    flat = np.full((EPAD + 2,), -1, np.int32)
    flat[1:-1] = dst_p
    T = lambda a: np.ascontiguousarray(np.asarray(a).T)
    arrays = {
        "x": xp, "src": src_p.reshape(P, ET), "dst": dst_p.reshape(P, ET), "dst_flat": flat,
        "etype_rows": T(et_p.reshape(P, ET)).reshape(-1),
        "W": L0_gnn_W, "WT": T(L0_gnn_W), "att_src": L0_gnn_att_src, "att_dst": L0_gnn_att_dst, "bias": L0_gnn_bias,
        "W1_lT": T(L1_gnn_W1_l), "W1_rT": T(L1_gnn_W1_r), "L1_b1": L1_gnn_b1, "W2_lT": T(L1_gnn_W2_l),
        "W2_rT": T(L1_gnn_W2_r), "L1_b2": L1_gnn_b2, "L2_W1": L2_gnn_W1, "L2_b1": L2_gnn_b1, "L2_W2": L2_gnn_W2,
        "L2_b2": L2_gnn_b2, "weight": np.transpose(np.asarray(L3_gnn_weight), (1, 2, 0)).reshape(F, NB * F), "w_comp": L3_gnn_w_comp, "slw": L3_gnn_self_loop_weight,
        "A1_wT": T(L3_gnn_A1_w), "A1_b": L3_gnn_A1_b, "A2_wT": T(L3_gnn_A2_w), "A2_b": L3_gnn_A2_b,
        "rel_emb": L3_gnn_rel_emb,
    }
    arrays = {k: np.ascontiguousarray(np.asarray(a)) for k, a in arrays.items()}
    import concourse.bacc as bacc
    from concourse.bass_utils import run_bass_kernel_spmd

    nc = bacc.Bacc("TRN2", target_bir_lowering=False, num_devices=1)
    A = {k: nc.dram_tensor(f"in_{k}", a.shape, mybir.dt.from_np(a.dtype), kind="ExternalInput").ap() for k, a in arrays.items()}
    A["out"] = nc.dram_tensor("out_x", (NPAD, F), f32, kind="ExternalOutput").ap()
    if launch is not None:
        return launch(nc, A, arrays)
    build(nc, A)
    r = run_bass_kernel_spmd(nc, [{f"in_{k}": a for k, a in arrays.items()}], core_ids=[0])
    return r.results[0]["out_x"][:N]
```
